# Optimizing a Trainium2 kernel written in Bass

```python
import numpy as np
import jax
import jax.numpy as jnp

def _softmax(x, axis=-1):
    return jax.nn.softmax(x, axis=axis)

def _gelu(x):
    return jax.nn.gelu(x, approximate=True)

def _silu(x):
    return jax.nn.silu(x)

def _sigmoid(x):
    return jax.nn.sigmoid(x)

def _layernorm(x, axis=-1, eps=1e-05):
    m = jnp.mean(x, axis=axis, keepdims=True)
    v = jnp.var(x, axis=axis, keepdims=True)
    return (x - m) / jnp.sqrt(v + eps)

def _scatter_add(tgt, idx, src, axis=0):
    return tgt.at[idx].add(src)

def _segment_sum(src, seg, n):
    return jax.ops.segment_sum(src, seg, n)
kernel_name = 'mk_gnn_preln_d2_gnn_r16_865118'

def setup_inputs(seed: int=0):
    np.random.seed(seed)
    _w = jnp.asarray

    def _rec_inputs():
        import jax
        import jax.numpy as jnp
        _gk = jax.random.key(seed)
        x = -0.000364 + 1 * jax.random.normal(jax.random.fold_in(_gk, 1), (1250, 768), jnp.float32)
        src = jax.random.randint(jax.random.fold_in(_gk, 2), (20000,), 0, 1250, jnp.int32)
        dst = jax.random.randint(jax.random.fold_in(_gk, 3), (20000,), 0, 1250, jnp.int32)
        _o = jnp.argsort(dst, stable=True)
        src = src[_o]
        dst = dst[_o]
        edge_type_34 = jax.random.randint(jax.random.fold_in(_gk, 13), (20000,), 0, 34, jnp.int32)
        return (x, src, dst, edge_type_34)
    x, src, dst, edge_type_34 = _rec_inputs()

    def _L0_gnn_setup():
        import jax, jax.numpy as jnp
        import numpy as np
        N, E, DIM, HEADS = (1250, 20000, 768, 8)
        HD = DIM // HEADS
        EPS = 1e-05

        def layer_norm(x, w, b):
            mu = jnp.mean(x, axis=-1, keepdims=True)
            var = jnp.var(x, axis=-1, keepdims=True)
            return (x - mu) * jax.lax.rsqrt(var + EPS) * w + b

        def gatv2(x, src, dst, Ws, bs, Wd, bd, attn):
            H, D = attn.shape
            fs = (x @ Ws + bs).reshape(-1, H, D)
            fd = (x @ Wd + bd).reshape(-1, H, D)
            e = jax.nn.leaky_relu(fs[src] + fd[dst], 0.2)
            logits = jnp.einsum('ehd,hd->eh', e, attn)
            m = jax.ops.segment_max(logits, dst, num_segments=N)
            ex = jnp.exp(logits - m[dst])
            denom = jax.ops.segment_sum(ex, dst, num_segments=N)
            alpha = ex / denom[dst]
            out = jax.ops.segment_sum(alpha[:, :, None] * fs[src], dst, num_segments=N)
            return jax.nn.elu(out)
        key = jax.random.key(seed)
        ks = jax.random.split(key, 10)
        s = 1.0 / np.sqrt(DIM)
        return {'x': jax.random.normal(ks[0], (N, DIM), jnp.float32), 'src': jax.random.randint(ks[1], (E,), 0, N, jnp.int32), 'dst': jax.random.randint(ks[2], (E,), 0, N, jnp.int32), 'W1s': jax.random.normal(ks[3], (DIM, DIM), jnp.float32) * s, 'b1s': jnp.zeros((DIM,), jnp.float32), 'W1d': jax.random.normal(ks[4], (DIM, DIM), jnp.float32) * s, 'b1d': jnp.zeros((DIM,), jnp.float32), 'attn1': jax.random.normal(ks[5], (HEADS, HD), jnp.float32) * s, 'ln1_w': jnp.ones((DIM,), jnp.float32), 'ln1_b': jnp.zeros((DIM,), jnp.float32), 'Wos': jax.random.normal(ks[6], (DIM, DIM), jnp.float32) * s, 'bos': jnp.zeros((DIM,), jnp.float32), 'Wod': jax.random.normal(ks[7], (DIM, DIM), jnp.float32) * s, 'bod': jnp.zeros((DIM,), jnp.float32), 'attno': jax.random.normal(ks[8], (1, DIM), jnp.float32) * s, 'lno_w': jnp.ones((DIM,), jnp.float32), 'lno_b': jnp.zeros((DIM,), jnp.float32)}
    _L0_gnn_all = _L0_gnn_setup()
    _L0_gnn_in = {k: v for k, v in _L0_gnn_all.items() if k in ('W1s', 'b1s', 'W1d', 'b1d', 'attn1', 'ln1_w', 'ln1_b', 'Wos', 'bos', 'Wod', 'bod', 'attno', 'lno_w', 'lno_b')}
    del _L0_gnn_all

    def _L1_gnn_setup():
        import jax, jax.numpy as jnp
        import numpy as np
        N_NODES = 625
        N_EDGES = 6250
        N_REL = 34
        DIM = 768

        def _graph_encoder(x, edge_index, edge_type, W_rel, W_root, b_rgcn, W_gcn, b_gcn):
            n = x.shape[0]
            src, dst = (edge_index[0], edge_index[1])
            ones = jnp.ones((src.shape[0],), dtype=x.dtype)
            seg = edge_type * n + dst
            agg = jax.ops.segment_sum(x[src], seg, num_segments=N_REL * n)
            cnt = jax.ops.segment_sum(ones, seg, num_segments=N_REL * n)
            mean = agg.reshape(N_REL, n, -1) / jnp.maximum(cnt, 1.0).reshape(N_REL, n, 1)
            h1 = jnp.einsum('rni,rio->no', mean, W_rel) + x @ W_root + b_rgcn
            xw = h1 @ W_gcn
            deg = jax.ops.segment_sum(ones, dst, num_segments=n) + 1.0
            dinv = jax.lax.rsqrt(deg)
            norm = dinv[src] * dinv[dst]
            out = jax.ops.segment_sum(xw[src] * norm[:, None], dst, num_segments=n)
            out = out + xw * (dinv * dinv)[:, None]
            return out + b_gcn
        key = jax.random.key(seed)
        ks = jax.random.split(key, 6)
        scale = 1.0 / np.sqrt(DIM)
        x = jax.random.normal(ks[0], (N_NODES, DIM), dtype=jnp.float32)
        edge_index = jax.random.randint(ks[1], (2, N_EDGES), 0, N_NODES, dtype=jnp.int32)
        edge_type = jax.random.randint(ks[2], (N_EDGES,), 0, N_REL, dtype=jnp.int32)
        W_rel = jax.random.normal(ks[3], (N_REL, DIM, DIM), dtype=jnp.float32) * scale
        W_root = jax.random.normal(ks[4], (DIM, DIM), dtype=jnp.float32) * scale
        b_rgcn = jnp.zeros((DIM,), dtype=jnp.float32)
        W_gcn = jax.random.normal(ks[5], (DIM, DIM), dtype=jnp.float32) * scale
        b_gcn = jnp.zeros((DIM,), dtype=jnp.float32)
        return {'x': x, 'edge_index': edge_index, 'edge_type': edge_type, 'W_rel': W_rel, 'W_root': W_root, 'b_rgcn': b_rgcn, 'W_gcn': W_gcn, 'b_gcn': b_gcn}
    _L1_gnn_all = _L1_gnn_setup()
    _L1_gnn_in = {k: v for k, v in _L1_gnn_all.items() if k in ('W_rel', 'W_root', 'b_rgcn', 'W_gcn', 'b_gcn')}
    del _L1_gnn_all
    return {'x': x, 'src': src, 'dst': dst, 'edge_type_34': edge_type_34, 'L0_gnn_W1s': _L0_gnn_in['W1s'], 'L0_gnn_b1s': _L0_gnn_in['b1s'], 'L0_gnn_W1d': _L0_gnn_in['W1d'], 'L0_gnn_b1d': _L0_gnn_in['b1d'], 'L0_gnn_attn1': _L0_gnn_in['attn1'], 'L0_gnn_ln1_w': _L0_gnn_in['ln1_w'], 'L0_gnn_ln1_b': _L0_gnn_in['ln1_b'], 'L0_gnn_Wos': _L0_gnn_in['Wos'], 'L0_gnn_bos': _L0_gnn_in['bos'], 'L0_gnn_Wod': _L0_gnn_in['Wod'], 'L0_gnn_bod': _L0_gnn_in['bod'], 'L0_gnn_attno': _L0_gnn_in['attno'], 'L0_gnn_lno_w': _L0_gnn_in['lno_w'], 'L0_gnn_lno_b': _L0_gnn_in['lno_b'], 'L1_gnn_W_rel': _L1_gnn_in['W_rel'], 'L1_gnn_W_root': _L1_gnn_in['W_root'], 'L1_gnn_b_rgcn': _L1_gnn_in['b_rgcn'], 'L1_gnn_W_gcn': _L1_gnn_in['W_gcn'], 'L1_gnn_b_gcn': _L1_gnn_in['b_gcn']}

def reference(x, src, dst, edge_type_34, L0_gnn_W1s, L0_gnn_b1s, L0_gnn_W1d, L0_gnn_b1d, L0_gnn_attn1, L0_gnn_ln1_w, L0_gnn_ln1_b, L0_gnn_Wos, L0_gnn_bos, L0_gnn_Wod, L0_gnn_bod, L0_gnn_attno, L0_gnn_lno_w, L0_gnn_lno_b, L1_gnn_W_rel, L1_gnn_W_root, L1_gnn_b_rgcn, L1_gnn_W_gcn, L1_gnn_b_gcn):
    import jax
    import jax.numpy as jnp

    def _L0_gnn_ref(x, src, dst, W1s, b1s, W1d, b1d, attn1, ln1_w, ln1_b, Wos, bos, Wod, bod, attno, lno_w, lno_b):
        import jax, jax.numpy as jnp
        import numpy as np
        N, E, DIM, HEADS = (1250, 20000, 768, 8)
        HD = DIM // HEADS
        EPS = 1e-05

        def layer_norm(x, w, b):
            mu = jnp.mean(x, axis=-1, keepdims=True)
            var = jnp.var(x, axis=-1, keepdims=True)
            return (x - mu) * jax.lax.rsqrt(var + EPS) * w + b

        def gatv2(x, src, dst, Ws, bs, Wd, bd, attn):
            H, D = attn.shape
            fs = (x @ Ws + bs).reshape(-1, H, D)
            fd = (x @ Wd + bd).reshape(-1, H, D)
            e = jax.nn.leaky_relu(fs[src] + fd[dst], 0.2)
            logits = jnp.einsum('ehd,hd->eh', e, attn)
            m = jax.ops.segment_max(logits, dst, num_segments=N)
            ex = jnp.exp(logits - m[dst])
            denom = jax.ops.segment_sum(ex, dst, num_segments=N)
            alpha = ex / denom[dst]
            out = jax.ops.segment_sum(alpha[:, :, None] * fs[src], dst, num_segments=N)
            return jax.nn.elu(out)
        h = gatv2(x, src, dst, W1s, b1s, W1d, b1d, attn1).reshape(N, DIM)
        h = layer_norm(h + x, ln1_w, ln1_b)
        out = gatv2(h, src, dst, Wos, bos, Wod, bod, attno).reshape(N, DIM)
        return layer_norm(out, lno_w, lno_b)

    def _L1_gnn_ref(x, edge_index, edge_type, W_rel, W_root, b_rgcn, W_gcn, b_gcn):
        import jax, jax.numpy as jnp
        import numpy as np
        N_NODES = 625
        N_EDGES = 6250
        N_REL = 34
        DIM = 768

        def _graph_encoder(x, edge_index, edge_type, W_rel, W_root, b_rgcn, W_gcn, b_gcn):
            n = x.shape[0]
            src, dst = (edge_index[0], edge_index[1])
            ones = jnp.ones((src.shape[0],), dtype=x.dtype)
            seg = edge_type * n + dst
            agg = jax.ops.segment_sum(x[src], seg, num_segments=N_REL * n)
            cnt = jax.ops.segment_sum(ones, seg, num_segments=N_REL * n)
            mean = agg.reshape(N_REL, n, -1) / jnp.maximum(cnt, 1.0).reshape(N_REL, n, 1)
            h1 = jnp.einsum('rni,rio->no', mean, W_rel) + x @ W_root + b_rgcn
            xw = h1 @ W_gcn
            deg = jax.ops.segment_sum(ones, dst, num_segments=n) + 1.0
            dinv = jax.lax.rsqrt(deg)
            norm = dinv[src] * dinv[dst]
            out = jax.ops.segment_sum(xw[src] * norm[:, None], dst, num_segments=n)
            out = out + xw * (dinv * dinv)[:, None]
            return out + b_gcn
        return _graph_encoder(x, edge_index, edge_type, W_rel, W_root, b_rgcn, W_gcn, b_gcn)
    edge_index = jnp.stack([src, dst])
    h = jnp.maximum(_layernorm(x, axis=-1), 0.0)
    x = x + _L0_gnn_ref(h, src, dst, L0_gnn_W1s, L0_gnn_b1s, L0_gnn_W1d, L0_gnn_b1d, L0_gnn_attn1, L0_gnn_ln1_w, L0_gnn_ln1_b, L0_gnn_Wos, L0_gnn_bos, L0_gnn_Wod, L0_gnn_bod, L0_gnn_attno, L0_gnn_lno_w, L0_gnn_lno_b)
    h = jnp.maximum(_layernorm(x, axis=-1), 0.0)
    x = x + _L1_gnn_ref(h, edge_index, edge_type_34, L1_gnn_W_rel, L1_gnn_W_root, L1_gnn_b_rgcn, L1_gnn_W_gcn, L1_gnn_b_gcn)
    return x

_drawn_inputs = setup_inputs


def setup_inputs(seed=0):
    import zlib

    import numpy as np

    out = dict(_drawn_inputs(seed))
    spreads = {'L0_gnn_b1s': (0.0, 0.1),
     'L0_gnn_b1d': (0.0, 0.8),
     'L0_gnn_ln1_w': (1.0, 0.2),
     'L0_gnn_ln1_b': (0.0, 0.1),
     'L0_gnn_bos': (0.0, 0.1),
     'L0_gnn_bod': (0.0, 0.8),
     'L0_gnn_lno_w': (1.0, 0.2),
     'L0_gnn_lno_b': (0.0, 0.1),
     'L1_gnn_b_rgcn': (0.0, 0.1),
     'L1_gnn_b_gcn': (0.0, 0.1)}
    factors = {'L0_gnn_W1d': 8.0, 'L0_gnn_attn1': 3.369}
    for name, (base, spread) in spreads.items():
        noise = np.random.default_rng([zlib.crc32(name.encode()), seed]).standard_normal(out[name].shape)
        drawn = base * np.exp(spread * noise) if base else spread * noise
        out[name] = jnp.asarray(drawn.astype(out[name].dtype))
    for name, factor in factors.items():
        out[name] = (out[name] * factor).astype(out[name].dtype)
    return out
```

```python
import concourse.bass as bass
from concourse import mybir
from contextlib import ExitStack, contextmanager

F32, I32, BF16 = mybir.dt.float32, mybir.dt.int32, mybir.dt.bfloat16
ALU = mybir.AluOpType
ACT = mybir.ActivationFunctionType
X = mybir.AxisListType.X
ds = bass.ds

N, E, D, HEADS, RELS = 1250, 20000, 768, 8, 34
P = 128
NT = (N + P - 1) // P
NP = NT * P
LAST = N - (NT - 1) * P
EP, EC = 125, 160
assert EP * EC == E
KC = D // P
W = D + HEADS
HALF = D // 2
ROWS_AHEAD = 2
S = 4
U = 4
TBACK = 2
NROW = NP
ZB = 16
ZBLOCKS = -(-(E // S + U) // ZB)
GROUPS = ZBLOCKS * ZB
TG = 5120
MAX_TURNS = (E // S + NT) // U + 1
RT = E // P + RELS
BIG = 1e30
EPS = 1e-5
DA, DB = 40, 32


class Steps:

    def __init__(self, eng, sem, base=0, carrier=None):
        self.eng, self.sem, self.base, self.n, self.carrier = eng, sem, base, 0, carrier

    def mark(self, ins):
        ins.then_inc(self.sem, 1)
        self.n += 1
        return self.n

    def wait(self, n=None):
        self.eng.wait_ge(self.sem, self.base + (self.n if n is None else n))
        if self.carrier is not None:
            self.eng.sem_inc(self.carrier, 1)

    def tick(self):
        self.eng.sem_inc(self.sem, 1)
        self.n += 1

    def link(self, ins):
        self.mark(ins)
        self.wait()


def over(ap, axis, shape):
    return ap.unsqueeze(axis).to_broadcast(shape)


def gnn_kernel(nc, io, out):
    ctx = ExitStack()
    with ctx:
        taken = {}

        def fresh(name):
            taken[name] = taken.get(name, 0) + 1
            return name if taken[name] == 1 else f"{name}_{taken[name]}"

        def sb(name, shape, dt, where=ctx):
            return where.enter_context(nc.sbuf_tensor(fresh(name), shape, dt))

        def pb(name, shape, dt, where):
            return where.enter_context(nc.psum_tensor(fresh(name), shape, dt))

        def dram(name, shape, dt):
            return nc.dram_tensor(name, shape, dt, kind="Internal").ap()

        deg_d = dram("deg_d", (NP,), F32)
        by_rank_d = dram("by_rank_d", (NP, 2), I32)
        tile_of_group_d = dram("tile_of_group_d", (TG,), I32)
        slots_d = dram("slots_d", (GROUPS * NROW * S, 2), I32)
        byrel_d = dram("byrel_d", (RT * P, 1), I32)
        h0_d = dram("h0_d", (NP, D), F32)
        fs_d = dram("fs_d", (NP, W), F32)
        fd_d = dram("fd_d", (NP, W), F32)

        ident = sb("ident", [P, P], F32)
        ones = sb("ones", [P, P], F32)
        ctl = sb("ctl", [1, 64], I32)
        C_TURNS, C_ZERO, C_RANKS, C_BEHIND, C_REL = 0, 1, 2, 3, 8
        tile_of_group = sb("tile_of_group", [1, TG], I32)
        perm = sb("perm", [P, NT + 1], I32)
        permc = sb("permc", [P, NT + 1], I32)
        degr = sb("degr", [P, NT + 1], F32)
        relbase = sb("relbase", [P, RELS + 1], F32)
        recs = sb("recs", [EP, EC, 2], I32)
        slotpos = sb("slotpos", [EP, EC], I32)
        dstf = sb("dstf", [EP, EC], F32)
        ksort = sb("ksort", [EP, EC], F32)
        unsorted = sb("unsorted", [P, 1], F32)
        zero_i = sb("zero_i", [P, 1], I32)
        nrow = sb("nrow", [P, NP], F32)

        def sems(where, *names):
            made = [nc.alloc_semaphore(fresh(n)) for n in names]
            where.semaphores += made
            return made

        @contextmanager
        def stage():
            with ExitStack() as st:
                st.semaphores = []
                yield st
                nc.clear_and_free_semaphores(st.semaphores)
                nc.all_engine_barrier()

        with stage() as st:
            lower = sb("lower", [P, P], F32, st)
            before = sb("before", [P, P], F32, st)
            mrow = sb("mrow", [P, 1792], F32, st)
            arow = sb("arow", [P, DA], F32, st)
            eidx = sb("eidx", [EP, EC], F32, st)
            gidx = sb("gidx", [P, TG // P], F32, st)
            ncol = sb("ncol", [P, NT], F32, st)
            zeros = sb("zeros", [P, ZB * NROW * S * 2 // P], I32, st)
            dsti = sb("dsti", [EP, EC], I32, st)
            srci = sb("srci", [EP, EC], I32, st)
            typi = sb("typi", [EP, EC], I32, st)
            previ = sb("previ", [EP, EC], I32, st)
            ai = sb("ai", [EP, EC], I32, st)
            bi = sb("bi", [EP, EC], I32, st)
            af = sb("af", [EP, EC], F32, st)
            bf = sb("bf", [EP, EC], F32, st)
            oa = sb("oa", [EP, EC, DA], BF16, st)
            ob = sb("ob", [EP, EC, DB], BF16, st)
            ot = sb("ot", [EP, RELS, EC], F32, st)
            sc = sb("sc", [EP, RELS, EC], F32, st)
            cn = sb("cn", [EP, RELS], F32, st)
            reli = sb("reli", [P, RELS], I32, st)
            relt = sb("relt", [P, RELS], F32, st)
            rele = sb("rele", [P, RELS], F32, st)
            adj = sb("adj", [EP, RELS], F32, st)
            place = sb("place", [EP, EC], F32, st)
            start = sb("start", [EP, EC], F32, st)
            diag = sb("diag", [EP, EP], F32, st)
            carry = sb("carry", [EP, 1], F32, st)
            back = sb("back", [EP, 1], F32, st)
            degab = sb("degab", [DA, DB], F32, st)
            keyrow = sb("keyrow", [P, NP], F32, st)
            keycol = sb("keycol", [P, NT], F32, st)
            junk = sb("junk", [P, 1792], F32, st)
            rank = sb("rank", [P, NT], F32, st)
            ranki = sb("ranki", [P, NT], I32, st)
            nodeinfo = sb("nodeinfo", [P, NT, 2], I32, st)
            byrank = sb("byrank", [P, NT, 2], I32, st)
            kmax = sb("kmax", [P, NT], F32, st)
            kmaxi = sb("kmaxi", [P, NT], I32, st)
            gend = sb("gend", [P, NT], F32, st)
            small = sb("small", [P, 4], F32, st)
            tog = sb("tog", [P, TG // P], F32, st)
            togi = sb("togi", [P, TG // P], I32, st)
            p_deg = pb("p_deg", [DA, 512], F32, st)
            p_rel = pb("p_rel", [P, 512], F32, st)
            p_tot = pb("p_tot", [P, 512], F32, st)
            p_car = pb("p_car", [P, 512], F32, st)
            p_uns = pb("p_uns", [P, 512], F32, st)
            (const_built, dve_step, edges_in, prev_in, onehots, degrees, counted, relsums, starts,
             carries, deg_sb, deg_out, deg_in, ranks, by_rank_out, by_rank_in, maxima, tog_ready,
             tog_out, tog_in, zero_ready, clear, degr_ready, cleared, rel_clear) = sems(
                 st, "const_built", "dve_step", "edges_in", "prev_in", "onehots", "degrees",
                 "counted", "relsums", "starts", "carries", "deg_sb", "deg_out", "deg_in", "ranks",
                 "by_rank_out", "by_rank_in", "maxima", "tog_ready", "tog_out", "tog_in",
                 "zero_ready", "clear", "degr_ready", "cleared",
                 "rel_clear")
            CONSTS = 15
            with nc.Block() as block:
                @block.sync
                def _(sp):
                    e2 = lambda a: a.rearrange("(p c) -> p c", p=EP)
                    sp.dma_start(dsti[:], e2(io["dst"])).then_inc(edges_in, 16)
                    sp.dma_start(typi[:], e2(io["edge_type_34"])).then_inc(edges_in, 16)
                    sp.dma_start(srci[:], e2(io["src"])).then_inc(edges_in, 16)
                    sp.dma_start(previ[1:EP, 0:1], e2(io["dst"])[0:EP - 1, EC - 1:EC],
                                 allow_slow_non_contiguous=True).then_inc(prev_in, 16)
                    sp.wait_ge(deg_sb, 1)
                    sp.dma_start(deg_d.rearrange("(a b) -> a b", a=DA), degab[:]).then_inc(deg_out, 16)
                    sp.wait_ge(deg_out, 16)
                    sp.dma_start(keyrow[:], deg_d.partition_broadcast(P)).then_inc(deg_in, 16)
                    sp.dma_start(keycol[:], deg_d.rearrange("(t p) -> p t", p=P),
                                 allow_slow_non_contiguous=True).then_inc(deg_in, 16)
                    sp.wait_ge(by_rank_out, 16 * NT)
                    sp.dma_start(byrank[:], by_rank_d.rearrange("(t p) c -> p t c", p=P)).then_inc(by_rank_in, 16)
                    sp.wait_ge(tog_ready, 1)
                    sp.dma_start(tile_of_group_d.rearrange("(p c) -> p c", p=P), togi[:]).then_inc(tog_out, 16)
                    sp.wait_ge(tog_out, 16)
                    sp.dma_start(tile_of_group[:], tile_of_group_d.unsqueeze(0)).then_inc(tog_in, 16)
                    n_zero = sp.value_load(ctl[0:1, C_ZERO:C_ZERO + 1], min_val=1, max_val=ZBLOCKS)
                    slots_z = slots_d.rearrange("(z p f) c -> z p (f c)", z=ZBLOCKS, p=P)
                    sp.wait_ge(zero_ready, 1)
                    with sp.Fori(0, n_zero) as z:
                        sp.wait_ge(clear, z * 16)
                        sp.dma_start(slots_z[ds(z, 1)].rearrange("z p f -> (z p) f"), zeros[:]).then_inc(clear, 16)
                    sp.dma_start(byrel_d.rearrange("(p f) o -> p (f o)", p=P), zeros[:, 0:RT]).then_inc(rel_clear, 16)
                    sp.wait_ge(rel_clear, 16)
                    sp.wait_ge(clear, n_zero * 16)
                    sp.sem_inc(cleared, 1)
                    sp.wait_ge(tog_in, 16)

                @block.gpsimd
                def _(pool):
                    c = Steps(pool, const_built)
                    iota = dict(allow_small_or_imprecise_dtypes=True)
                    pool.memset(zeros[:], 0).then_inc(zero_ready, 1)
                    c.mark(pool.memset(zero_i[:], 0))
                    c.mark(pool.memset(ones[:], 1.0))
                    c.mark(pool.iota(arow[:], [[1, DA]], base=0, channel_multiplier=0, **iota))
                    c.mark(pool.iota(eidx[:], [[1, EC]], base=0, channel_multiplier=EC, **iota))
                    c.mark(pool.memset(previ[0:1, 0:1], -1))
                    c.mark(pool.memset(lower[:], 1.0))
                    c.mark(pool.memset(before[:], 1.0))
                    c.link(pool.memset(ident[:], 0.0))
                    c.mark(pool.affine_select(out=ident[:], in_=ident[:], compare_op=ALU.not_equal, fill=1.0,
                                              base=0, pattern=[[-1, P]], channel_multiplier=1))
                    c.mark(pool.affine_select(out=lower[:], in_=lower[:], compare_op=ALU.is_gt, fill=0.0,
                                              base=0, pattern=[[1, P]], channel_multiplier=-1))
                    c.mark(pool.affine_select(out=before[:], in_=before[:], compare_op=ALU.is_gt, fill=0.0,
                                              base=0, pattern=[[-1, P]], channel_multiplier=1))
                    c.mark(pool.iota(mrow[:], [[1, 1792]], base=0, channel_multiplier=0, **iota))
                    c.mark(pool.iota(nrow[:], [[1, NP]], base=0, channel_multiplier=0, **iota))
                    c.mark(pool.iota(gidx[:], [[1, TG // P]], base=-TBACK, channel_multiplier=TG // P, **iota))
                    c.mark(pool.iota(ncol[:], [[P, NT]], base=0, channel_multiplier=1, **iota))
                    assert c.n == CONSTS
                    pool.wait_ge(ranks, 1)
                    for t in range(NT):
                        pool.indirect_dma_start(by_rank_d, bass.IndirectOffsetOnAxis(ap=ranki[:, t:t + 1], axis=0),
                                                nodeinfo[:, t, :], None).then_inc(by_rank_out, 16)
                    pool.wait_ge(by_rank_out, 16 * NT)
                    pool.wait_ge(degr_ready, 1)
                    pool.partition_all_reduce(kmax[:], degr[:, 0:NT], P, bass.bass_isa.ReduceOp.max).then_inc(maxima, 1)

                @block.tensor
                def _(pe):
                    pe.wait_ge(onehots, 1)
                    for c in range(EC):
                        last = pe.matmul(p_deg[:, 0:DB], oa[:, c, :], ob[:, c, :], start=c == 0, stop=c == EC - 1)
                    last.then_inc(degrees, 1)
                    pe.wait_ge(counted, 1)
                    pe.wait_ge(const_built, CONSTS)
                    pe.matmul(p_rel[0:EP, 0:RELS], lower[0:EP, 0:EP], cn[:], start=True, stop=True)
                    pe.matmul(p_tot[:, 0:RELS], ones[0:EP, :], cn[:], start=True, stop=True).then_inc(relsums, 1)
                    pe.wait_ge(starts, 1)
                    pe.matmul(p_car[0:EP, 0:EP], ones[0:EP, 0:EP], diag[:], start=True, stop=True)
                    pe.matmul(p_uns[:, 0:1], ones[0:EP, :], back[:], start=True, stop=True).then_inc(carries, 1)

                @block.vector
                def _(dve):
                    v = Steps(dve, dve_step)
                    e3 = [EP, EC, DA]
                    dve.wait_ge(edges_in, 48)
                    dve.wait_ge(const_built, CONSTS)
                    v.link(dve.memset(ctl[:], 0))
                    v.mark(dve.tensor_scalar(ai[:], dsti[:], 5, None, ALU.logical_shift_right))
                    v.mark(dve.tensor_scalar(bi[:], dsti[:], DB - 1, None, ALU.bitwise_and))
                    v.link(dve.tensor_copy(dstf[:], dsti[:]))
                    v.mark(dve.tensor_copy(af[:], ai[:]))
                    v.link(dve.tensor_copy(bf[:], bi[:]))
                    v.mark(dve.tensor_tensor(oa[:], over(af[:], 2, e3), over(arow[0:EP], 1, e3), ALU.is_equal))
                    e3 = [EP, EC, DB]
                    v.link(dve.tensor_tensor(ob[:], over(bf[:], 2, e3), over(arow[0:EP, 0:DB], 1, e3), ALU.is_equal))
                    dve.sem_inc(onehots, 1)
                    r3 = [EP, RELS, EC]
                    v.link(dve.tensor_copy(af[:], typi[:]))
                    v.link(dve.tensor_tensor(ot[:], over(af[:], 1, r3), over(arow[0:EP, 0:RELS], 2, r3), ALU.is_equal))
                    v.link(dve.tensor_reduce(cn[:], ot[:], X, ALU.add))
                    dve.sem_inc(counted, 1)
                    flat = "p r c -> p (r c)"
                    v.link(dve.tensor_tensor_scan(sc[:].rearrange(flat), ot[:].rearrange(flat), ot[:].rearrange(flat),
                                                  0.0, ALU.add, ALU.max))
                    dve.wait_ge(relsums, 1)
                    v.link(dve.tensor_scalar(relt[:], p_tot[:, 0:RELS], float(P - 1), None, ALU.add))
                    v.link(dve.tensor_copy(reli[:], relt[:]))
                    v.link(dve.tensor_scalar(reli[:], reli[:], 7, None, ALU.logical_shift_right))
                    v.link(dve.tensor_scalar(relt[:], reli[:], 1.0, None, ALU.max))
                    v.link(dve.tensor_tensor_scan(rele[:], relt[:], relt[:], 0.0, ALU.add, ALU.max))
                    v.mark(dve.tensor_copy(ctl[0:1, C_REL:C_REL + RELS], rele[0:1, :]))
                    v.mark(dve.memset(ctl[0:1, C_REL - 1:C_REL], 0))
                    v.mark(dve.tensor_scalar(ctl[0:1, C_BEHIND:C_BEHIND + 1], rele[0:1, RELS - 1:RELS], -1.0,
                                             float(RT + 1), ALU.mult, ALU.add))
                    v.mark(dve.memset(relbase[:, RELS:RELS + 1], BIG))
                    v.link(dve.tensor_tensor(relt[:], rele[:], relt[:], ALU.subtract))
                    v.link(dve.tensor_scalar(relbase[:, 0:RELS], relt[:], float(P), None, ALU.mult))
                    v.link(dve.tensor_tensor(adj[:], relbase[0:EP, 0:RELS], p_rel[0:EP, 0:RELS], ALU.add))
                    v.link(dve.tensor_tensor(adj[:], adj[:], cn[:], ALU.add))
                    v.link(dve.tensor_tensor(adj[:], adj[:], sc[:, :, EC - 1], ALU.subtract))
                    v.link(dve.tensor_tensor(sc[:], sc[:], over(adj[:], 2, r3), ALU.add))
                    v.link(dve.tensor_tensor(sc[:], sc[:], ot[:], ALU.mult))
                    v.link(dve.tensor_reduce(place[:], sc[:].rearrange("p r c -> p c r"), X, ALU.add))
                    v.mark(dve.tensor_scalar(recs[:, :, 1], place[:], -1.0, None, ALU.add))
                    v.mark(dve.tensor_copy(recs[:, :, 0], srci[:]))
                    dve.wait_ge(prev_in, 16)
                    v.link(dve.tensor_copy(previ[:, 1:EC], dsti[:, 0:EC - 1]))
                    v.link(dve.tensor_copy(bf[:], previ[:]))
                    v.mark(dve.tensor_tensor(start[:], dstf[:], bf[:], ALU.not_equal))
                    v.link(dve.tensor_tensor(af[:], dstf[:], bf[:], ALU.is_lt))
                    v.mark(dve.tensor_reduce(back[:], af[:], X, ALU.max))
                    v.link(dve.tensor_tensor(start[:], start[:], eidx[:], ALU.mult))
                    v.link(dve.tensor_tensor_scan(bf[:], start[:], start[:], 0.0, ALU.max, ALU.max))
                    v.link(dve.tensor_scalar(diag[:], ident[0:EP, 0:EP], bf[:, EC - 1:EC], None, ALU.mult))
                    dve.sem_inc(starts, 1)
                    dve.wait_ge(carries, 1)
                    v.mark(dve.tensor_tensor_reduce(out=junk[0:EP, 0:EP], in0=p_car[0:EP, 0:EP], in1=before[0:EP, 0:EP],
                                                    scale=1.0, scalar=0.0, op0=ALU.mult, op1=ALU.max,
                                                    accum_out=carry[:]))
                    v.link(dve.tensor_scalar(unsorted[:], p_uns[:, 0:1], 1.0, None, ALU.min))
                    v.mark(dve.tensor_scalar(ctl[0:1, C_RANKS:C_RANKS + 1], unsorted[0:1, :], float(EC - 1), 1.0,
                                             ALU.mult, ALU.add))
                    v.link(dve.tensor_scalar(bf[:], bf[:], carry[:], None, ALU.max))
                    v.link(dve.tensor_tensor(ksort[:], eidx[:], bf[:], ALU.subtract))
                    dve.wait_ge(degrees, 1)
                    v.link(dve.tensor_copy(degab[:], p_deg[:, 0:DB]))
                    dve.sem_inc(deg_sb, 1)
                    dve.wait_ge(deg_in, 32)
                    v.mark(dve.tensor_copy(nodeinfo[:, :, 0], ncol[:]))
                    v.link(dve.tensor_copy(nodeinfo[:, :, 1], keycol[:]))
                    v.mark(dve.tensor_scalar(keyrow[:], keyrow[:], 4095.0, 2048.0, ALU.min, ALU.mult))
                    v.link(dve.tensor_scalar(keycol[:], keycol[:], 4095.0, 2048.0, ALU.min, ALU.mult))
                    v.mark(dve.tensor_tensor(keyrow[:], keyrow[:], nrow[:], ALU.subtract))
                    v.link(dve.tensor_tensor(keycol[:], keycol[:], ncol[:], ALU.subtract))
                    for t in range(NT):
                        v.link(dve.tensor_scalar(junk[:, 0:NP], keyrow[:], keycol[:, t:t + 1], 0.0, ALU.is_gt, ALU.add,
                                                 accum_out=rank[:, t:t + 1]))
                    v.link(dve.tensor_copy(ranki[:], rank[:]))
                    dve.sem_inc(ranks, 1)
                    dve.wait_ge(by_rank_in, 16)
                    v.mark(dve.memset(perm[:, NT:NT + 1], NP - 1))
                    v.mark(dve.memset(degr[:, NT:NT + 1], 0.0))
                    v.mark(dve.tensor_copy(perm[:, 0:NT], byrank[:, :, 0]))
                    v.link(dve.tensor_copy(degr[:, 0:NT], byrank[:, :, 1]))
                    dve.sem_inc(degr_ready, 1)
                    v.mark(dve.tensor_scalar(permc[:], perm[:], float(N - 1), None, ALU.min))
                    dve.wait_ge(maxima, 1)
                    v.link(dve.tensor_reduce(small[:, 0:1], kmax[:], X, ALU.max))
                    v.link(dve.tensor_scalar(kmaxi[:], kmax[:], float(S - 1), None, ALU.add))
                    v.link(dve.tensor_scalar(kmaxi[:], kmaxi[:], 2, None, ALU.logical_shift_right))
                    v.link(dve.tensor_copy(kmax[:], kmaxi[:]))
                    v.link(dve.tensor_tensor_scan(gend[:], kmax[:], kmax[:], 0.0, ALU.add, ALU.max))
                    v.mark(dve.tensor_scalar(small[:, 2:3], small[:, 0:1], 1.0 / (S * ZB), None, ALU.mult))
                    v.link(dve.tensor_scalar(small[:, 3:4], gend[:, NT - 1:NT], 1.0 / U, -0.125, ALU.mult, ALU.add))
                    v.link(dve.tensor_scalar(junk[:], mrow[:], small[:, 2:3], 0.0, ALU.is_lt, ALU.add,
                                             accum_out=small[:, 0:1]))
                    v.link(dve.tensor_scalar(junk[:], mrow[:], small[:, 3:4], 0.0, ALU.is_lt, ALU.add,
                                             accum_out=small[:, 1:2]))
                    v.mark(dve.tensor_scalar(ctl[0:1, C_ZERO:C_ZERO + 1], small[0:1, 0:1], 1.0, None, ALU.max))
                    v.mark(dve.tensor_scalar(ctl[0:1, C_TURNS:C_TURNS + 1], small[0:1, 1:2], 1.0, None, ALU.max))
                    v.link(dve.memset(tog[:], 0.0))
                    for t in range(NT):
                        v.link(dve.scalar_tensor_tensor(out=tog[:], in0=gidx[:], scalar=gend[:, t:t + 1], in1=tog[:],
                                                        op0=ALU.is_ge, op1=ALU.add))
                    v.link(dve.tensor_copy(togi[:], tog[:]))
                    dve.sem_inc(tog_ready, 1)

        with stage() as st:
            lowb = sb("lowb", [EP, EP], BF16, st)
            onesb = sb("onesb", [EP, EP], BF16, st)
            onehot = sb("onehot", [EP, NP], BF16, st)
            seen = sb("seen", [EP, NP], F32, st)
            ahead = sb("ahead", [EP, NP], F32, st)
            kcol = sb("kcol", [EP, 1], F32, st)
            dcol = sb("dcol", [EP, 1], F32, st)
            kgen = sb("kgen", [EP, EC], F32, st)
            ki = sb("ki", [EP, EC], I32, st)
            hi = sb("hi", [EP, EC], I32, st)
            p_low = pb("p_low", [P, 3, 512], F32, st)
            p_all = pb("p_all", [P, 3, 512], F32, st)
            tri, step2, hot_ready, sums = sems(st, "tri", "step2", "hot_ready", "sums")
            BANKS = [(0, 512), (1, 512), (2, NP - 1024)]
            with nc.Block() as block:
                @block.gpsimd
                def _(pool):
                    pool.memset(onesb[:], 1.0).then_inc(tri, 1)
                    pool.memset(lowb[:], 1.0).then_inc(tri, 1)
                    pool.wait_ge(tri, 2)
                    pool.affine_select(out=lowb[:], in_=lowb[:], compare_op=ALU.is_gt, fill=0.0, base=0,
                                       pattern=[[1, EP]], channel_multiplier=-1).then_inc(tri, 1)

                @block.tensor
                def _(pe):
                    n = pe.value_load(ctl[0:1, C_RANKS:C_RANKS + 1], min_val=1, max_val=EC)
                    pe.wait_ge(tri, 3)
                    with pe.Fori(0, n) as c:
                        pe.wait_ge(hot_ready, c + 1)
                        for q, w in BANKS:
                            pe.matmul(p_low[0:EP, q, 0:w], lowb[:], onehot[:, q * 512:q * 512 + w], start=True, stop=True)
                        for q, w in BANKS:
                            last = pe.matmul(p_all[0:EP, q, 0:w], onesb[:], onehot[:, q * 512:q * 512 + w],
                                             start=True, stop=True)
                        last.then_inc(sums, 1)

                @block.vector
                def _(dve):
                    n = dve.value_load(ctl[0:1, C_RANKS:C_RANKS + 1], min_val=1, max_val=EC)
                    v = Steps(dve, step2)
                    v.mark(dve.memset(kgen[:], 0.0))
                    v.link(dve.memset(seen[:], 0.0))
                    PER = 7
                    with dve.Fori(0, n) as c:
                        w = Steps(dve, step2, c * PER + v.n)
                        w.wait()
                        w.link(dve.tensor_copy(dcol[:], dstf[:, ds(c, 1)]))
                        w.link(dve.tensor_scalar(onehot[:], nrow[0:EP, :], dcol[:], None, ALU.is_equal))
                        dve.sem_inc(hot_ready, 1)
                        dve.wait_ge(sums, c + 1)
                        w.link(dve.tensor_tensor(ahead[:], seen[:], p_low[0:EP].rearrange("p q f -> p (q f)")[:, 0:NP],
                                                 ALU.add))
                        w.link(dve.tensor_tensor(ahead[:], ahead[:], onehot[:], ALU.mult))
                        w.link(dve.tensor_reduce(kcol[:], ahead[:], X, ALU.add))
                        w.mark(dve.tensor_copy(kgen[:, ds(c, 1)], kcol[:]))
                        w.mark(dve.tensor_tensor(seen[:], seen[:], p_all[0:EP].rearrange("p q f -> p (q f)")[:, 0:NP],
                                                 ALU.add))
                        assert w.n == PER
                    v.base = n * PER
                    v.wait()
                    v.link(dve.tensor_tensor(kgen[:], kgen[:], ksort[:], ALU.subtract))
                    v.link(dve.scalar_tensor_tensor(out=kgen[:], in0=kgen[:], scalar=unsorted[0:EP, :], in1=ksort[:],
                                                    op0=ALU.mult, op1=ALU.add))
                    v.link(dve.tensor_copy(ki[:], kgen[:]))
                    v.link(dve.tensor_scalar(hi[:], ki[:], 2, None, ALU.logical_shift_right))
                    v.link(dve.scalar_tensor_tensor(out=kgen[:], in0=hi[:], scalar=float(NROW), in1=dstf[:],
                                                    op0=ALU.mult, op1=ALU.add))
                    v.link(dve.tensor_copy(hi[:], kgen[:]))
                    v.mark(dve.tensor_scalar(ki[:], ki[:], S - 1, None, ALU.bitwise_and))
                    v.link(dve.tensor_scalar(hi[:], hi[:], 2, None, ALU.logical_shift_left))
                    v.mark(dve.tensor_tensor(slotpos[:], hi[:], ki[:], ALU.bitwise_or))

        fdt = sb("fdt", [P, NT + 1, W], F32)
        acc = sb("acc", [P, NT + 1, D], F32)
        den = sb("den", [P, NT + 1, HEADS], F32)
        cntge = sb("cntge", [P, NT + 1, S * (RELS + 1)], F32)
        hr_d = dram("hr_d", (NP, D), F32)
        y_d = dram("y_d", ((RT + 1) * P, D), F32)
        HB = [(0, 0, HALF), (1, HALF, D)]

        def halves(psum, rows=P):
            return psum[0:rows, :, 0:HALF]

        def split(ap):
            return ap.rearrange("p (a b) -> p a b", a=2)

        def pe_transpose(pe, dst, src, rows):
            for c in range(KC):
                last = pe.transpose(dst[:, c // 3, (c % 3) * P:(c % 3) * P + rows], src[0:rows, c * P:(c + 1) * P],
                                    ident[0:rows, 0:rows])
            return last

        def pe_product(pe, dst, rows_t, w, rows):
            for q, lo, up in HB:
                for c in range(KC):
                    last = pe.matmul(dst[0:rows, q, 0:HALF], rows_t[:, c * P:c * P + rows], w[:, c, lo:up],
                                     start=c == 0, stop=c == KC - 1)
            return last

        def row_stats(dve, v, row, stats, mv, rows):
            for q, lo, up in HB:
                v.mark(dve.bn_stats(stats[0:rows, q, :], row[0:rows, lo:up]))
            v.wait()
            v.tick()
            v.link(dve.bn_aggr(mv[0:rows, 0:2], stats[0:rows].rearrange("p a b -> p (a b)")))
            v.link(dve.tensor_scalar(mv[0:rows, 1:2], mv[0:rows, 1:2], EPS, None, ALU.add))

        def row_affine(dve, v, mv, rows):
            v.link(dve.reciprocal(mv[0:rows, 2:3], mv[0:rows, 2:3]))
            v.link(dve.scalar_tensor_tensor(out=mv[0:rows, 3:4], in0=mv[0:rows, 0:1], scalar=-1.0,
                                            in1=mv[0:rows, 2:3], op0=ALU.mult, op1=ALU.mult))

        def linear_part(dve, v, rows_w, attr, lost, heads, rows):
            hd = D // heads
            for h in range(heads):
                v.mark(dve.tensor_tensor_reduce(
                    out=lost[0:rows, h * hd:(h + 1) * hd], in0=rows_w[0:rows, h * hd:(h + 1) * hd],
                    in1=attr[0:rows, h * hd:(h + 1) * hd], scale=0.2, scalar=0.0, op0=ALU.mult, op1=ALU.add,
                    accum_out=rows_w[0:rows, D + h:D + h + 1]))
            v.wait()

        def w_view(w):
            return w.rearrange("(c p) n -> p c n", p=P)

        class Signal:

            def __init__(self, where, name, rate, lead=0, turn=1):
                self.sem, = sems(where, name)
                self.rate, self.lead, self.turn = rate, lead, turn

            def open(self, eng):
                eng.sem_inc(self.sem, self.rate * self.lead)

            def wait(self, eng, i, off, k=None):
                k = self.rate if k is None else k
                eng.wait_ge(self.sem, i * (self.turn * self.rate) + (self.rate * (off + self.lead) + k))

        with stage() as st:
            xt = [sb(f"xt{b}", [P, D], F32, st) for b in range(2)]
            ht = [sb(f"ht{b}", [P, D], F32, st) for b in range(2)]
            hT = [sb(f"hT{b}", [P, D], F32, st) for b in range(2)]
            of = [[sb(f"of{w}{b}", [P, W], F32, st) for b in range(2)] for w in range(2)]
            wt = [sb(f"wt{w}", [P, KC, D], F32, st) for w in range(2)]
            bias = [sb(f"bias{w}", [P, D], F32, st) for w in range(2)]
            attr = sb("attr", [P, D], F32, st)
            lost = sb("lost", [P, D], F32, st)
            stats = sb("stats", [P, 2, 6], F32, st)
            mv = [sb(f"mv{b}", [P, 4], F32, st) for b in range(2)]
            recc = [sb(f"recc{b}", [EP, 8, 2], I32, st) for b in range(2)]
            posc = [sb(f"posc{b}", [EP, 8], I32, st) for b in range(2)]
            pT = pb("pT", [P, 2, 512], F32, st)
            pO = [pb(f"pO{w}", [P, 2, 512], F32, st) for w in range(2)]
            w_in, dve3, dve3b, copied, placed0, placed1, posted = sems(st, "w_in", "dve3", "dve3b", "copied", "placed0", "placed1", "posted")
            x_in = sems(st, "x_in0", "x_in1")
            h_out = sems(st, "h_out0", "h_out1")
            f_out = [sems(st, f"f_out{w}0", f"f_out{w}1") for w in range(2)]
            var_ok = Signal(st, "var_ok", 1, 2, 2)
            root_ok = Signal(st, "root_ok", 1, 2, 2)
            affine_ok = Signal(st, "affine_ok", 1, 2, 2)
            h_ok = Signal(st, "h_ok", 1, 2, 2)
            t_ok = Signal(st, "t_ok", 1, 2, 2)
            hT_ok = Signal(st, "hT_ok", 1, 2, 2)
            prod_ok = Signal(st, "prod_ok", 2, 2, 2)
            evac_ok = Signal(st, "evac_ok", 2, 2, 2)
            tiles = [(4, 0, P), (4, 1, LAST)]

            def x_rows(a, i, b, rows):
                if isinstance(i, int):
                    n = 2 * i + b
                    return a[n * P:n * P + rows, :]
                return a[ds(i * (2 * P) + b * P, P), :]

            with nc.Block() as block:
                @block.sync
                def _(sp):
                    for w, (wn, bn) in enumerate((("L0_gnn_W1s", "L0_gnn_b1s"), ("L0_gnn_W1d", "L0_gnn_b1d"))):
                        sp.dma_start(wt[w][:], w_view(io[wn])).then_inc(w_in, 16)
                        sp.dma_start(bias[w][:], io[bn].partition_broadcast(P)).then_inc(w_in, 16)

                    sp.dma_start(attr[:], io["L0_gnn_attn1"].rearrange("h d -> (h d)").partition_broadcast(P))\
                      .then_inc(w_in, 16)

                    def load(i, b, rows):
                        h_ok.wait(sp, i, b - 2)
                        sp.dma_start(xt[b][0:rows], x_rows(io["x"], i, b, rows)).then_inc(x_in[b], 16)

                    def store(i, b, rows):
                        h_ok.wait(sp, i, b)
                        sp.dma_start(x_rows(h0_d, i, b, rows), ht[b][0:rows]).then_inc(h_out[b], 16)
                        for w, d in enumerate((fs_d, fd_d)):
                            evac_ok.wait(sp, i, b, w + 1)
                            sp.dma_start(x_rows(d, i, b, rows), of[w][b][0:rows]).then_inc(f_out[w][b], 16)

                    load(0, 0, P)
                    with sp.Fori(0, 4) as i:
                        load(i, 1, P)
                        store(i, 0, P)
                        load(i + 1, 0, P)
                        store(i, 1, P)
                    load(4, 1, LAST)
                    store(4, 0, P)
                    store(4, 1, LAST)
                    for s in h_out + f_out[0] + f_out[1]:
                        sp.wait_ge(s, 16 * 5)

                @block.gpsimd
                def _(pool):
                    slots = slots_d
                    with pool.Fori(0, EC // 16) as i:
                        for b, placed in enumerate((placed0, placed1)):
                            pool.wait_ge(placed, i * 128)
                            pool.tensor_copy(posc[b][:], slotpos[:, ds(i * 16 + b * 8, 8)]).then_inc(copied, 1)
                            pool.tensor_copy(recc[b][:], recs[:, ds(i * 16 + b * 8, 8), :]).then_inc(copied, 1)
                            pool.wait_ge(copied, i * 4 + (b * 2 + 2))
                            pool.sem_inc(posted, 1)
                            for j in range(8):
                                pool.indirect_dma_start(slots, bass.IndirectOffsetOnAxis(ap=posc[b][:, j:j + 1], axis=0),
                                                        recc[b][:, j, :], None).then_inc(placed, 16)
                    for placed in (placed0, placed1):
                        pool.wait_ge(placed, EC // 16 * 128)

                @block.scalar
                def _(act):
                    for s in (root_ok, h_ok, hT_ok):
                        s.open(act)

                    def norm(i, b, rows):
                        var_ok.wait(act, i, b)
                        act.activation(mv[b][0:rows, 2:3], mv[b][0:rows, 1:2], ACT.Sqrt).then_inc(root_ok.sem, 1)
                        affine_ok.wait(act, i, b)
                        t_ok.wait(act, i, b - 2)
                        act.wait_ge(h_out[b], 16 * i)
                        act.activation(ht[b][0:rows], xt[b][0:rows], ACT.Relu, bias=mv[b][0:rows, 3:4],
                                       scale=mv[b][0:rows, 2:3]).then_inc(h_ok.sem, 1)

                    def copy(i, b, rows):
                        t_ok.wait(act, i, b)
                        prod_ok.wait(act, i, b - 2)
                        v = hT[b][:].rearrange("p (a c n) -> p a c n", a=2, n=P)[:, :, :, 0:rows]
                        act.activation(v, halves(pT).rearrange("p a (c n) -> p a c n", n=P)[:, :, :, 0:rows],
                                       ACT.Copy).then_inc(hT_ok.sem, 1)

                    norm(0, 0, P)
                    copy(0, 0, P)
                    with act.Fori(0, 4) as i:
                        norm(i, 1, P)
                        copy(i, 1, P)
                        norm(i + 1, 0, P)
                        copy(i + 1, 0, P)
                    norm(4, 1, LAST)
                    copy(4, 1, LAST)

                @block.tensor
                def _(pe):
                    for s in (t_ok, prod_ok):
                        s.open(pe)

                    def turn(i, b, rows):
                        h_ok.wait(pe, i, b)
                        hT_ok.wait(pe, i, b - 1)
                        pe_transpose(pe, pT, ht[b], rows).then_inc(t_ok.sem, 1)

                    def product(i, b, rows):
                        hT_ok.wait(pe, i, b)
                        for w in range(2):
                            evac_ok.wait(pe, i, b - 1, w + 1)
                            pe_product(pe, pO[w], hT[b], wt[w], rows).then_inc(prod_ok.sem, 1)

                    turn(0, 0, P)
                    pe.wait_ge(w_in, 80)
                    with pe.Fori(0, 4) as i:
                        turn(i, 1, P)
                        product(i, 0, P)
                        turn(i + 1, 0, P)
                        product(i, 1, P)
                    turn(4, 1, LAST)
                    product(4, 0, P)
                    product(4, 1, LAST)

                @block.vector
                def _(dve):
                    for s in (var_ok, affine_ok, evac_ok):
                        s.open(dve)
                    PER = 7
                    PER_EVAC = 1 + HEADS

                    def norm(i, b, rows):
                        v = Steps(dve, dve3, i * (2 * PER) + b * PER)
                        v.wait()
                        dve.wait_ge(x_in[b], 16 * i + 16)
                        h_ok.wait(dve, i, b - 2)
                        row_stats(dve, v, xt[b], stats, mv[b], rows)
                        dve.sem_inc(var_ok.sem, 1)
                        root_ok.wait(dve, i, b)
                        row_affine(dve, v, mv[b], rows)
                        dve.sem_inc(affine_ok.sem, 1)
                        assert v.n == PER

                    def evacuate(i, b, rows):
                        v = Steps(dve, dve3b, i * (4 * PER_EVAC) + b * (2 * PER_EVAC))
                        for w in range(2):
                            prod_ok.wait(dve, i, b, w + 1)
                            dve.wait_ge(f_out[w][b], 16 * i)
                            v.wait()
                            v.link(dve.tensor_tensor(split(of[w][b][0:rows, 0:D]), halves(pO[w], rows),
                                                     split(bias[w][0:rows]), ALU.add))
                            linear_part(dve, v, of[w][b], attr, lost, HEADS, rows)
                            dve.sem_inc(evac_ok.sem, 1)

                    norm(0, 0, P)
                    dve.wait_ge(w_in, 80)
                    with dve.Fori(0, 4) as i:
                        norm(i, 1, P)
                        evacuate(i, 0, P)
                        norm(i + 1, 0, P)
                        evacuate(i, 1, P)
                    norm(4, 1, LAST)
                    evacuate(4, 0, P)
                    evacuate(4, 1, LAST)

        def sum_tiles(eng, tile_from, count, i):
            return [eng.value_load(tile_of_group[0:1, ds(i * U + (tile_from + TBACK + k), 1)], min_val=0, max_val=NT)
                    for k in range(count)]

        def slot_buffers(st, width):
            b = {}
            b["rec"] = [sb(f"rec{u}", [P, S * 2], I32, st) for u in range(U)]
            b["row"] = [[sb(f"row{u}{j}", [P, width], F32, st) for j in range(S)] for u in range(U)]
            b["val"] = [sb(f"val{u}", [P, S], F32, st) for u in range(U)]
            b["neg"] = [sb(f"neg{u}", [P, S], F32, st) for u in range(U)]
            b["index"] = [sb(f"index{u}", [P, 1], I32, st) for u in range(U)]
            b["next"] = sb("next", [P, NT + 1], I32, st)
            b["left"] = sb("left", [P, NT + 1], F32, st)
            b["step"] = sb("step", [P, 1], I32, st)
            b["slot"] = sb("slot", [P, S], F32, st)
            b["fours"] = sb("fours", [P, 1], F32, st)
            b["over"] = sb("over", [P, S], F32, st)
            b["rec_in"] = sems(st, *[f"rec_in{u}" for u in range(U)])
            b["row_in"] = sems(st, *[f"row_in{u}" for u in range(U)])
            b["pool_step"], = sems(st, "pool_step")
            b["pool_pre"], = sems(st, "pool_pre")
            b["valid"] = Signal(st, "valid", 1, U, U)
            return b

        def gather_edges(pool, b, table, field, used, count_relations=False, keep_places=False):
            b["valid"].open(pool)
            pre = Steps(pool, b["pool_pre"])
            pre.mark(pool.tensor_copy(b["next"][:], perm[:]))
            pre.mark(pool.tensor_copy(b["left"][:], degr[:]))
            pre.mark(pool.memset(b["step"][:], NROW))
            pre.mark(pool.iota(b["slot"][:], [[1, S]], base=0, channel_multiplier=0, allow_small_or_imprecise_dtypes=True))
            pre.mark(pool.memset(b["fours"][:], float(S)))
            if count_relations:
                pre.mark(pool.tensor_scalar(b["lessone"][:], relbase[:], -1.0, None, ALU.add))
                pre.mark(pool.memset(cntge[:], 0.0))
            pre.wait()
            PER = 10 if count_relations else 7 if keep_places else 6
            table_rows = slots_d.rearrange("(r s) c -> r (s c)", s=S)

            def record(v, u, t):
                v.mark(pool.tensor_copy(b["index"][u][:], b["next"][:, ds(t, 1)]))
                v.wait()
                v.mark(pool.tensor_tensor(b["next"][:, ds(t, 1)], b["next"][:, ds(t, 1)], b["step"][:], ALU.add))
                pool.indirect_dma_start(b["rec"][u][:], None, table_rows,
                                        bass.IndirectOffsetOnAxis(ap=b["index"][u][:], axis=0)).then_inc(b["rec_in"][u], 16)

            def rows(u):
                for j in range(S):
                    pool.indirect_dma_start(b["row"][u][j][:], None, table, bass.IndirectOffsetOnAxis(
                        ap=b["rec"][u][:, 2 * j + field:2 * j + field + 1], axis=0)).then_inc(b["row_in"][u], 16)

            ahead = sum_tiles(pool, 0, U - 1, 0)
            for u in range(U - 1):
                record(pre, u, ahead[u])
                pre.wait()
            for u in range(ROWS_AHEAD):
                pool.wait_ge(b["rec_in"][u], 16)
                rows(u)
            turns = pool.value_load(ctl[0:1, C_TURNS:C_TURNS + 1], min_val=1, max_val=MAX_TURNS)
            with pool.Fori(0, turns) as i:
                t = sum_tiles(pool, 0, 2 * U - 1, i)
                v = Steps(pool, b["pool_step"], i * (PER * U), b["posted"])
                for u in range(U):
                    v.wait()
                    used.wait(pool, i, u - U)
                    pool.sem_inc(b["posted"], 1)
                    left = b["left"][:, ds(t[u], 1)]
                    v.link(pool.tensor_tensor(b["over"][:], left.to_broadcast([P, S]), b["slot"][:], ALU.subtract))
                    v.mark(pool.tensor_tensor(left, left, b["fours"][:], ALU.subtract))
                    v.link(pool.tensor_scalar(b["val"][u][:], b["over"][:], 0.0, 1.0, ALU.max, ALU.min))
                    v.mark(pool.tensor_scalar(b["neg"][u][:], b["val"][u][:], -1.0, BIG, ALU.add, ALU.mult))
                    if keep_places:
                        pool.wait_ge(b["rec_in"][u], i * 16 + 16)
                        pool.sem_inc(b["posted"], 1)
                        v.mark(pool.tensor_copy(b["places"][u][:], b["rec"][u][:].rearrange("p (s c) -> p s c", c=2)[:, :, 1]))
                    if count_relations:
                        pool.wait_ge(b["rec_in"][u], i * 16 + 16)
                        pool.sem_inc(b["posted"], 1)
                        place_of = b["rec"][u][:].rearrange("p (s c) -> p s c", c=2)[:, :, 1]
                        shape = [P, S, RELS + 1]
                        v.link(pool.tensor_copy(b["place"][:], place_of))
                        v.link(pool.tensor_tensor(b["ge"][:], over(b["place"][:], 2, shape), over(b["lessone"][:], 1, shape),
                                                  ALU.subtract))
                        v.link(pool.tensor_scalar(b["ge"][:], b["ge"][:], 0.0, 1.0, ALU.max, ALU.min))
                        into = cntge[:, ds(t[u], 1), :].rearrange("p o f -> p (o f)")
                        v.mark(pool.tensor_tensor(into, into, b["ge"][:].rearrange("p s r -> p (s r)"), ALU.add))
                    v.wait()
                    pool.sem_inc(b["valid"].sem, 1)
                    w = (u + U - 1) % U
                    rows_wait(pool, b, i, u - 1)
                    pool.sem_inc(b["posted"], 1)
                    record(v, w, t[u + U - 1])
                    w = u + ROWS_AHEAD
                    pool.wait_ge(b["rec_in"][w % U], i * 16 + 16 * (w // U + 1))
                    used.wait(pool, i, w - U)
                    pool.sem_inc(b["posted"], 1)
                    rows(w % U)
                    assert v.n == PER * (u + 1), (v.n, PER)
            for u in range(U):
                pool.wait_ge(b["rec_in"][u], turns * 16 + (16 if u < U - 1 else 0))
                pool.wait_ge(b["row_in"][u], turns * (16 * S) + (16 * S if u < ROWS_AHEAD else 0))
            pool.sem_inc(b["posted"], 1)

        def rows_wait(eng, b, i, off):
            eng.wait_ge(b["row_in"][off % U], i * (16 * S) + 16 * S * (off // U + 1))

        def attention(name, heads, attn, fd_table):
            HD = D // heads
            H1 = [P, S + 1, heads]
            with stage() as st:
                b = slot_buffers(st, W)
                b["ge"] = sb("ge", [P, S, RELS + 1], F32, st)
                b["place"] = sb("place_f", [P, S], F32, st)
                b["lessone"] = sb("lessone", [P, RELS + 1], F32, st)
                b["posted"], = sems(st, "rows_posted")
                sj = sb("sj", [P, S, W], F32, st)
                lin = [sb(f"lin{u}", [P, S, heads], F32, st) for u in range(U)]
                scaled = sb("scaled", [P, D], F32, st)
                attr = sb("attr", [P, D], F32, st)
                top = sb("top", [P, NT + 1, heads], F32, st)
                ex = [sb(f"ex{u}", [P, S + 1, heads], F32, st) for u in range(U)]
                pe_ = [sb(f"pe{u}", [P, S + 1, heads], F32, st) for u in range(U)]
                lg = sb("lg", [P, S, heads], F32, st)
                mj = sb("mj", [P, heads], F32, st)
                mnew = sb("mnew", [P, heads], F32, st)
                dsum = sb("dsum", [P, heads], F32, st)
                dots = [sb(f"dots{u}", [P, S, heads], F32, st) for u in range(U)]
                pA = pb("pA", [P, 2, 512], F32, st)
                att_in, att_ok, dve_step, init_ok, fd_in = sems(st, "att_in", "att_ok", "dve_step", "init_ok", "fd_in")
                sum_ok = Signal(st, "sum_ok", S, U, U)
                leaky = Signal(st, "leaky", S, U, U)
                logits = Signal(st, "logits", S, U, U)
                ex_in = Signal(st, "ex_in", 1, U, U)
                ex_ok = Signal(st, "ex_ok", 1, U, U)
                weighted = Signal(st, "weighted", S, U, U)
                summed = Signal(st, "summed", S, U, U)
                scaled_ok = Signal(st, "scaled_ok", 1, U, U)
                added = Signal(st, "added", 1, U, U)
                lin_ok = Signal(st, "lin_ok", 1, U, U)
                top_ok = Signal(st, "top_ok", 1, U, U)
                den_ok = Signal(st, "den_ok", 1, U, U)
                row = b["row"]
                with nc.Block() as block:
                    @block.sync
                    def _(sp):
                        sp.dma_start(attr[:], attn.rearrange("h d -> (h d)").partition_broadcast(P)).then_inc(att_in, 16)
                        sp.wait_ge(att_in, 16)

                    @block.gpsimd
                    def _(pool):
                        if fd_table is not None:
                            for t in range(NT):
                                pool.indirect_dma_start(fdt[:, t, :], None, fd_table, bass.IndirectOffsetOnAxis(
                                    ap=permc[:, t:t + 1], axis=0)).then_inc(fd_in, 16)
                            pool.wait_ge(fd_in, 16 * NT)
                        pool.sem_inc(init_ok, 1)
                        gather_edges(pool, b, fs_d[0:N], 0, summed, fd_table is not None)

                    @block.scalar
                    def _(act):
                        for s in (ex_ok, scaled_ok) + ((logits,) if heads > 1 else ()):
                            s.open(act)

                        def sums(i, off):
                            for j in range(S if heads > 1 else 0):
                                leaky.wait(act, i, off, j + 1)
                                if j == 0:
                                    ex_ok.wait(act, i, off - U)
                                for h in range(heads):
                                    of_head = sj[:, j, h * HD:(h + 1) * HD]
                                    last = act.activation(of_head, of_head, ACT.Copy,
                                                          accum_out=dots[off % U][:, j, h:h + 1])
                                last.then_inc(logits.sem, 1)

                        sums(0, 0)
                        turns = act.value_load(ctl[0:1, C_TURNS:C_TURNS + 1], min_val=1, max_val=MAX_TURNS)
                        with act.Fori(0, turns) as i:
                            t = sum_tiles(act, 0, U, i)
                            for u in range(U):
                                ex_in.wait(act, i, u)
                                act.activation(pe_[u][:], ex[u][:], ACT.Exp).then_inc(ex_ok.sem, 1)
                                sums(i, u + 1)
                                ex_ok.wait(act, i, u)
                                added.wait(act, i, u - 1)
                                old = acc[:, ds(t[u], 1), :].rearrange("p o f -> p (o f)")
                                for h in range(heads):
                                    last = act.activation(scaled[:, h * HD:(h + 1) * HD], old[:, h * HD:(h + 1) * HD],
                                                          ACT.Copy, scale=pe_[u][:, 0, h:h + 1])
                                last.then_inc(scaled_ok.sem, 1)

                    @block.tensor
                    def _(pe):
                        summed.open(pe)
                        turns = pe.value_load(ctl[0:1, C_TURNS:C_TURNS + 1], min_val=1, max_val=MAX_TURNS)
                        with pe.Fori(0, turns) as i:
                            for u in range(U):
                                added.wait(pe, i, u - 1)
                                for j in range(S):
                                    weighted.wait(pe, i, u, j + 1)
                                    for q, lo, up in HB:
                                        last = pe.matmul(pA[:, q, 0:HALF], ident[:], row[u][j][:, lo:up],
                                                         start=j == 0, stop=j == S - 1)
                                    last.then_inc(summed.sem, 1)

                    @block.vector
                    def _(dve):
                        for s in (sum_ok, leaky, ex_in, weighted, top_ok, den_ok, lin_ok) + ((logits,) if heads == 1 else ()):
                            s.open(dve)
                        dve.sem_inc(added.sem, U - 1)
                        PER = 9
                        v = Steps(dve, dve_step)
                        v.mark(dve.memset(acc[:], 0.0))
                        v.mark(dve.memset(den[:], 0.0))
                        v.mark(dve.memset(fdt[:, NT, :], 0.0))
                        v.mark(dve.memset(top[:], -BIG))
                        v.mark(dve.memset(scaled[:], 0.0))
                        dve.wait_ge(att_in, 16)
                        v.mark(dve.tensor_scalar(attr[:], attr[:], 0.8, None, ALU.mult))
                        v.link(dve.memset(pA[:], 0.0))
                        FIRST = v.n
                        dve.wait_ge(init_ok, 1)

                        def add(i, off, tile):
                            rows_wait(dve, b, i, off)
                            lin_ok.wait(dve, i, off - 1)
                            fd = fdt[:, tile if isinstance(tile, int) else ds(tile, 1), :]
                            if not isinstance(tile, int):
                                fd = fd.rearrange("p o f -> p (o f)")

                            def product(j):
                                sum_ok.wait(dve, i, off, j + 1)
                                if heads > 1:
                                    dve.scalar_tensor_tensor(out=sj[:, j, 0:D], in0=sj[:, j, 0:D], scalar=0.0, in1=attr[:],
                                                             op0=ALU.max, op1=ALU.mult).then_inc(leaky.sem, 1)
                                else:
                                    dve.scalar_tensor_tensor(out=sj[:, j, 0:D], in0=sj[:, j, 0:D], scalar=0.0, in1=attr[:],
                                                             op0=ALU.max, op1=ALU.mult,
                                                             accum_out=dots[off % U][:, j, 0:1]).then_inc(logits.sem, 1)

                            for j in range(S):
                                logits.wait(dve, i, off - 1, j + 1)
                                dve.tensor_tensor(sj[:, j, 0:D + heads], row[off % U][j][:, 0:D + heads],
                                                  fd[:, 0:D + heads], ALU.add).then_inc(sum_ok.sem, 1)
                                if j > 0:
                                    product(j - 1)
                            product(S - 1)
                            sum_ok.wait(dve, i, off)
                            dve.tensor_copy(lin[off % U][:], sj[:, :, D:D + heads]).then_inc(lin_ok.sem, 1)

                        def finish(i, off, tile):
                            summed.wait(dve, i, off)
                            scaled_ok.wait(dve, i, off)
                            dve.tensor_tensor(split(acc[:, ds(tile, 1), :].rearrange("p o f -> p (o f)")), halves(pA),
                                              split(scaled[:]), ALU.add).then_inc(added.sem, 1)

                        def arguments(v, i, u, tile):
                            sh = [P, S, heads]
                            logits.wait(dve, i, u)
                            lin_ok.wait(dve, i, u)
                            b["valid"].wait(dve, i, u)
                            v.link(dve.tensor_tensor(lg[:], dots[u][:],
                                                     over(b["neg"][u][:], 2, sh), ALU.add))
                            v.link(dve.tensor_tensor(lg[:], lg[:], lin[u][:], ALU.add))
                            v.link(dve.tensor_reduce(mj[:], lg[:].rearrange("p s h -> p h s"), X, ALU.max))
                            old = top[:, ds(tile, 1), :].rearrange("p o h -> p (o h)")
                            v.link(dve.tensor_tensor(mnew[:], old, mj[:], ALU.max))
                            v.mark(dve.tensor_tensor(ex[u][:, 0, :], old, mnew[:], ALU.subtract))
                            v.mark(dve.tensor_tensor(ex[u][:, 1:S + 1, :], lg[:], over(mnew[:], 1, sh), ALU.subtract))
                            v.wait()
                            dve.sem_inc(ex_in.sem, 1)
                            dve.tensor_copy(old, mnew[:]).then_inc(top_ok.sem, 1)

                        def weigh(v, i, u, tile):
                            sh = [P, S, heads]
                            ex_ok.wait(dve, i, u)
                            v.link(dve.tensor_tensor(pe_[u][:, 1:S + 1, :], pe_[u][:, 1:S + 1, :],
                                                     over(b["val"][u][:], 2, sh), ALU.mult))
                            for j in range(S):
                                if heads == 1:
                                    ins = dve.tensor_scalar(row[u][j][:, 0:D], row[u][j][:, 0:D], pe_[u][:, 1 + j, :], None,
                                                            ALU.mult)
                                else:
                                    of_heads = row[u][j][:, 0:D].rearrange("p (h d) -> p h d", h=heads)
                                    ins = dve.tensor_tensor(of_heads, of_heads,
                                                            over(pe_[u][:, 1 + j, :], 2, [P, heads, HD]), ALU.mult)
                                ins\
                                   .then_inc(weighted.sem, 1)
                            v.mark(dve.tensor_reduce(dsum[:], pe_[u][:, 1:S + 1, :].rearrange("p s h -> p h s"), X, ALU.add))
                            d = den[:, ds(tile, 1), 0:heads].rearrange("p o h -> p (o h)")
                            v.mark(dve.tensor_tensor(d, d, pe_[u][:, 0, :], ALU.mult))
                            v.wait()
                            dve.tensor_tensor(d, d, dsum[:], ALU.add).then_inc(den_ok.sem, 1)
                            assert v.n % PER == 0, v.n

                        add(0, 0, 0)
                        turns = dve.value_load(ctl[0:1, C_TURNS:C_TURNS + 1], min_val=1, max_val=MAX_TURNS)
                        with dve.Fori(0, turns) as i:
                            t = sum_tiles(dve, -1, U + 2, i)
                            v = Steps(dve, dve_step, i * (PER * U) + FIRST)
                            for u in range(U):
                                top_ok.wait(dve, i, u - 1)
                                arguments(v, i, u, t[u + 1])
                                add(i, u + 1, t[u + 2])
                                finish(i, u - 1, t[u])
                                den_ok.wait(dve, i, u - 1)
                                weigh(v, i, u, t[u + 1])
                        last, = sum_tiles(dve, -1, 1, turns)
                        finish(turns, -1, last)

        attention("first", HEADS, io["L0_gnn_attn1"], fd_d[0:N])

        rcnt = sb("rcnt", [P, NT + 1, RELS], F32)

        def settle(first):
            heads = HEADS if first else 1
            HD = D // heads
            table = h0_d[0:N] if first else io["x"]
            ln = ("L0_gnn_ln1_w", "L0_gnn_ln1_b") if first else ("L0_gnn_lno_w", "L0_gnn_lno_b")
            prods = ([("L0_gnn_Wos", "L0_gnn_bos"), ("L0_gnn_Wod", "L0_gnn_bod")] if first
                     else [("L1_gnn_W_root", "L1_gnn_b_rgcn")])
            NW = len(prods)
            with stage() as st:
                wt = [sb(f"wt{w}", [P, KC, D], F32, st) for w in range(NW)]
                bias = [sb(f"bias{w}", [P, D], F32, st) for w in range(NW)]
                lnw = sb("lnw", [P, D], F32, st)
                lnb = sb("lnb", [P, D], F32, st)
                attr = sb("attr", [P, D], F32, st)
                lost = sb("lost", [P, D], F32, st)
                rden = sb("rden", [P, NT, heads], F32, st)
                csum = sb("csum", [P, NT + 1, RELS + 1], F32, st)
                o = sb("o", [P, D], F32, st)
                low = sb("low", [P, D], F32, st)
                y = sb("y", [P, D], F32, st)
                hg = [sb(f"hg{b}", [P, D], F32, st) for b in range(2)]
                ht = [sb(f"ht{b}", [P, D], F32, st) for b in range(2)]
                hT = [sb(f"hT{b}", [P, D], F32, st) for b in range(2)]
                of = [sb(f"of{b}", [P, W], F32, st) for b in range(2)]
                stats = sb("stats", [P, 2, 6], F32, st)
                mv = sb("mv", [P, 4], F32, st)
                gindex = [sb(f"gindex{b}", [P, 1], I32, st) for b in range(2)]
                sindex = [sb(f"sindex{b}", [P, 1], I32, st) for b in range(2)]
                recc = [sb(f"recc{b}", [EP, 8, 2], I32, st) for b in range(2)]
                pT = pb("pT", [P, 2, 512], F32, st)
                pO = [pb(f"pO{w}", [P, 2, 512], F32, st) for w in range(NW)]
                w_in, dve4, dve4b, copied, posted, pre_ok = sems(st, "w_in", "dve4", "dve4b", "copied", "posted", "pre_ok")
                hg_in = sems(st, "hg_in0", "hg_in1")
                placed = sems(st, "placed0", "placed1")
                f_out = sems(st, "f_out0", "f_out1")
                low_ok = Signal(st, "low_ok", 1, 2, 2)
                exp_ok = Signal(st, "exp_ok", 1, 2, 2)
                y_ok = Signal(st, "y_ok", 1, 2, 2)
                NV = 1 if first else 2
                var_ok = Signal(st, "var_ok", NV, 2, 2)
                root_ok = Signal(st, "root_ok", NV, 2, 2)
                affine_ok = Signal(st, "affine_ok", 1, 2, 2)
                h_ok = Signal(st, "h_ok", 1, 2, 2)
                t_ok = Signal(st, "t_ok", 1, 2, 2)
                hT_ok = Signal(st, "hT_ok", 1, 2, 2)
                prod_ok = Signal(st, "prod_ok", NW, 2, 2)
                evac_ok = Signal(st, "evac_ok", NW, 2, 2)
                kept_ok = Signal(st, "kept_ok", 1, 2, 2)

                def of_tile(ap, i, b):
                    if isinstance(i, int):
                        return ap[:, 2 * i + b]
                    x = ap[:, ds(i * 2 + b, 1)]
                    return x.rearrange("p o f -> p (o f)") if len(x.shape) == 3 else x

                def twice(step, eng):
                    step(eng, 0, 0, True)
                    with eng.Fori(0, 4) as i:
                        step(eng, i, 1, True)
                        step(eng, i, 0, False)
                        step(eng, i + 1, 0, True)
                        step(eng, i, 1, False)
                    step(eng, 4, 1, True)
                    step(eng, 4, 0, False)
                    step(eng, 4, 1, False)

                with nc.Block() as block:
                    @block.sync
                    def _(sp):
                        for w, (wn, bn) in enumerate(prods):
                            sp.dma_start(wt[w][:], w_view(io[wn])).then_inc(w_in, 16)
                            sp.dma_start(bias[w][:], io[bn].partition_broadcast(P)).then_inc(w_in, 16)
                        sp.dma_start(lnw[:], io[ln[0]].partition_broadcast(P)).then_inc(w_in, 16)
                        sp.dma_start(lnb[:], io[ln[1]].partition_broadcast(P)).then_inc(w_in, 16)
                        sp.dma_start(attr[:], io["L0_gnn_attno"].rearrange("h d -> (h d)").partition_broadcast(P))\
                          .then_inc(w_in, 16)
                        sp.wait_ge(w_in, 16 * (2 * NW + 3))

                    @block.gpsimd
                    def _(pool):
                        def gather(i, b, c):
                            y_ok.wait(pool, i, b - 2)
                            pool.sem_inc(posted, 1)
                            pool.tensor_copy(gindex[b][:], of_col(permc, i, b)).then_inc(copied, 1)
                            return c

                        def of_col(ap, i, b):
                            return ap[:, ds(i * 2 + b, 1)] if not isinstance(i, int) else ap[:, 2 * i + b:2 * i + b + 1]

                        def fetch(b):
                            pool.indirect_dma_start(hg[b][:], None, table, bass.IndirectOffsetOnAxis(
                                ap=gindex[b][:], axis=0)).then_inc(hg_in[b], 16)

                        pool.tensor_copy(gindex[0][:], permc[:, 0:1]).then_inc(copied, 1)
                        pool.wait_ge(copied, 1)
                        fetch(0)
                        COPIES = 8 if first else 4
                        with pool.Fori(0, NT // 2) as i:
                            for b in range(2):
                                n = COPIES // 2 * b
                                y_ok.wait(pool, i, b - 1)
                                pool.wait_ge(hg_in[1 - b], i * 16 + 16 * b)
                                pool.sem_inc(posted, 1)
                                pool.tensor_copy(gindex[1 - b][:], permc[:, ds(i * 2 + (b + 1), 1)]).then_inc(copied, 1)
                                pool.wait_ge(f_out[b], i * 16)
                                pool.sem_inc(posted, 1)
                                pool.tensor_copy(sindex[b][:], perm[:, ds(i * 2 + b, 1)]).then_inc(copied, 1)
                                pool.wait_ge(copied, i * COPIES + (n + 3))
                                pool.sem_inc(posted, 1)
                                fetch(1 - b)
                                if first:
                                    for q in range(2):
                                        pool.wait_ge(placed[q], i * 256 + b * 128)
                                        pool.sem_inc(posted, 1)
                                        pool.tensor_copy(recc[q][:], recs[:, ds(i * 32 + (b * 16 + q * 8), 8), :])\
                                            .then_inc(copied, 1)
                                        pool.wait_ge(copied, i * COPIES + (n + 4 + q))
                                        pool.sem_inc(posted, 1)
                                        for j in range(8):
                                            pool.indirect_dma_start(byrel_d, bass.IndirectOffsetOnAxis(
                                                ap=recc[q][:, j, 1:2], axis=0), recc[q][:, j, 0:1], None)\
                                                .then_inc(placed[q], 16)
                                if first:
                                    evac_ok.wait(pool, i, b, 1)
                                    pool.sem_inc(posted, 1)
                                    pool.indirect_dma_start(fs_d, bass.IndirectOffsetOnAxis(ap=sindex[b][:], axis=0),
                                                            of[b][:], None).then_inc(f_out[b], 16)
                                else:
                                    h_ok.wait(pool, i, b)
                                    pool.sem_inc(posted, 1)
                                    pool.indirect_dma_start(hr_d, bass.IndirectOffsetOnAxis(ap=sindex[b][:], axis=0),
                                                            ht[b][:], None).then_inc(f_out[b], 16)
                        for b in range(2):
                            pool.wait_ge(f_out[b], 16 * NT // 2)
                            pool.wait_ge(hg_in[b], 16 * NT // 2 + 16 * (1 - b))
                            if first:
                                pool.wait_ge(placed[b], EC // 2 * 16)

                    @block.scalar
                    def _(act):
                        for s in (exp_ok, root_ok, h_ok, hT_ok, kept_ok):
                            if s is not h_ok or not first:
                                s.open(act)

                        def step(act, i, b, ahead):
                            if ahead:
                                low_ok.wait(act, i, b)
                                act.activation(low[:], low[:], ACT.Exp).then_inc(exp_ok.sem, 1)
                                for k in range(NV):
                                    var_ok.wait(act, i, b, k + 1)
                                    act.activation(mv[:, 2:3], mv[:, 1:2], ACT.Sqrt).then_inc(root_ok.sem, 1)
                                if not first:
                                    affine_ok.wait(act, i, b)
                                    act.activation(of_tile(fdt, i, b)[:, 0:D], y[:], ACT.Copy).then_inc(kept_ok.sem, 1)
                                    t_ok.wait(act, i, b - 2)
                                    act.wait_ge(f_out[b], 16 * i)
                                    act.activation(ht[b][:], y[:], ACT.Relu, bias=mv[:, 3:4], scale=mv[:, 2:3])\
                                       .then_inc(h_ok.sem, 1)
                                t_ok.wait(act, i, b)
                                prod_ok.wait(act, i, b - 2)
                                act.activation(split(hT[b][:]), halves(pT), ACT.Copy).then_inc(hT_ok.sem, 1)

                        twice(step, act)

                    @block.tensor
                    def _(pe):
                        for s in (t_ok, prod_ok):
                            s.open(pe)

                        def step(pe, i, b, ahead):
                            if ahead:
                                h_ok.wait(pe, i, b)
                                hT_ok.wait(pe, i, b - 1)
                                pe_transpose(pe, pT, ht[b], P).then_inc(t_ok.sem, 1)
                            else:
                                hT_ok.wait(pe, i, b)
                                for w in range(NW):
                                    evac_ok.wait(pe, i, b - 1, w + 1)
                                    pe_product(pe, pO[w], hT[b], wt[w], P).then_inc(prod_ok.sem, 1)

                        pe.wait_ge(w_in, 16 * (2 * NW + 3))
                        twice(step, pe)

                    @block.vector
                    def _(dve):
                        for s in (low_ok, y_ok, var_ok, affine_ok, evac_ok) + ((h_ok,) if first else ()):
                            s.open(dve)
                        dve.wait_ge(w_in, 16 * (2 * NW + 3))
                        pre = Steps(dve, pre_ok)
                        pre.link(dve.tensor_scalar(rden[:], den[:, 0:NT, 0:heads], 1e-30, None, ALU.max))
                        pre.link(dve.reciprocal(rden[:], rden[:]))
                        if first:
                            for b in range(2):
                                pre.link(dve.memset(of[b][:, D:W], 0.0))
                        else:
                            pre.link(dve.tensor_reduce(csum[:], cntge[:].rearrange("p t (s r) -> p t r s", s=S), X, ALU.add))
                            pre.link(dve.tensor_copy(csum[:, :, 0], degr[:]))
                            pre.link(dve.tensor_tensor(rcnt[:], csum[:, :, 0:RELS], csum[:, :, 1:RELS + 1], ALU.subtract))
                            pre.link(dve.tensor_scalar(rcnt[:], rcnt[:], 1.0, None, ALU.max))
                            pre.link(dve.reciprocal(rcnt[:], rcnt[:]))
                        PER = 14 if first else 22

                        def step(dve, i, b, ahead):
                            if ahead:
                                v = Steps(dve, dve4, i * (2 * PER) + b * PER)
                                v.wait()
                                h_ok.wait(dve, i, b - 1)
                                rd = (rden[:, 2 * i + b, :] if isinstance(i, int)
                                      else rden[:, ds(i * 2 + b, 1), :].rearrange("p o h -> p (o h)"))
                                v.link(dve.tensor_tensor(
                                    o[:].rearrange("p (h d) -> p h d", h=heads),
                                    of_tile(acc, i, b)[:, 0:D].rearrange("p (h d) -> p h d", h=heads),
                                    over(rd, 2, [P, heads, HD]), ALU.mult))
                                v.link(dve.tensor_scalar(low[:], o[:], 0.0, None, ALU.min))
                                dve.sem_inc(low_ok.sem, 1)
                                exp_ok.wait(dve, i, b)
                                v.link(dve.scalar_tensor_tensor(out=o[:], in0=o[:], scalar=0.0, in1=low[:],
                                                                op0=ALU.max, op1=ALU.add))
                                dve.wait_ge(hg_in[b], i * 16 + 16)
                                if first:
                                    v.link(dve.scalar_tensor_tensor(out=y[:], in0=o[:], scalar=-1.0, in1=hg[b][:],
                                                                    op0=ALU.add, op1=ALU.add))
                                    dve.sem_inc(y_ok.sem, 1)
                                else:
                                    kept_ok.wait(dve, i, b - 1)
                                    v.link(dve.tensor_scalar(y[:], o[:], -1.0, None, ALU.add))
                                row_stats(dve, v, y, stats, mv, P)
                                dve.sem_inc(var_ok.sem, 1)
                                root_ok.wait(dve, i, b, 1)
                                row_affine(dve, v, mv, P)
                                v.link(dve.tensor_scalar(y[:], y[:], mv[:, 2:3], mv[:, 3:4], ALU.mult, ALU.add))
                                if first:
                                    v.link(dve.tensor_tensor(y[:], y[:], lnw[:], ALU.mult))
                                    t_ok.wait(dve, i, b - 2)
                                    v.mark(dve.tensor_tensor(ht[b][:], y[:], lnb[:], ALU.add))
                                    v.wait()
                                    dve.sem_inc(h_ok.sem, 1)
                                else:
                                    v.link(dve.tensor_tensor(y[:], y[:], lnw[:], ALU.mult))
                                    v.link(dve.tensor_tensor(y[:], y[:], lnb[:], ALU.add))
                                    v.link(dve.tensor_tensor(y[:], y[:], hg[b][:], ALU.add))
                                    dve.sem_inc(y_ok.sem, 1)
                                    row_stats(dve, v, y, stats, mv, P)
                                    dve.sem_inc(var_ok.sem, 1)
                                    root_ok.wait(dve, i, b, 2)
                                    row_affine(dve, v, mv, P)
                                    dve.sem_inc(affine_ok.sem, 1)
                                assert v.n == PER, v.n
                                return
                            if first:
                                v = Steps(dve, dve4b, i * 8 + b * 4)
                                v.wait()
                                prod_ok.wait(dve, i, b, 1)
                                dve.wait_ge(f_out[b], 16 * i)
                                v.link(dve.tensor_tensor(split(of[b][:, 0:D]), halves(pO[0]), split(bias[0][:]), ALU.add))
                                linear_part(dve, v, of[b], attr, lost, 1, P)
                                dve.sem_inc(evac_ok.sem, 1)
                                prod_ok.wait(dve, i, b, 2)
                                row = of_tile(fdt, i, b)
                                v.link(dve.tensor_tensor(split(o2[:]), halves(pO[1]), split(bias[1][:]), ALU.add))
                                v.mark(dve.tensor_tensor_reduce(
                                    out=lost[:], in0=o2[:], in1=attr[:], scale=0.2, scalar=0.0, op0=ALU.mult,
                                    op1=ALU.add, accum_out=lin2[:]))
                                v.wait()
                                dve.sem_inc(evac_ok.sem, 1)
                                kept(dve, row, i, b)
                            else:
                                prod_ok.wait(dve, i, b, 1)
                                dve.tensor_tensor(split(of_tile(acc, i, b)[:, 0:D]), halves(pO[0]), split(bias[0][:]),
                                                  ALU.add).then_inc(evac_ok.sem, 1)

                        if first:
                            o2 = sb("o2", [P, D], F32, st)
                            lin2 = sb("lin2", [P, 1], F32, st)
                            fd_ok = Signal(st, "fd_ok", 2, 2, 2)
                            fd_ok.open(dve)

                            def kept(dve, row, i, b):
                                dve.tensor_copy(row[:, 0:D], o2[:]).then_inc(fd_ok.sem, 1)
                                dve.tensor_copy(row[:, D:D + 1], lin2[:]).then_inc(fd_ok.sem, 1)
                                fd_ok.wait(dve, i, b)

                        twice(step, dve)

        settle(True)
        attention("second", 1, io["L0_gnn_attno"], None)
        settle(False)

        with stage() as st:
            byrel = [sb(f"byrel{k}", [P, P], I32, st) for k in range(2)]
            byrelf = [sb(f"byrelf{k}", [P, P], F32, st) for k in range(2)]
            source = sb("source", [P, 2 * P], I32, st)
            gindex = sb("gindex", [P, 1], I32, st)
            g = sb("g", [P, D], F32, st)
            gT = sb("gT", [P, D], F32, st)
            y = sb("y", [P, D], F32, st)
            nothing = sb("nothing", [P, D], F32, st)
            wr = [sb(f"wr{b}", [P, KC, D], F32, st) for b in range(2)]
            pT = pb("pT", [P, 2, 512], F32, st)
            pO = pb("pO", [P, 2, 512], F32, st)
            pI = pb("pI", [P, 512], F32, st)
            byrel_in, byrel_f, byrel_t, source_ok, copied, posted, g_in, y_out, all_out, zeroed, pe_posted, y_zero, sp_posted = sems(
                st, "byrel_in", "byrel_f", "byrel_t", "source_ok", "copied", "posted", "g_in", "y_out",
                "all_out", "zeroed", "pe_posted", "y_zero", "sp_posted")
            w_in = sems(st, "w_in0", "w_in1")
            t_ok = Signal(st, "t_ok", 1, 1)
            gT_ok = Signal(st, "gT_ok", KC, 1)
            used = Signal(st, "used", KC, 1)
            prod_ok = Signal(st, "prod_ok", 1, 1)
            evac_ok = Signal(st, "evac_ok", 2, 1)
            MAXT = RT
            MORE = RT - P

            def tiles_of(eng):
                return eng.value_load(ctl[0:1, C_REL + RELS - 1:C_REL + RELS], min_val=1, max_val=MAXT)

            with nc.Block() as block:
                @block.sync
                def _(sp):
                    sp.dma_start(byrel[0][:], byrel_d[0:P * P].rearrange("(t p) o -> t (p o)", p=P)).then_inc(byrel_in, 16)
                    sp.dma_start(byrel[1][0:MORE], byrel_d[P * P:RT * P].rearrange("(t p) o -> t (p o)", p=P))\
                      .then_inc(byrel_in, 16)
                    w_all = io["L1_gnn_W_rel"].rearrange("r (c p) n -> r p c n", p=P)
                    for b in range(2):
                        sp.dma_start(wr[b][:], w_all[b]).then_inc(w_in[b], 16)
                    sp.wait_ge(zeroed, 1)
                    with sp.Fori(tiles_of(sp), RT + 1) as n:
                        sp.dma_start(y_d[ds(n * P, P), :], nothing[:]).then_inc(y_zero, 16)
                    behind = sp.value_load(ctl[0:1, C_BEHIND:C_BEHIND + 1], min_val=1, max_val=RT)
                    sp.wait_ge(y_zero, behind * 16)
                    sp.sem_inc(sp_posted, 1)
                    with sp.Fori(1, RELS // 2) as i:
                        for b in range(2):
                            end = sp.value_load(ctl[0:1, ds(i * 2 + (C_REL + b - 2), 1)], min_val=1, max_val=MAXT)
                            used.wait(sp, end, -1)
                            sp.dma_start(wr[b][:], w_all[ds(i * 2 + b, 1)].rearrange("r p c n -> p (r c) n"))\
                              .then_inc(w_in[b], 16)
                    for b in range(2):
                        sp.wait_ge(w_in[b], 16 * (RELS // 2))

                @block.gpsimd
                def _(pool):
                    def fetch():
                        pool.indirect_dma_start(g[:], None, hr_d, bass.IndirectOffsetOnAxis(ap=gindex[:], axis=0))\
                            .then_inc(g_in, 16)

                    pool.wait_ge(source_ok, 3)
                    pool.tensor_copy(gindex[:], source[:, 0:1]).then_inc(copied, 1)
                    pool.wait_ge(copied, 1)
                    fetch()
                    tiles = tiles_of(pool)
                    with pool.Fori(0, tiles) as n:
                        pool.wait_ge(g_in, n * 16 + 16)
                        pool.sem_inc(posted, 1)
                        pool.tensor_copy(gindex[:], source[:, ds(n + 1, 1)]).then_inc(copied, 1)
                        pool.wait_ge(copied, n + 2)
                        t_ok.wait(pool, n, 0)
                        pool.sem_inc(posted, 1)
                        fetch()
                    pool.wait_ge(g_in, tiles * 16 + 16)
                    pool.sem_inc(posted, 1)

                @block.scalar
                def _(act):
                    gT_ok.open(act)

                    def copy(n, off):
                        t_ok.wait(act, n, off)
                        for c in range(KC):
                            used.wait(act, n, off - 1, c + 1)
                            act.activation(gT[:, c * P:(c + 1) * P], pT[:, c // 3, (c % 3) * P:(c % 3 + 1) * P],
                                           ACT.Copy).then_inc(gT_ok.sem, 1)

                    copy(0, 0)
                    tiles = tiles_of(act)
                    with act.Fori(0, tiles) as n:
                        copy(n, 1)
                        evac_ok.wait(act, n, 0)
                        act.dma_start(y_d[ds(n * P, P), :], y[:]).then_inc(y_out, 16)
                    act.wait_ge(y_out, tiles * 16)
                    act.sem_inc(all_out, 1)

                @block.tensor
                def _(pe):
                    for s in (t_ok, used, prod_ok):
                        s.open(pe)
                    for k in range(2):
                        rows = P if k == 0 else MORE
                        pe.wait_ge(byrel_f, k + 1)
                        pe.transpose(pI[:, k * P:k * P + rows], byrelf[k][0:rows, :], ident[0:rows, 0:rows])\
                            .then_inc(byrel_t, 1)

                    def turn(n, off):
                        pe.wait_ge(g_in, n * 16 + 16 * (off + 1))
                        gT_ok.wait(pe, n, off - 1)
                        pe_transpose(pe, pT, g, P).then_inc(t_ok.sem, 1)

                    turn(0, 0)
                    with pe.Fori(0, RELS // 2) as i:
                        for b in range(2):
                            first = pe.value_load(ctl[0:1, ds(i * 2 + (C_REL + b - 1), 1)], min_val=0, max_val=MAXT - 1)
                            end = pe.value_load(ctl[0:1, ds(i * 2 + (C_REL + b), 1)], min_val=1, max_val=MAXT)
                            pe.wait_ge(w_in[b], i * 16 + 16)
                            pe.sem_inc(pe_posted, 1)
                            with pe.Fori(first, end) as n:
                                for q, lo, up in HB:
                                    evac_ok.wait(pe, n, -1, q + 1)
                                    for c in range(KC):
                                        if q == 0:
                                            gT_ok.wait(pe, n, 0, c + 1)
                                        last = pe.matmul(pO[:, q, 0:HALF], gT[:, c * P:(c + 1) * P], wr[b][:, c, lo:up],
                                                         start=c == 0, stop=c == KC - 1)
                                        if q == 1:
                                            last.then_inc(used.sem, 1)
                                    if q == 0:
                                        last.then_inc(prod_ok.sem, 1)
                                        turn(n, 1)

                @block.vector
                def _(dve):
                    evac_ok.open(dve)
                    dve.memset(nothing[:], 0.0).then_inc(zeroed, 1)
                    dve.wait_ge(byrel_in, 32)
                    dve.memset(source[:, RT:2 * P], 0).then_inc(source_ok, 1)
                    for k in range(2):
                        rows = P if k == 0 else MORE
                        dve.tensor_copy(byrelf[k][0:rows], byrel[k][0:rows]).then_inc(byrel_f, 1)
                    dve.wait_ge(byrel_t, 2)
                    for k in range(2):
                        rows = P if k == 0 else MORE
                        dve.tensor_copy(source[:, k * P:k * P + rows], pI[:, k * P:k * P + rows]).then_inc(source_ok, 1)
                    tiles = tiles_of(dve)
                    with dve.Fori(0, tiles) as n:
                        for q, lo, up in HB:
                            (prod_ok, used)[q].wait(dve, n, 0)
                            dve.wait_ge(y_out, n * 16)
                            dve.tensor_copy(y[:, lo:up], pO[:, q, 0:HALF]).then_inc(evac_ok.sem, 1)

        def slot_sum(relations):
            with stage() as st:
                b = slot_buffers(st, D)
                b["places"] = [sb(f"places{u}", [P, S], F32, st) for u in range(U)]
                b["posted"], = sems(st, "rows_posted")
                ge = sb("ge", [P, S, RELS + 1], F32, st)
                of_rel = sb("of_rel", [P, S, RELS], F32, st)
                weight = sb("weight", [P, S], F32, st)
                dve_step, = sems(st, "dve_step")
                used = Signal(st, "used", S, U, U)
                with nc.Block() as block:
                    @block.gpsimd
                    def _(pool):
                        if relations:
                            gather_edges(pool, b, y_d, 1, used, keep_places=True)
                        else:
                            gather_edges(pool, b, xs_d, 0, used)

                    @block.vector
                    def _(dve):
                        used.open(dve)
                        PER = 5 if relations else 0
                        turns = dve.value_load(ctl[0:1, C_TURNS:C_TURNS + 1], min_val=1, max_val=MAX_TURNS)
                        with dve.Fori(0, turns) as i:
                            t = sum_tiles(dve, 0, U, i)
                            for u in range(U):
                                v = Steps(dve, dve_step, i * (PER * U) + u * PER)
                                b["valid"].wait(dve, i, u)
                                used.wait(dve, i, u - 1)
                                w = b["val"][u]
                                if relations:
                                    v.wait()
                                    shape = [P, S, RELS + 1]
                                    v.link(dve.tensor_tensor(ge[:], over(b["places"][u][:], 2, shape),
                                                             over(relbase[:], 1, shape), ALU.is_ge))
                                    v.link(dve.tensor_tensor(of_rel[:], ge[:, :, 0:RELS], ge[:, :, 1:RELS + 1],
                                                             ALU.subtract))
                                    rc = rcnt[:, ds(t[u], 1), :].rearrange("p o r -> p (o r)")
                                    v.link(dve.tensor_tensor(of_rel[:], of_rel[:], over(rc, 1, [P, S, RELS]), ALU.mult))
                                    v.link(dve.tensor_reduce(weight[:], of_rel[:], X, ALU.add))
                                    v.link(dve.tensor_tensor(weight[:], weight[:], w[:], ALU.mult))
                                    w = weight
                                rows_wait(dve, b, i, u)
                                into = acc[:, ds(t[u], 1), 0:D].rearrange("p o f -> p (o f)")
                                for j in range(S):
                                    used.wait(dve, i, u, j)
                                    dve.scalar_tensor_tensor(out=into, in0=b["row"][u][j][:], scalar=w[:, j:j + 1], in1=into,
                                                             op0=ALU.mult, op1=ALU.add).then_inc(used.sem, 1)

        slot_sum(True)

        dinv = sb("dinv", [P, NT + 1], F32)
        xs_d = dram("xs_d", (NP, D), F32)
        with stage() as st:
            wg = sb("wg", [P, KC, D], F32, st)
            ht = [sb(f"ht{b}", [P, D], F32, st) for b in range(2)]
            hT = [sb(f"hT{b}", [P, D], F32, st) for b in range(2)]
            of = [sb(f"of{b}", [P, D], F32, st) for b in range(2)]
            pT = pb("pT", [P, 2, 512], F32, st)
            pO = pb("pO", [P, 2, 512], F32, st)
            w_in, deg_ok, root_ok = sems(st, "w_in", "deg_ok", "root_ok")
            f_out = sems(st, "f_out0", "f_out1")
            h_ok, t_ok, hT_ok, prod_ok = (Signal(st, n, 1, 2, 2) for n in ("h_ok", "t_ok", "hT_ok", "prod_ok"))
            evac_ok = Signal(st, "evac_ok", 1, 2, 2)
            kept_ok = Signal(st, "kept_ok", 1, 2, 2)
            with nc.Block() as block:
                @block.sync
                def _(sp):
                    sp.dma_start(wg[:], w_view(io["L1_gnn_W_gcn"])).then_inc(w_in, 16)
                    sp.wait_ge(w_in, 16)

                @block.gpsimd
                def _(pool):
                    for n in range(NT):
                        evac_ok.wait(pool, 0, n)
                        pool.indirect_dma_start(xs_d, bass.IndirectOffsetOnAxis(ap=perm[:, n:n + 1], axis=0),
                                                of[n % 2][:], None).then_inc(f_out[n % 2], 16)
                    for b in range(2):
                        pool.wait_ge(f_out[b], 16 * NT // 2)

                @block.scalar
                def _(act):
                    for s in (h_ok, hT_ok):
                        s.open(act)
                    act.wait_ge(deg_ok, 1)
                    act.activation(dinv[:], dinv[:], ACT.Sqrt).then_inc(root_ok, 1)

                    def rows(i, b):
                        t_ok.wait(act, i, b - 2)
                        act.activation(ht[b][:], acc[:, ds(i * 2 + b, 1), 0:D].rearrange("p o f -> p (o f)"), ACT.Copy)\
                           .then_inc(h_ok.sem, 1)

                    with act.Fori(0, NT // 2) as i:
                        for b in range(2):
                            rows(i, b)
                            t_ok.wait(act, i, b)
                            prod_ok.wait(act, i, b - 2)
                            act.activation(split(hT[b][:]), halves(pT), ACT.Copy).then_inc(hT_ok.sem, 1)

                @block.tensor
                def _(pe):
                    for s in (t_ok, prod_ok):
                        s.open(pe)

                    def product(i, off):
                        hT_ok.wait(pe, i, off)
                        evac_ok.wait(pe, i, off - 1)
                        pe_product(pe, pO, hT[off % 2], wg, P).then_inc(prod_ok.sem, 1)

                    def turn(i, off):
                        h_ok.wait(pe, i, off)
                        hT_ok.wait(pe, i, off - 1)
                        pe_transpose(pe, pT, ht[off % 2], P).then_inc(t_ok.sem, 1)

                    pe.wait_ge(w_in, 16)
                    turn(0, 0)
                    with pe.Fori(0, NT // 2 - 1) as i:
                        for b in range(2):
                            turn(i, b + 1)
                            product(i, b)
                    turn(NT // 2 - 1, 1)
                    product(NT // 2 - 1, 0)
                    product(NT // 2 - 1, 1)

                @block.vector
                def _(dve):
                    for s in (evac_ok, kept_ok):
                        s.open(dve)
                    dve.tensor_scalar(dinv[:], degr[:], 1.0, None, ALU.add).then_inc(deg_ok, 1)
                    dve.wait_ge(root_ok, 1)
                    dve.reciprocal(dinv[:], dinv[:]).then_inc(root_ok, 1)
                    dve.wait_ge(root_ok, 2)
                    with dve.Fori(0, NT // 2) as i:
                        for b in range(2):
                            prod_ok.wait(dve, i, b)
                            dve.wait_ge(f_out[b], i * 16)
                            kept_ok.wait(dve, i, b - 2)
                            dve.tensor_scalar(split(of[b][:]), halves(pO), dinv[:, ds(i * 2 + b, 1)], None, ALU.mult)\
                               .then_inc(evac_ok.sem, 1)
                            evac_ok.wait(dve, i, b)
                            dve.tensor_copy(acc[:, ds(i * 2 + b, 1), 0:D].rearrange("p o f -> p (o f)"), of[b][:])\
                               .then_inc(kept_ok.sem, 1)

        slot_sum(False)

        with stage() as st:
            bg = sb("bg", [P, D], F32, st)
            b_in, stored = sems(st, "b_in", "stored")
            scaled2, final = sems(st, "scaled2", "final")
            with nc.Block() as block:
                @block.sync
                def _(sp):
                    sp.dma_start(bg[:], io["L1_gnn_b_gcn"].partition_broadcast(P)).then_inc(b_in, 16)
                    sp.wait_ge(b_in, 16)

                @block.vector
                def _(dve):
                    dve.wait_ge(b_in, 16)
                    for t in range(NT):
                        dve.scalar_tensor_tensor(out=acc[:, t, 0:D], in0=acc[:, t, 0:D], scalar=dinv[:, t:t + 1],
                                                 in1=bg[:], op0=ALU.mult, op1=ALU.add).then_inc(scaled2, 1)
                        dve.wait_ge(scaled2, t + 1)
                        dve.tensor_tensor(acc[:, t, 0:D], acc[:, t, 0:D], fdt[:, t, 0:D], ALU.add).then_inc(final, 1)

                @block.gpsimd
                def _(pool):
                    for t in range(NT):
                        rows = P if t < NT - 1 else LAST
                        pool.wait_ge(final, t + 1)
                        pool.indirect_dma_start(out, bass.IndirectOffsetOnAxis(ap=perm[0:rows, t:t + 1], axis=0),
                                                acc[0:rows, t, 0:D], None).then_inc(stored, 16)
                    pool.wait_ge(stored, 16 * NT)


_INS = ['x', 'src', 'dst', 'edge_type_34', 'L0_gnn_W1s', 'L0_gnn_b1s', 'L0_gnn_W1d', 'L0_gnn_b1d', 'L0_gnn_attn1',
        'L0_gnn_ln1_w', 'L0_gnn_ln1_b', 'L0_gnn_Wos', 'L0_gnn_bos', 'L0_gnn_Wod', 'L0_gnn_bod', 'L0_gnn_attno',
        'L0_gnn_lno_w', 'L0_gnn_lno_b', 'L1_gnn_W_rel', 'L1_gnn_W_root', 'L1_gnn_b_rgcn', 'L1_gnn_W_gcn',
        'L1_gnn_b_gcn']


def kernel(**inputs):
    import numpy as _np
    import concourse.bacc as _bacc
    from concourse import mybir as _mybir
    from concourse.bass_utils import run_bass_kernel_spmd as _run

    nc = _bacc.Bacc("TRN2", target_bir_lowering=False, num_devices=1)
    arrays, io = {}, {}
    for name in _INS:
        a = _np.ascontiguousarray(inputs[name])
        arrays[f"in_{name}_dram"] = a
        io[name] = nc.dram_tensor(f"in_{name}_dram", a.shape, _mybir.dt.from_np(a.dtype), kind="ExternalInput").ap()
    out = nc.dram_tensor("out_0_dram", (N, D), _mybir.dt.float32, kind="ExternalOutput").ap()
    gnn_kernel(nc, io, out)
    r = _run(nc, [arrays], core_ids=[0])
    return r.results[0]["out_0_dram"]
```

```python
import concourse.bass as bass
from concourse import mybir
from contextlib import ExitStack, contextmanager

F32, I32, BF16 = mybir.dt.float32, mybir.dt.int32, mybir.dt.bfloat16
ALU = mybir.AluOpType
ACT = mybir.ActivationFunctionType
X = mybir.AxisListType.X
ds = bass.ds

N, E, D, HEADS, RELS = 1250, 20000, 768, 8, 34
P = 128
NT = (N + P - 1) // P
NP = NT * P
LAST = N - (NT - 1) * P
EP, EC = 125, 160
assert EP * EC == E and NT < 16
KC = D // P
W = D + HEADS
HALF = D // 2
ROWS_AHEAD = 2
S = 4
U = 4
TBACK = 2
PACK = 6
NROW = NP
ZB = 16
ZBLOCKS = -(-(E // S + U) // ZB)
GROUPS = ZBLOCKS * ZB
TG = 5120
MAX_TURNS = (E // S + NT) // U + 1
LEAST = 2
RT = E // P + LEAST * RELS
BIG = 1e30
EPS = 1e-5
DA, DB = 40, 32


class Steps:

    def __init__(self, eng, sem, base=0, carrier=None):
        self.eng, self.sem, self.base, self.n, self.carrier = eng, sem, base, 0, carrier

    def mark(self, ins):
        ins.then_inc(self.sem, 1)
        self.n += 1
        return self.n

    def wait(self, n=None):
        self.eng.wait_ge(self.sem, self.base + (self.n if n is None else n))
        if self.carrier is not None:
            self.eng.sem_inc(self.carrier, 1)

    def tick(self):
        self.eng.sem_inc(self.sem, 1)
        self.n += 1

    def link(self, ins):
        self.mark(ins)
        self.wait()


def over(ap, axis, shape):
    return ap.unsqueeze(axis).to_broadcast(shape)


def gnn_kernel(nc, io, out):
    ctx = ExitStack()
    with ctx:
        taken = {}

        def fresh(name):
            taken[name] = taken.get(name, 0) + 1
            return name if taken[name] == 1 else f"{name}_{taken[name]}"

        def sb(name, shape, dt, where=ctx):
            return where.enter_context(nc.sbuf_tensor(fresh(name), shape, dt))

        def pb(name, shape, dt, where):
            return where.enter_context(nc.psum_tensor(fresh(name), shape, dt))

        def dram(name, shape, dt):
            return nc.dram_tensor(name, shape, dt, kind="Internal").ap()

        deg_d = dram("deg_d", (NP,), F32)
        by_rank_d = dram("by_rank_d", (NP, 2), I32)
        tile_of_group_d = dram("tile_of_group_d", (TG,), I32)
        slots_d = dram("slots_d", (GROUPS * NROW * S, 2), I32)
        byrel_d = dram("byrel_d", (RT * P, 1), I32)
        h0_d = dram("h0_d", (NP, D), F32)
        fs_d = dram("fs_d", (NP, W), F32)
        fd_d = dram("fd_d", (NP, W), F32)

        ident = sb("ident", [P, P], F32)
        ones = sb("ones", [P, P], F32)
        ctl = sb("ctl", [1, 64], I32)
        C_TURNS, C_ZERO, C_RANKS, C_BEHIND, C_REL = 0, 1, 2, 3, 8
        tile_of_group = sb("tile_of_group", [1, TG], I32)
        perm = sb("perm", [P, NT + 1], I32)
        permc = sb("permc", [P, NT + 1], I32)
        degr = sb("degr", [P, NT + 1], F32)
        relbase = sb("relbase", [P, RELS + 1], F32)
        recs = sb("recs", [EP, EC, 2], I32)
        slotpos = sb("slotpos", [EP, EC], I32)
        dstf = sb("dstf", [EP, EC], F32)
        ksort = sb("ksort", [EP, EC], F32)
        unsorted = sb("unsorted", [P, 1], F32)
        zero_i = sb("zero_i", [P, 1], I32)
        nrow = sb("nrow", [P, NP], F32)

        def sems(where, *names):
            made = [nc.alloc_semaphore(fresh(n)) for n in names]
            where.semaphores += made
            return made

        @contextmanager
        def stage():
            with ExitStack() as st:
                st.semaphores = []
                yield st
                nc.clear_and_free_semaphores(st.semaphores)
                nc.all_engine_barrier()

        with stage() as st:
            lower = sb("lower", [P, P], F32, st)
            before = sb("before", [P, P], F32, st)
            mrow = sb("mrow", [P, 1792], F32, st)
            arow = sb("arow", [P, DA], F32, st)
            eidx = sb("eidx", [EP, EC], F32, st)
            gidx = sb("gidx", [P, TG // P, PACK], F32, st)
            ncol = sb("ncol", [P, NT], F32, st)
            zeros = sb("zeros", [P, ZB * NROW * S * 2 // P], I32, st)
            dsti = sb("dsti", [EP, EC], I32, st)
            srci = sb("srci", [EP, EC], I32, st)
            typi = sb("typi", [EP, EC], I32, st)
            previ = sb("previ", [EP, EC], I32, st)
            ai = sb("ai", [EP, EC], I32, st)
            bi = sb("bi", [EP, EC], I32, st)
            af = sb("af", [EP, EC], F32, st)
            bf = sb("bf", [EP, EC], F32, st)
            oa = sb("oa", [EP, EC, DA], BF16, st)
            ob = sb("ob", [EP, EC, DB], BF16, st)
            ot = sb("ot", [EP, RELS, EC], F32, st)
            sc = sb("sc", [EP, RELS, EC], F32, st)
            cn = sb("cn", [EP, RELS], F32, st)
            reli = sb("reli", [P, RELS], I32, st)
            relt = sb("relt", [P, RELS], F32, st)
            rele = sb("rele", [P, RELS], F32, st)
            adj = sb("adj", [EP, RELS], F32, st)
            place = sb("place", [EP, EC], F32, st)
            start = sb("start", [EP, EC], F32, st)
            diag = sb("diag", [EP, EP], F32, st)
            carry = sb("carry", [EP, 1], F32, st)
            back = sb("back", [EP, 1], F32, st)
            degab = sb("degab", [DA, DB], F32, st)
            keyrow = sb("keyrow", [P, NP], F32, st)
            keycol = sb("keycol", [P, NT], F32, st)
            junk = sb("junk", [P, 1792], F32, st)
            rank = sb("rank", [P, NT], F32, st)
            ranki = sb("ranki", [P, NT], I32, st)
            nodeinfo = sb("nodeinfo", [P, NT, 2], I32, st)
            byrank = sb("byrank", [P, NT, 2], I32, st)
            kmax = sb("kmax", [P, NT], F32, st)
            kmaxi = sb("kmaxi", [P, NT], I32, st)
            gend = sb("gend", [P, NT], F32, st)
            small = sb("small", [P, 4], F32, st)
            tog = sb("tog", [P, TG // P, PACK], F32, st)
            packed = sb("packed", [P, TG // P], F32, st)
            togi = sb("togi", [P, TG // P], I32, st)
            p_deg = pb("p_deg", [DA, 512], F32, st)
            p_rel = pb("p_rel", [P, 512], F32, st)
            p_tot = pb("p_tot", [P, 512], F32, st)
            p_car = pb("p_car", [P, 512], F32, st)
            p_uns = pb("p_uns", [P, 512], F32, st)
            (const_built, dve_step, edges_in, prev_in, onehots, degrees, counted, relsums, starts,
             carries, deg_sb, deg_out, deg_in, ranks, by_rank_out, by_rank_in, maxima, tog_ready,
             tog_out, tog_in, zero_ready, clear, degr_ready, cleared, rel_clear) = sems(
                 st, "const_built", "dve_step", "edges_in", "prev_in", "onehots", "degrees",
                 "counted", "relsums", "starts", "carries", "deg_sb", "deg_out", "deg_in", "ranks",
                 "by_rank_out", "by_rank_in", "maxima", "tog_ready", "tog_out", "tog_in",
                 "zero_ready", "clear", "degr_ready", "cleared",
                 "rel_clear")
            CONSTS = 15
            with nc.Block() as block:
                @block.sync
                def _(sp):
                    e2 = lambda a: a.rearrange("(p c) -> p c", p=EP)
                    sp.dma_start(dsti[:], e2(io["dst"])).then_inc(edges_in, 16)
                    sp.dma_start(typi[:], e2(io["edge_type_34"])).then_inc(edges_in, 16)
                    sp.dma_start(srci[:], e2(io["src"])).then_inc(edges_in, 16)
                    sp.dma_start(previ[1:EP, 0:1], e2(io["dst"])[0:EP - 1, EC - 1:EC],
                                 allow_slow_non_contiguous=True).then_inc(prev_in, 16)
                    sp.wait_ge(deg_sb, 1)
                    sp.dma_start(deg_d.rearrange("(a b) -> a b", a=DA), degab[:]).then_inc(deg_out, 16)
                    sp.wait_ge(deg_out, 16)
                    sp.dma_start(keyrow[:], deg_d.partition_broadcast(P)).then_inc(deg_in, 16)
                    sp.dma_start(keycol[:], deg_d.rearrange("(t p) -> p t", p=P),
                                 allow_slow_non_contiguous=True).then_inc(deg_in, 16)
                    sp.wait_ge(by_rank_out, 16 * NT)
                    sp.dma_start(byrank[:], by_rank_d.rearrange("(t p) c -> p t c", p=P)).then_inc(by_rank_in, 16)
                    sp.wait_ge(tog_ready, 1)
                    sp.dma_start(tile_of_group_d.rearrange("(p c) -> p c", p=P), togi[:]).then_inc(tog_out, 16)
                    sp.wait_ge(tog_out, 16)
                    sp.dma_start(tile_of_group[:], tile_of_group_d.unsqueeze(0)).then_inc(tog_in, 16)
                    n_zero = sp.value_load(ctl[0:1, C_ZERO:C_ZERO + 1], min_val=1, max_val=ZBLOCKS)
                    slots_z = slots_d.rearrange("(z p f) c -> z p (f c)", z=ZBLOCKS, p=P)
                    sp.wait_ge(zero_ready, 1)
                    with sp.Fori(0, n_zero) as z:
                        sp.wait_ge(clear, z * 16)
                        sp.dma_start(slots_z[ds(z, 1)].rearrange("z p f -> (z p) f"), zeros[:]).then_inc(clear, 16)
                    sp.dma_start(byrel_d.rearrange("(p f) o -> p (f o)", p=P), zeros[:, 0:RT]).then_inc(rel_clear, 16)
                    sp.wait_ge(rel_clear, 16)
                    sp.wait_ge(clear, n_zero * 16)
                    sp.sem_inc(cleared, 1)
                    sp.wait_ge(tog_in, 16)

                @block.gpsimd
                def _(pool):
                    c = Steps(pool, const_built)
                    iota = dict(allow_small_or_imprecise_dtypes=True)
                    pool.memset(zeros[:], 0).then_inc(zero_ready, 1)
                    c.mark(pool.memset(zero_i[:], 0))
                    c.mark(pool.memset(ones[:], 1.0))
                    c.mark(pool.iota(arow[:], [[1, DA]], base=0, channel_multiplier=0, **iota))
                    c.mark(pool.iota(eidx[:], [[1, EC]], base=0, channel_multiplier=EC, **iota))
                    c.mark(pool.memset(previ[0:1, 0:1], -1))
                    c.mark(pool.memset(lower[:], 1.0))
                    c.mark(pool.memset(before[:], 1.0))
                    c.link(pool.memset(ident[:], 0.0))
                    c.mark(pool.affine_select(out=ident[:], in_=ident[:], compare_op=ALU.not_equal, fill=1.0,
                                              base=0, pattern=[[-1, P]], channel_multiplier=1))
                    c.mark(pool.affine_select(out=lower[:], in_=lower[:], compare_op=ALU.is_gt, fill=0.0,
                                              base=0, pattern=[[1, P]], channel_multiplier=-1))
                    c.mark(pool.affine_select(out=before[:], in_=before[:], compare_op=ALU.is_gt, fill=0.0,
                                              base=0, pattern=[[-1, P]], channel_multiplier=1))
                    c.mark(pool.iota(mrow[:], [[1, 1792]], base=0, channel_multiplier=0, **iota))
                    c.mark(pool.iota(nrow[:], [[1, NP]], base=0, channel_multiplier=0, **iota))
                    c.mark(pool.iota(gidx[:], [[1, TG // P], [1, PACK]], base=-TBACK, channel_multiplier=TG // P, **iota))
                    c.mark(pool.iota(ncol[:], [[P, NT]], base=0, channel_multiplier=1, **iota))
                    assert c.n == CONSTS
                    pool.wait_ge(ranks, 1)
                    for t in range(NT):
                        pool.indirect_dma_start(by_rank_d, bass.IndirectOffsetOnAxis(ap=ranki[:, t:t + 1], axis=0),
                                                nodeinfo[:, t, :], None).then_inc(by_rank_out, 16)
                    pool.wait_ge(by_rank_out, 16 * NT)
                    pool.wait_ge(degr_ready, 1)
                    pool.partition_all_reduce(kmax[:], degr[:, 0:NT], P, bass.bass_isa.ReduceOp.max).then_inc(maxima, 1)

                @block.tensor
                def _(pe):
                    pe.wait_ge(onehots, 1)
                    for c in range(EC):
                        last = pe.matmul(p_deg[:, 0:DB], oa[:, c, :], ob[:, c, :], start=c == 0, stop=c == EC - 1)
                    last.then_inc(degrees, 1)
                    pe.wait_ge(counted, 1)
                    pe.wait_ge(const_built, CONSTS)
                    pe.matmul(p_rel[0:EP, 0:RELS], lower[0:EP, 0:EP], cn[:], start=True, stop=True)
                    pe.matmul(p_tot[:, 0:RELS], ones[0:EP, :], cn[:], start=True, stop=True).then_inc(relsums, 1)
                    pe.wait_ge(starts, 1)
                    pe.matmul(p_car[0:EP, 0:EP], ones[0:EP, 0:EP], diag[:], start=True, stop=True)
                    pe.matmul(p_uns[:, 0:1], ones[0:EP, :], back[:], start=True, stop=True).then_inc(carries, 1)

                @block.vector
                def _(dve):
                    v = Steps(dve, dve_step)
                    e3 = [EP, EC, DA]
                    dve.wait_ge(edges_in, 48)
                    dve.wait_ge(const_built, CONSTS)
                    v.link(dve.memset(ctl[:], 0))
                    v.mark(dve.tensor_scalar(ai[:], dsti[:], 5, None, ALU.logical_shift_right))
                    v.mark(dve.tensor_scalar(bi[:], dsti[:], DB - 1, None, ALU.bitwise_and))
                    v.link(dve.tensor_copy(dstf[:], dsti[:]))
                    v.mark(dve.tensor_copy(af[:], ai[:]))
                    v.link(dve.tensor_copy(bf[:], bi[:]))
                    v.mark(dve.tensor_tensor(oa[:], over(af[:], 2, e3), over(arow[0:EP], 1, e3), ALU.is_equal))
                    e3 = [EP, EC, DB]
                    v.link(dve.tensor_tensor(ob[:], over(bf[:], 2, e3), over(arow[0:EP, 0:DB], 1, e3), ALU.is_equal))
                    dve.sem_inc(onehots, 1)
                    r3 = [EP, RELS, EC]
                    v.link(dve.tensor_copy(af[:], typi[:]))
                    v.link(dve.tensor_tensor(ot[:], over(af[:], 1, r3), over(arow[0:EP, 0:RELS], 2, r3), ALU.is_equal))
                    v.link(dve.tensor_reduce(cn[:], ot[:], X, ALU.add))
                    dve.sem_inc(counted, 1)
                    flat = "p r c -> p (r c)"
                    v.link(dve.tensor_tensor_scan(sc[:].rearrange(flat), ot[:].rearrange(flat), ot[:].rearrange(flat),
                                                  0.0, ALU.add, ALU.max))
                    dve.wait_ge(relsums, 1)
                    v.link(dve.tensor_scalar(relt[:], p_tot[:, 0:RELS], float(P - 1), None, ALU.add))
                    v.link(dve.tensor_copy(reli[:], relt[:]))
                    v.link(dve.tensor_scalar(reli[:], reli[:], 7, None, ALU.logical_shift_right))
                    v.link(dve.tensor_scalar(relt[:], reli[:], float(LEAST), None, ALU.max))
                    v.link(dve.tensor_tensor_scan(rele[:], relt[:], relt[:], 0.0, ALU.add, ALU.max))
                    v.mark(dve.tensor_copy(ctl[0:1, C_REL:C_REL + RELS], rele[0:1, :]))
                    v.mark(dve.memset(ctl[0:1, C_REL - 1:C_REL], 0))
                    v.mark(dve.tensor_scalar(ctl[0:1, C_BEHIND:C_BEHIND + 1], rele[0:1, RELS - 1:RELS], -1.0,
                                             float(RT + 1), ALU.mult, ALU.add))
                    v.mark(dve.memset(relbase[:, RELS:RELS + 1], BIG))
                    v.link(dve.tensor_tensor(relt[:], rele[:], relt[:], ALU.subtract))
                    v.link(dve.tensor_scalar(relbase[:, 0:RELS], relt[:], float(P), None, ALU.mult))
                    v.link(dve.tensor_tensor(adj[:], relbase[0:EP, 0:RELS], p_rel[0:EP, 0:RELS], ALU.add))
                    v.link(dve.tensor_tensor(adj[:], adj[:], cn[:], ALU.add))
                    v.link(dve.tensor_tensor(adj[:], adj[:], sc[:, :, EC - 1], ALU.subtract))
                    v.link(dve.tensor_tensor(sc[:], sc[:], over(adj[:], 2, r3), ALU.add))
                    v.link(dve.tensor_tensor(sc[:], sc[:], ot[:], ALU.mult))
                    v.link(dve.tensor_reduce(place[:], sc[:].rearrange("p r c -> p c r"), X, ALU.add))
                    v.mark(dve.tensor_scalar(recs[:, :, 1], place[:], -1.0, None, ALU.add))
                    v.mark(dve.tensor_copy(recs[:, :, 0], srci[:]))
                    dve.wait_ge(prev_in, 16)
                    v.link(dve.tensor_copy(previ[:, 1:EC], dsti[:, 0:EC - 1]))
                    v.link(dve.tensor_copy(bf[:], previ[:]))
                    v.mark(dve.tensor_tensor(start[:], dstf[:], bf[:], ALU.not_equal))
                    v.link(dve.tensor_tensor(af[:], dstf[:], bf[:], ALU.is_lt))
                    v.mark(dve.tensor_reduce(back[:], af[:], X, ALU.max))
                    v.link(dve.tensor_tensor(start[:], start[:], eidx[:], ALU.mult))
                    v.link(dve.tensor_tensor_scan(bf[:], start[:], start[:], 0.0, ALU.max, ALU.max))
                    v.link(dve.tensor_scalar(diag[:], ident[0:EP, 0:EP], bf[:, EC - 1:EC], None, ALU.mult))
                    dve.sem_inc(starts, 1)
                    dve.wait_ge(carries, 1)
                    v.mark(dve.tensor_tensor_reduce(out=junk[0:EP, 0:EP], in0=p_car[0:EP, 0:EP], in1=before[0:EP, 0:EP],
                                                    scale=1.0, scalar=0.0, op0=ALU.mult, op1=ALU.max,
                                                    accum_out=carry[:]))
                    v.link(dve.tensor_scalar(unsorted[:], p_uns[:, 0:1], 1.0, None, ALU.min))
                    v.mark(dve.tensor_scalar(ctl[0:1, C_RANKS:C_RANKS + 1], unsorted[0:1, :], float(EC - 1), 1.0,
                                             ALU.mult, ALU.add))
                    v.link(dve.tensor_scalar(bf[:], bf[:], carry[:], None, ALU.max))
                    v.link(dve.tensor_tensor(ksort[:], eidx[:], bf[:], ALU.subtract))
                    dve.wait_ge(degrees, 1)
                    v.link(dve.tensor_copy(degab[:], p_deg[:, 0:DB]))
                    dve.sem_inc(deg_sb, 1)
                    dve.wait_ge(deg_in, 32)
                    v.mark(dve.tensor_copy(nodeinfo[:, :, 0], ncol[:]))
                    v.link(dve.tensor_copy(nodeinfo[:, :, 1], keycol[:]))
                    v.mark(dve.tensor_scalar(keyrow[:], keyrow[:], 4095.0, 2048.0, ALU.min, ALU.mult))
                    v.link(dve.tensor_scalar(keycol[:], keycol[:], 4095.0, 2048.0, ALU.min, ALU.mult))
                    v.mark(dve.tensor_tensor(keyrow[:], keyrow[:], nrow[:], ALU.subtract))
                    v.link(dve.tensor_tensor(keycol[:], keycol[:], ncol[:], ALU.subtract))
                    for t in range(NT):
                        v.link(dve.tensor_scalar(junk[:, 0:NP], keyrow[:], keycol[:, t:t + 1], 0.0, ALU.is_gt, ALU.add,
                                                 accum_out=rank[:, t:t + 1]))
                    v.link(dve.tensor_copy(ranki[:], rank[:]))
                    dve.sem_inc(ranks, 1)
                    dve.wait_ge(by_rank_in, 16)
                    v.mark(dve.memset(perm[:, NT:NT + 1], NP - 1))
                    v.mark(dve.memset(degr[:, NT:NT + 1], 0.0))
                    v.mark(dve.tensor_copy(perm[:, 0:NT], byrank[:, :, 0]))
                    v.link(dve.tensor_copy(degr[:, 0:NT], byrank[:, :, 1]))
                    dve.sem_inc(degr_ready, 1)
                    v.mark(dve.tensor_scalar(permc[:], perm[:], float(N - 1), None, ALU.min))
                    dve.wait_ge(maxima, 1)
                    v.link(dve.tensor_reduce(small[:, 0:1], kmax[:], X, ALU.max))
                    v.link(dve.tensor_scalar(kmaxi[:], kmax[:], float(S - 1), None, ALU.add))
                    v.link(dve.tensor_scalar(kmaxi[:], kmaxi[:], 2, None, ALU.logical_shift_right))
                    v.link(dve.tensor_copy(kmax[:], kmaxi[:]))
                    v.link(dve.tensor_tensor_scan(gend[:], kmax[:], kmax[:], 0.0, ALU.add, ALU.max))
                    v.mark(dve.tensor_scalar(small[:, 2:3], small[:, 0:1], 1.0 / (S * ZB), None, ALU.mult))
                    v.link(dve.tensor_scalar(small[:, 3:4], gend[:, NT - 1:NT], 1.0 / U, -0.125, ALU.mult, ALU.add))
                    v.link(dve.tensor_scalar(junk[:], mrow[:], small[:, 2:3], 0.0, ALU.is_lt, ALU.add,
                                             accum_out=small[:, 0:1]))
                    v.link(dve.tensor_scalar(junk[:], mrow[:], small[:, 3:4], 0.0, ALU.is_lt, ALU.add,
                                             accum_out=small[:, 1:2]))
                    v.mark(dve.tensor_scalar(ctl[0:1, C_ZERO:C_ZERO + 1], small[0:1, 0:1], 1.0, None, ALU.max))
                    v.mark(dve.tensor_scalar(ctl[0:1, C_TURNS:C_TURNS + 1], small[0:1, 1:2], 1.0, None, ALU.max))
                    v.link(dve.memset(tog[:], 0.0))
                    for t in range(NT):
                        v.link(dve.scalar_tensor_tensor(out=tog[:], in0=gidx[:], scalar=gend[:, t:t + 1], in1=tog[:],
                                                        op0=ALU.is_ge, op1=ALU.add))
                    v.link(dve.tensor_copy(packed[:], tog[:, :, PACK - 1]))
                    for k in reversed(range(PACK - 1)):
                        v.link(dve.scalar_tensor_tensor(out=packed[:], in0=packed[:], scalar=16.0, in1=tog[:, :, k],
                                                        op0=ALU.mult, op1=ALU.add))
                    v.link(dve.tensor_copy(togi[:], packed[:]))
                    dve.sem_inc(tog_ready, 1)

        with stage() as st:
            lowb = sb("lowb", [EP, EP], BF16, st)
            onesb = sb("onesb", [EP, EP], BF16, st)
            onehot = sb("onehot", [EP, NP], BF16, st)
            seen = sb("seen", [EP, NP], F32, st)
            ahead = sb("ahead", [EP, NP], F32, st)
            kcol = sb("kcol", [EP, 1], F32, st)
            dcol = sb("dcol", [EP, 1], F32, st)
            kgen = sb("kgen", [EP, EC], F32, st)
            ki = sb("ki", [EP, EC], I32, st)
            hi = sb("hi", [EP, EC], I32, st)
            p_low = pb("p_low", [P, 3, 512], F32, st)
            p_all = pb("p_all", [P, 3, 512], F32, st)
            tri, step2, hot_ready, sums = sems(st, "tri", "step2", "hot_ready", "sums")
            BANKS = [(0, 512), (1, 512), (2, NP - 1024)]
            with nc.Block() as block:
                @block.gpsimd
                def _(pool):
                    pool.memset(onesb[:], 1.0).then_inc(tri, 1)
                    pool.memset(lowb[:], 1.0).then_inc(tri, 1)
                    pool.wait_ge(tri, 2)
                    pool.affine_select(out=lowb[:], in_=lowb[:], compare_op=ALU.is_gt, fill=0.0, base=0,
                                       pattern=[[1, EP]], channel_multiplier=-1).then_inc(tri, 1)

                @block.tensor
                def _(pe):
                    n = pe.value_load(ctl[0:1, C_RANKS:C_RANKS + 1], min_val=1, max_val=EC)
                    pe.wait_ge(tri, 3)
                    with pe.Fori(0, n) as c:
                        pe.wait_ge(hot_ready, c + 1)
                        for q, w in BANKS:
                            pe.matmul(p_low[0:EP, q, 0:w], lowb[:], onehot[:, q * 512:q * 512 + w], start=True, stop=True)
                        for q, w in BANKS:
                            last = pe.matmul(p_all[0:EP, q, 0:w], onesb[:], onehot[:, q * 512:q * 512 + w],
                                             start=True, stop=True)
                        last.then_inc(sums, 1)

                @block.vector
                def _(dve):
                    n = dve.value_load(ctl[0:1, C_RANKS:C_RANKS + 1], min_val=1, max_val=EC)
                    v = Steps(dve, step2)
                    v.mark(dve.memset(kgen[:], 0.0))
                    v.link(dve.memset(seen[:], 0.0))
                    PER = 7
                    with dve.Fori(0, n) as c:
                        w = Steps(dve, step2, c * PER + v.n)
                        w.wait()
                        w.link(dve.tensor_copy(dcol[:], dstf[:, ds(c, 1)]))
                        w.link(dve.tensor_scalar(onehot[:], nrow[0:EP, :], dcol[:], None, ALU.is_equal))
                        dve.sem_inc(hot_ready, 1)
                        dve.wait_ge(sums, c + 1)
                        w.link(dve.tensor_tensor(ahead[:], seen[:], p_low[0:EP].rearrange("p q f -> p (q f)")[:, 0:NP],
                                                 ALU.add))
                        w.link(dve.tensor_tensor(ahead[:], ahead[:], onehot[:], ALU.mult))
                        w.link(dve.tensor_reduce(kcol[:], ahead[:], X, ALU.add))
                        w.mark(dve.tensor_copy(kgen[:, ds(c, 1)], kcol[:]))
                        w.mark(dve.tensor_tensor(seen[:], seen[:], p_all[0:EP].rearrange("p q f -> p (q f)")[:, 0:NP],
                                                 ALU.add))
                        assert w.n == PER
                    v.base = n * PER
                    v.wait()
                    v.link(dve.tensor_tensor(kgen[:], kgen[:], ksort[:], ALU.subtract))
                    v.link(dve.scalar_tensor_tensor(out=kgen[:], in0=kgen[:], scalar=unsorted[0:EP, :], in1=ksort[:],
                                                    op0=ALU.mult, op1=ALU.add))
                    v.link(dve.tensor_copy(ki[:], kgen[:]))
                    v.link(dve.tensor_scalar(hi[:], ki[:], 2, None, ALU.logical_shift_right))
                    v.link(dve.scalar_tensor_tensor(out=kgen[:], in0=hi[:], scalar=float(NROW), in1=dstf[:],
                                                    op0=ALU.mult, op1=ALU.add))
                    v.link(dve.tensor_copy(hi[:], kgen[:]))
                    v.mark(dve.tensor_scalar(ki[:], ki[:], S - 1, None, ALU.bitwise_and))
                    v.link(dve.tensor_scalar(hi[:], hi[:], 2, None, ALU.logical_shift_left))
                    v.mark(dve.tensor_tensor(slotpos[:], hi[:], ki[:], ALU.bitwise_or))

        fdt = sb("fdt", [P, NT + 1, W], F32)
        acc = sb("acc", [P, NT + 1, D], F32)
        den = sb("den", [P, NT + 1, HEADS], F32)
        cntge = sb("cntge", [P, NT + 1, S * (RELS + 1)], F32)
        hr_d = dram("hr_d", (NP, D), F32)
        y_d = dram("y_d", ((RT + 1) * P, D), F32)
        HB = [(0, 0, HALF), (1, HALF, D)]

        def halves(psum, rows=P):
            return psum[0:rows, :, 0:HALF]

        def split(ap):
            return ap.rearrange("p (a b) -> p a b", a=2)

        def pe_transpose(pe, dst, src, rows):
            for c in range(KC):
                last = pe.transpose(dst[:, c // 3, (c % 3) * P:(c % 3) * P + rows], src[0:rows, c * P:(c + 1) * P],
                                    ident[0:rows, 0:rows])
            return last

        def pe_product(pe, dst, rows_t, w, rows):
            for q, lo, up in HB:
                for c in range(KC):
                    last = pe.matmul(dst[0:rows, q, 0:HALF], rows_t[:, c * P:c * P + rows], w[:, c, lo:up],
                                     start=c == 0, stop=c == KC - 1)
            return last

        def row_stats(dve, v, row, stats, mv, rows):
            for q, lo, up in HB:
                v.mark(dve.bn_stats(stats[0:rows, q, :], row[0:rows, lo:up]))
            v.wait()
            v.tick()
            v.link(dve.bn_aggr(mv[0:rows, 0:2], stats[0:rows].rearrange("p a b -> p (a b)")))
            v.link(dve.tensor_scalar(mv[0:rows, 1:2], mv[0:rows, 1:2], EPS, None, ALU.add))

        def row_affine(dve, v, mv, rows):
            v.link(dve.reciprocal(mv[0:rows, 2:3], mv[0:rows, 2:3]))
            v.link(dve.scalar_tensor_tensor(out=mv[0:rows, 3:4], in0=mv[0:rows, 0:1], scalar=-1.0,
                                            in1=mv[0:rows, 2:3], op0=ALU.mult, op1=ALU.mult))

        def linear_part(dve, v, rows_w, attr, lost, heads, rows):
            hd = D // heads
            for h in range(heads):
                v.mark(dve.tensor_tensor_reduce(
                    out=lost[0:rows, h * hd:(h + 1) * hd], in0=rows_w[0:rows, h * hd:(h + 1) * hd],
                    in1=attr[0:rows, h * hd:(h + 1) * hd], scale=0.2, scalar=0.0, op0=ALU.mult, op1=ALU.add,
                    accum_out=rows_w[0:rows, D + h:D + h + 1]))
            v.wait()

        def w_view(w):
            return w.rearrange("(c p) n -> p c n", p=P)

        class Signal:

            def __init__(self, where, name, rate, lead=0, turn=1):
                self.sem, = sems(where, name)
                self.rate, self.lead, self.turn = rate, lead, turn

            def open(self, eng):
                eng.sem_inc(self.sem, self.rate * self.lead)

            def wait(self, eng, i, off, k=None):
                k = self.rate if k is None else k
                eng.wait_ge(self.sem, i * (self.turn * self.rate) + (self.rate * (off + self.lead) + k))

        with stage() as st:
            xt = [sb(f"xt{b}", [P, D], F32, st) for b in range(2)]
            ht = [sb(f"ht{b}", [P, D], F32, st) for b in range(2)]
            hT = [sb(f"hT{b}", [P, D], F32, st) for b in range(2)]
            of = [[sb(f"of{w}{b}", [P, W], F32, st) for b in range(2)] for w in range(2)]
            wt = [sb(f"wt{w}", [P, KC, D], F32, st) for w in range(2)]
            bias = [sb(f"bias{w}", [P, D], F32, st) for w in range(2)]
            attr = sb("attr", [P, D], F32, st)
            lost = sb("lost", [P, D], F32, st)
            stats = sb("stats", [P, 2, 6], F32, st)
            mv = [sb(f"mv{b}", [P, 4], F32, st) for b in range(2)]
            recc = [sb(f"recc{b}", [EP, 8, 2], I32, st) for b in range(2)]
            posc = [sb(f"posc{b}", [EP, 8], I32, st) for b in range(2)]
            pT = pb("pT", [P, 2, 512], F32, st)
            pO = [pb(f"pO{w}", [P, 2, 512], F32, st) for w in range(2)]
            w_in, dve3, dve3b, copied, placed0, placed1, posted = sems(st, "w_in", "dve3", "dve3b", "copied", "placed0", "placed1", "posted")
            x_in = sems(st, "x_in0", "x_in1")
            h_out = sems(st, "h_out0", "h_out1")
            f_out = [sems(st, f"f_out{w}0", f"f_out{w}1") for w in range(2)]
            var_ok = Signal(st, "var_ok", 1, 2, 2)
            root_ok = Signal(st, "root_ok", 1, 2, 2)
            affine_ok = Signal(st, "affine_ok", 1, 2, 2)
            h_ok = Signal(st, "h_ok", 1, 2, 2)
            t_ok = Signal(st, "t_ok", 1, 2, 2)
            hT_ok = Signal(st, "hT_ok", 1, 2, 2)
            prod_ok = Signal(st, "prod_ok", 2, 2, 2)
            evac_ok = Signal(st, "evac_ok", 2, 2, 2)
            tiles = [(4, 0, P), (4, 1, LAST)]

            def x_rows(a, i, b, rows):
                if isinstance(i, int):
                    n = 2 * i + b
                    return a[n * P:n * P + rows, :]
                return a[ds(i * (2 * P) + b * P, P), :]

            with nc.Block() as block:
                @block.sync
                def _(sp):
                    def load(i, b, rows):
                        h_ok.wait(sp, i, b - 2)
                        sp.dma_start(xt[b][0:rows], x_rows(io["x"], i, b, rows)).then_inc(x_in[b], 16)

                    def store(i, b, rows):
                        h_ok.wait(sp, i, b)
                        sp.dma_start(x_rows(h0_d, i, b, rows), ht[b][0:rows]).then_inc(h_out[b], 16)
                        for w, d in enumerate((fs_d, fd_d)):
                            evac_ok.wait(sp, i, b, w + 1)
                            sp.dma_start(x_rows(d, i, b, rows), of[w][b][0:rows]).then_inc(f_out[w][b], 16)

                    load(0, 0, P)
                    for w, (wn, bn) in enumerate((("L0_gnn_W1s", "L0_gnn_b1s"), ("L0_gnn_W1d", "L0_gnn_b1d"))):
                        sp.dma_start(wt[w][:], w_view(io[wn])).then_inc(w_in, 16)
                        sp.dma_start(bias[w][:], io[bn].partition_broadcast(P)).then_inc(w_in, 16)
                    sp.dma_start(attr[:], io["L0_gnn_attn1"].rearrange("h d -> (h d)").partition_broadcast(P))\
                      .then_inc(w_in, 16)
                    with sp.Fori(0, 4) as i:
                        load(i, 1, P)
                        store(i, 0, P)
                        load(i + 1, 0, P)
                        store(i, 1, P)
                    load(4, 1, LAST)
                    store(4, 0, P)
                    store(4, 1, LAST)
                    for s in h_out + f_out[0] + f_out[1]:
                        sp.wait_ge(s, 16 * 5)

                @block.gpsimd
                def _(pool):
                    slots = slots_d
                    with pool.Fori(0, EC // 16) as i:
                        for b, placed in enumerate((placed0, placed1)):
                            pool.wait_ge(placed, i * 128)
                            pool.tensor_copy(posc[b][:], slotpos[:, ds(i * 16 + b * 8, 8)]).then_inc(copied, 1)
                            pool.tensor_copy(recc[b][:], recs[:, ds(i * 16 + b * 8, 8), :]).then_inc(copied, 1)
                            pool.wait_ge(copied, i * 4 + (b * 2 + 2))
                            pool.sem_inc(posted, 1)
                            for j in range(8):
                                pool.indirect_dma_start(slots, bass.IndirectOffsetOnAxis(ap=posc[b][:, j:j + 1], axis=0),
                                                        recc[b][:, j, :], None).then_inc(placed, 16)
                    for placed in (placed0, placed1):
                        pool.wait_ge(placed, EC // 16 * 128)

                @block.scalar
                def _(act):
                    for s in (root_ok, h_ok, hT_ok):
                        s.open(act)

                    def norm(i, b, rows):
                        var_ok.wait(act, i, b)
                        act.activation(mv[b][0:rows, 2:3], mv[b][0:rows, 1:2], ACT.Sqrt).then_inc(root_ok.sem, 1)
                        affine_ok.wait(act, i, b)
                        t_ok.wait(act, i, b - 2)
                        act.wait_ge(h_out[b], 16 * i)
                        act.activation(ht[b][0:rows], xt[b][0:rows], ACT.Relu, bias=mv[b][0:rows, 3:4],
                                       scale=mv[b][0:rows, 2:3]).then_inc(h_ok.sem, 1)

                    def copy(i, b, rows):
                        t_ok.wait(act, i, b)
                        prod_ok.wait(act, i, b - 2)
                        v = hT[b][:].rearrange("p (a c n) -> p a c n", a=2, n=P)[:, :, :, 0:rows]
                        act.activation(v, halves(pT).rearrange("p a (c n) -> p a c n", n=P)[:, :, :, 0:rows],
                                       ACT.Copy).then_inc(hT_ok.sem, 1)

                    norm(0, 0, P)
                    copy(0, 0, P)
                    with act.Fori(0, 4) as i:
                        norm(i, 1, P)
                        copy(i, 1, P)
                        norm(i + 1, 0, P)
                        copy(i + 1, 0, P)
                    norm(4, 1, LAST)
                    copy(4, 1, LAST)

                @block.tensor
                def _(pe):
                    for s in (t_ok, prod_ok):
                        s.open(pe)

                    def turn(i, b, rows):
                        h_ok.wait(pe, i, b)
                        hT_ok.wait(pe, i, b - 1)
                        pe_transpose(pe, pT, ht[b], rows).then_inc(t_ok.sem, 1)

                    def product(i, b, rows):
                        hT_ok.wait(pe, i, b)
                        for w in range(2):
                            evac_ok.wait(pe, i, b - 1, w + 1)
                            pe_product(pe, pO[w], hT[b], wt[w], rows).then_inc(prod_ok.sem, 1)

                    turn(0, 0, P)
                    pe.wait_ge(w_in, 80)
                    with pe.Fori(0, 4) as i:
                        product(i, 0, P)
                        turn(i, 1, P)
                        product(i, 1, P)
                        turn(i + 1, 0, P)
                    product(4, 0, P)
                    turn(4, 1, LAST)
                    product(4, 1, LAST)

                @block.vector
                def _(dve):
                    for s in (var_ok, affine_ok, evac_ok):
                        s.open(dve)
                    PER = 7
                    PER_EVAC = 1 + HEADS

                    def norm(i, b, rows):
                        v = Steps(dve, dve3, i * (2 * PER) + b * PER)
                        v.wait()
                        dve.wait_ge(x_in[b], 16 * i + 16)
                        h_ok.wait(dve, i, b - 2)
                        row_stats(dve, v, xt[b], stats, mv[b], rows)
                        dve.sem_inc(var_ok.sem, 1)
                        root_ok.wait(dve, i, b)
                        row_affine(dve, v, mv[b], rows)
                        dve.sem_inc(affine_ok.sem, 1)
                        assert v.n == PER

                    def evacuate(i, b, rows):
                        v = Steps(dve, dve3b, i * (4 * PER_EVAC) + b * (2 * PER_EVAC))
                        for w in range(2):
                            prod_ok.wait(dve, i, b, w + 1)
                            dve.wait_ge(f_out[w][b], 16 * i)
                            v.wait()
                            v.link(dve.tensor_tensor(split(of[w][b][0:rows, 0:D]), halves(pO[w], rows),
                                                     split(bias[w][0:rows]), ALU.add))
                            linear_part(dve, v, of[w][b], attr, lost, HEADS, rows)
                            dve.sem_inc(evac_ok.sem, 1)

                    norm(0, 0, P)
                    dve.wait_ge(w_in, 80)
                    with dve.Fori(0, 4) as i:
                        norm(i, 1, P)
                        evacuate(i, 0, P)
                        norm(i + 1, 0, P)
                        evacuate(i, 1, P)
                    norm(4, 1, LAST)
                    evacuate(4, 0, P)
                    evacuate(4, 1, LAST)

        def sum_tiles(eng, tile_from, count, i):
            tiles = []
            for lo in range(0, count, PACK):
                packed = eng.value_load(tile_of_group[0:1, ds(i * U + (tile_from + TBACK + lo), 1)], min_val=0,
                                        max_val=(1 << 4 * PACK) - 1)
                for k in range(min(PACK, count - lo)):
                    tiles.append(eng.snap((packed >> (4 * k)) & 15).with_bounds(min_val=0, max_val=NT))
            return tiles

        def tiles_of(eng):
            return eng.value_load(ctl[0:1, C_REL + RELS - 1:C_REL + RELS], min_val=1, max_val=RT)

        def slot_buffers(st, width):
            b = {}
            b["rec"] = [sb(f"rec{u}", [P, S * 2], I32, st) for u in range(U)]
            b["row"] = [sb(f"row{u}", [P, S, width], F32, st) for u in range(U)]
            b["val"] = [sb(f"val{u}", [P, S], F32, st) for u in range(U)]
            b["neg"] = [sb(f"neg{u}", [P, S], F32, st) for u in range(U)]
            b["index"] = [sb(f"index{u}", [P, 1], I32, st) for u in range(U)]
            b["next"] = sb("next", [P, NT + 1], I32, st)
            b["left"] = sb("left", [P, NT + 1], F32, st)
            b["step"] = sb("step", [P, 1], I32, st)
            b["slot"] = sb("slot", [P, S], F32, st)
            b["fours"] = sb("fours", [P, 1], F32, st)
            b["over"] = sb("over", [P, S], F32, st)
            b["rec_in"] = sems(st, *[f"rec_in{u}" for u in range(U)])
            b["row_in"] = sems(st, *[f"row_in{u}" for u in range(U)])
            b["pool_step"], = sems(st, "pool_step")
            b["pool_pre"], = sems(st, "pool_pre")
            b["slot_ok"], = sems(st, "slot_ok")
            b["valid"] = Signal(st, "valid", 1, U, U)
            return b

        def gather_edges(pool, b, table, field, used, masks=True, count_relations=False, keep_places=False):
            b["valid"].open(pool)
            pre = Steps(pool, b["pool_pre"])
            pre.mark(pool.tensor_copy(b["next"][:], perm[:]))
            if masks:
                pre.mark(pool.tensor_copy(b["left"][:], degr[:]))
            pre.mark(pool.memset(b["step"][:], NROW))
            pre.mark(pool.iota(b["slot"][:], [[1, S]], base=0, channel_multiplier=0, allow_small_or_imprecise_dtypes=True))
            pre.mark(pool.memset(b["fours"][:], float(S)))
            if count_relations:
                pre.mark(pool.tensor_scalar(b["lessone"][:], relbase[:], -1.0, None, ALU.add))
                pre.mark(pool.memset(cntge[:], 0.0))
            pre.wait()
            PER = 2 + 4 * masks + 4 * count_relations + keep_places
            pool.sem_inc(b["slot_ok"], 1)
            table_rows = slots_d.rearrange("(r s) c -> r (s c)", s=S)

            def record(v, u, t):
                v.mark(pool.tensor_copy(b["index"][u][:], b["next"][:, ds(t, 1)]))
                v.wait()
                v.mark(pool.tensor_tensor(b["next"][:, ds(t, 1)], b["next"][:, ds(t, 1)], b["step"][:], ALU.add))
                pool.indirect_dma_start(b["rec"][u][:], None, table_rows,
                                        bass.IndirectOffsetOnAxis(ap=b["index"][u][:], axis=0)).then_inc(b["rec_in"][u], 16)

            def rows(u):
                for j in range(S):
                    pool.indirect_dma_start(b["row"][u][:, j, :], None, table, bass.IndirectOffsetOnAxis(
                        ap=b["rec"][u][:, 2 * j + field:2 * j + field + 1], axis=0)).then_inc(b["row_in"][u], 16)

            ahead = sum_tiles(pool, 0, U - 1, 0)
            for u in range(U - 1):
                record(pre, u, ahead[u])
                pre.wait()
            for u in range(ROWS_AHEAD):
                pool.wait_ge(b["rec_in"][u], 16)
                rows(u)
            turns = pool.value_load(ctl[0:1, C_TURNS:C_TURNS + 1], min_val=1, max_val=MAX_TURNS)
            with pool.Fori(0, turns) as i:
                t = sum_tiles(pool, 0, 2 * U - 1, i)
                v = Steps(pool, b["pool_step"], i * (PER * U), b["posted"])
                for u in range(U):
                    v.wait()
                    if masks or keep_places:
                        used.wait(pool, i, u - U)
                        pool.sem_inc(b["posted"], 1)
                    if masks:
                        left = b["left"][:, ds(t[u], 1)]
                        v.link(pool.tensor_tensor(b["over"][:], left.to_broadcast([P, S]), b["slot"][:], ALU.subtract))
                        v.mark(pool.tensor_tensor(left, left, b["fours"][:], ALU.subtract))
                        v.link(pool.tensor_scalar(b["val"][u][:], b["over"][:], 0.0, 1.0, ALU.max, ALU.min))
                        v.mark(pool.tensor_scalar(b["neg"][u][:], b["val"][u][:], -1.0, BIG, ALU.add, ALU.mult))
                    if keep_places:
                        pool.wait_ge(b["rec_in"][u], i * 16 + 16)
                        pool.sem_inc(b["posted"], 1)
                        v.mark(pool.tensor_copy(b["places"][u][:], b["rec"][u][:].rearrange("p (s c) -> p s c", c=2)[:, :, 1]))
                    if count_relations:
                        pool.wait_ge(b["rec_in"][u], i * 16 + 16)
                        pool.sem_inc(b["posted"], 1)
                        place_of = b["rec"][u][:].rearrange("p (s c) -> p s c", c=2)[:, :, 1]
                        shape = [P, S, RELS + 1]
                        v.link(pool.tensor_copy(b["place"][:], place_of))
                        v.link(pool.tensor_tensor(b["ge"][:], over(b["place"][:], 2, shape), over(b["lessone"][:], 1, shape),
                                                  ALU.subtract))
                        v.link(pool.tensor_scalar(b["ge"][:], b["ge"][:], 0.0, 1.0, ALU.max, ALU.min))
                        into = cntge[:, ds(t[u], 1), :].rearrange("p o f -> p (o f)")
                        v.mark(pool.tensor_tensor(into, into, b["ge"][:].rearrange("p s r -> p (s r)"), ALU.add))
                    if masks or keep_places:
                        v.wait()
                        pool.sem_inc(b["valid"].sem, 1)
                    w = (u + U - 1) % U
                    rows_wait(pool, b, i, u - 1)
                    pool.sem_inc(b["posted"], 1)
                    record(v, w, t[u + U - 1])
                    w = u + ROWS_AHEAD
                    pool.wait_ge(b["rec_in"][w % U], i * 16 + 16 * (w // U + 1))
                    used.wait(pool, i, w - U)
                    pool.sem_inc(b["posted"], 1)
                    rows(w % U)
                    assert v.n == PER * (u + 1), (v.n, PER)
            for u in range(U):
                pool.wait_ge(b["rec_in"][u], turns * 16 + (16 if u < U - 1 else 0))
                pool.wait_ge(b["row_in"][u], turns * (16 * S) + (16 * S if u < ROWS_AHEAD else 0))
            pool.sem_inc(b["posted"], 1)

        def rows_wait(eng, b, i, off):
            eng.wait_ge(b["row_in"][off % U], i * (16 * S) + 16 * S * (off // U + 1))

        def attention(name, heads, attn, fd_table):
            HD = D // heads
            BY_DVE = 1 if heads > 1 else 0
            with stage() as st:
                b = slot_buffers(st, W)
                b["ge"] = sb("ge", [P, S, RELS + 1], F32, st)
                b["place"] = sb("place_f", [P, S], F32, st)
                b["lessone"] = sb("lessone", [P, RELS + 1], F32, st)
                b["posted"], = sems(st, "rows_posted")
                sj = sb("sj", [P, S, D], F32, st)
                lin = [sb(f"lin{u}", [P, S, heads], F32, st) for u in range(U)]
                scaled = sb("scaled", [P, D], F32, st)
                attr = sb("attr", [P, D], F32, st)
                top = sb("top", [P, NT + 1, heads], F32, st)
                ex = [sb(f"ex{u}", [P, S + 1, heads], F32, st) for u in range(U)]
                pe_ = [sb(f"pe{u}", [P, S + 1, heads], F32, st) for u in range(U)]
                lg = sb("lg", [P, S, heads], F32, st)
                mj = sb("mj", [P, heads], F32, st)
                mnew = sb("mnew", [P, heads], F32, st)
                dsum = sb("dsum", [P, heads], F32, st)
                dots = [sb(f"dots{u}", [P, S, heads], F32, st) for u in range(U)]
                pA = pb("pA", [P, 2, 512], F32, st)
                pS = [pb(f"pS{j}", [P, 2, 512], F32, st) for j in range(S // 2)]
                nothing = sb("nothing", [P, D], F32, st)
                att_in, dve_step, init_ok, fd_in, zeroed, y_zero, sp_posted = sems(
                    st, "att_in", "dve_step", "init_ok", "fd_in", "zeroed", "y_zero", "sp_posted")
                sum_ok = Signal(st, "sum_ok", S // 2, U, U)
                sum_pe = Signal(st, "sum_pe", S // 2, U, U)
                leaky = Signal(st, "leaky", S, U, U)
                logits = Signal(st, "logits", S - BY_DVE, U, U)
                ex_in = Signal(st, "ex_in", 1, U, U)
                ex_ok = Signal(st, "ex_ok", 1, U, U)
                weighted = Signal(st, "weighted", S, U, U)
                summed = Signal(st, "summed", S, U, U)
                scaled_ok = Signal(st, "scaled_ok", 1, U, U)
                added = Signal(st, "added", 1, U, U)
                lin_ok = Signal(st, "lin_ok", 1, U, U)
                top_ok = Signal(st, "top_ok", 1, U, U)
                den_ok = Signal(st, "den_ok", 1, U, U)
                row = b["row"]

                def fdt_row(tile):
                    return fdt[:, tile, :] if isinstance(tile, int) else fdt[:, ds(tile, 1), :].rearrange("p o f -> p (o f)")

                with nc.Block() as block:
                    @block.sync
                    def _(sp):
                        sp.dma_start(attr[:], attn.rearrange("h d -> (h d)").partition_broadcast(P)).then_inc(att_in, 16)
                        sp.wait_ge(att_in, 16)
                        if fd_table is None:
                            sp.wait_ge(zeroed, 1)
                            tiles = tiles_of(sp)
                            behind = sp.value_load(ctl[0:1, C_BEHIND:C_BEHIND + 1], min_val=1, max_val=RT)
                            with sp.Fori(0, behind) as n:
                                sp.wait_ge(y_zero, n * 16)
                                sp.dma_start(y_d[ds(((tiles + n) * P).with_bounds(min_val=0, max_val=RT * P), P), :],
                                             nothing[:]).then_inc(y_zero, 16)
                            sp.wait_ge(y_zero, behind * 16)
                            sp.sem_inc(sp_posted, 1)

                    @block.gpsimd
                    def _(pool):
                        if fd_table is not None:
                            for t in range(NT):
                                pool.indirect_dma_start(fdt[:, t, :], None, fd_table, bass.IndirectOffsetOnAxis(
                                    ap=permc[:, t:t + 1], axis=0)).then_inc(fd_in, 16)
                            pool.wait_ge(fd_in, 16 * NT)
                        pool.sem_inc(init_ok, 1)
                        gather_edges(pool, b, fs_d[0:N], 0, summed, count_relations=fd_table is not None)

                    @block.scalar
                    def _(act):
                        for s in (ex_ok, scaled_ok) + ((logits,) if heads > 1 else ()):
                            s.open(act)

                        def sums(i, off):
                            for j in range(BY_DVE, S if heads > 1 else 0):
                                leaky.wait(act, i, off, j + 1)
                                if j == BY_DVE:
                                    ex_ok.wait(act, i, off - U)
                                for h in range(heads):
                                    of_head = sj[:, j, h * HD:(h + 1) * HD]
                                    last = act.activation(of_head, of_head, ACT.Copy,
                                                          accum_out=dots[off % U][:, j, h:h + 1])
                                last.then_inc(logits.sem, 1)

                        sums(0, 0)
                        turns = act.value_load(ctl[0:1, C_TURNS:C_TURNS + 1], min_val=1, max_val=MAX_TURNS)
                        with act.Fori(0, turns) as i:
                            t = sum_tiles(act, 0, U, i)
                            for u in range(U):
                                ex_in.wait(act, i, u)
                                act.activation(pe_[u][:], ex[u][:], ACT.Exp).then_inc(ex_ok.sem, 1)
                                sums(i, u + 1)
                                ex_ok.wait(act, i, u)
                                added.wait(act, i, u - 1)
                                old = acc[:, ds(t[u], 1), :].rearrange("p o f -> p (o f)")
                                for h in range(heads):
                                    last = act.activation(scaled[:, h * HD:(h + 1) * HD], old[:, h * HD:(h + 1) * HD],
                                                          ACT.Copy, scale=pe_[u][:, 0, h:h + 1])
                                last.then_inc(scaled_ok.sem, 1)

                    @block.tensor
                    def _(pe):
                        summed.open(pe)
                        sum_pe.open(pe)
                        pe.wait_ge(init_ok, 2)

                        def add(i, off, tile):
                            rows_wait(pe, b, i, off)
                            for j in range(S // 2):
                                (leaky if heads > 1 else logits).wait(pe, i, off - 1, S // 2 + j + 1)
                                for q, lo, up in HB:
                                    pe.matmul(pS[j][:, q, 0:HALF], ident[:], row[off % U][:, S // 2 + j, lo:up],
                                              start=True, stop=False)
                                    last = pe.matmul(pS[j][:, q, 0:HALF], ident[:], fdt_row(tile)[:, lo:up],
                                                     start=False, stop=True)
                                last.then_inc(sum_pe.sem, 1)

                        add(0, 0, 0)
                        second, = sum_tiles(pe, 1, 1, 0)
                        add(0, 1, second)
                        turns = pe.value_load(ctl[0:1, C_TURNS:C_TURNS + 1], min_val=1, max_val=MAX_TURNS)
                        with pe.Fori(0, turns) as i:
                            t = sum_tiles(pe, 2, U, i)
                            for u in range(U):
                                add(i, u + 2, t[u])
                                added.wait(pe, i, u - 1)
                                for j in range(S):
                                    weighted.wait(pe, i, u, j + 1)
                                    for q, lo, up in HB:
                                        last = pe.matmul(pA[:, q, 0:HALF], ident[:], row[u][:, j, lo:up],
                                                         start=j == 0, stop=j == S - 1)
                                    last.then_inc(summed.sem, 1)

                    @block.vector
                    def _(dve):
                        for s in (sum_ok, leaky, ex_in, weighted, top_ok, den_ok, lin_ok) + ((logits,) if heads == 1 else ()):
                            s.open(dve)
                        dve.sem_inc(added.sem, U - 1)
                        PER = 9
                        v = Steps(dve, dve_step)
                        dve.memset(nothing[:], 0.0).then_inc(zeroed, 1)
                        v.mark(dve.memset(acc[:], 0.0))
                        v.mark(dve.memset(den[:], 0.0))
                        v.mark(dve.memset(fdt[:, NT, :], 0.0))
                        v.mark(dve.memset(top[:], -BIG))
                        v.mark(dve.memset(scaled[:], 0.0))
                        dve.wait_ge(att_in, 16)
                        v.mark(dve.tensor_scalar(attr[:], attr[:], 0.8, None, ALU.mult))
                        v.link(dve.memset(pA[:], 0.0))
                        FIRST = v.n
                        dve.sem_inc(init_ok, 1)
                        dve.wait_ge(init_ok, 2)

                        def add(i, off, tile):
                            rows_wait(dve, b, i, off)
                            lin_ok.wait(dve, i, off - 1)
                            fd = fdt_row(tile)

                            for j in range(S // 2):
                                if j < BY_DVE:
                                    leaky.wait(dve, i, off - 1, j + 1)
                                else:
                                    logits.wait(dve, i, off - 1, j + 1 - BY_DVE)
                                dve.tensor_tensor(sj[:, j, 0:D], row[off % U][:, j, 0:D], fd[:, 0:D],
                                                  ALU.add).then_inc(sum_ok.sem, 1)
                            dve.tensor_tensor(lin[off % U][:], row[off % U][:, :, D:D + heads],
                                              over(fd[:, D:D + heads], 1, [P, S, heads]), ALU.add).then_inc(lin_ok.sem, 1)
                            for j in range(S):
                                if j < S // 2:
                                    sum_ok.wait(dve, i, off, j + 1)
                                    ins = dict(out=sj[:, j, :], in0=sj[:, j, :], in1=attr[:])
                                else:
                                    sum_pe.wait(dve, i, off, j - S // 2 + 1)
                                    logits.wait(dve, i, off - 1, j + 1 - BY_DVE)
                                    ins = dict(out=split(sj[:, j, :]), in0=halves(pS[j - S // 2]), in1=split(attr[:]))
                                if j < BY_DVE:
                                    for h in range(heads):
                                        of_head = sj[:, j, h * HD:(h + 1) * HD]
                                        last = dve.scalar_tensor_tensor(
                                            out=of_head, in0=of_head, scalar=0.0, in1=attr[:, h * HD:(h + 1) * HD],
                                            op0=ALU.max, op1=ALU.mult, accum_out=dots[off % U][:, j, h:h + 1])
                                    last.then_inc(leaky.sem, 1)
                                elif heads > 1:
                                    dve.scalar_tensor_tensor(scalar=0.0, op0=ALU.max, op1=ALU.mult, **ins)\
                                       .then_inc(leaky.sem, 1)
                                else:
                                    dve.scalar_tensor_tensor(scalar=0.0, op0=ALU.max, op1=ALU.mult, **ins,
                                                             accum_out=dots[off % U][:, j, 0:1]).then_inc(logits.sem, 1)

                        def finish(i, off, tile):
                            summed.wait(dve, i, off)
                            scaled_ok.wait(dve, i, off)
                            dve.tensor_tensor(split(acc[:, ds(tile, 1), :].rearrange("p o f -> p (o f)")), halves(pA),
                                              split(scaled[:]), ALU.add).then_inc(added.sem, 1)

                        def arguments(v, i, u, tile):
                            sh = [P, S, heads]
                            logits.wait(dve, i, u)
                            if BY_DVE:
                                leaky.wait(dve, i, u, BY_DVE)
                            lin_ok.wait(dve, i, u)
                            b["valid"].wait(dve, i, u)
                            v.link(dve.tensor_tensor(lg[:], dots[u][:],
                                                     over(b["neg"][u][:], 2, sh), ALU.add))
                            v.link(dve.tensor_tensor(lg[:], lg[:], lin[u][:], ALU.add))
                            v.link(dve.tensor_reduce(mj[:], lg[:].rearrange("p s h -> p h s"), X, ALU.max))
                            old = top[:, ds(tile, 1), :].rearrange("p o h -> p (o h)")
                            v.link(dve.tensor_tensor(mnew[:], old, mj[:], ALU.max))
                            v.mark(dve.tensor_tensor(ex[u][:, 0, :], old, mnew[:], ALU.subtract))
                            v.mark(dve.tensor_tensor(ex[u][:, 1:S + 1, :], lg[:], over(mnew[:], 1, sh), ALU.subtract))
                            v.wait()
                            dve.sem_inc(ex_in.sem, 1)
                            dve.tensor_copy(old, mnew[:]).then_inc(top_ok.sem, 1)

                        def weigh(v, i, u, tile):
                            sh = [P, S, heads]
                            ex_ok.wait(dve, i, u)
                            v.link(dve.tensor_tensor(pe_[u][:, 1:S + 1, :], pe_[u][:, 1:S + 1, :],
                                                     over(b["val"][u][:], 2, sh), ALU.mult))
                            for j in range(S):
                                if heads == 1:
                                    ins = dve.tensor_scalar(row[u][:, j, 0:D], row[u][:, j, 0:D], pe_[u][:, 1 + j, :], None,
                                                            ALU.mult)
                                else:
                                    of_heads = row[u][:, j, 0:D].rearrange("p (h d) -> p h d", h=heads)
                                    ins = dve.tensor_tensor(of_heads, of_heads,
                                                            over(pe_[u][:, 1 + j, :], 2, [P, heads, HD]), ALU.mult)
                                ins\
                                   .then_inc(weighted.sem, 1)
                            v.mark(dve.tensor_reduce(dsum[:], pe_[u][:, 1:S + 1, :].rearrange("p s h -> p h s"), X, ALU.add))
                            d = den[:, ds(tile, 1), 0:heads].rearrange("p o h -> p (o h)")
                            v.mark(dve.tensor_tensor(d, d, pe_[u][:, 0, :], ALU.mult))
                            v.wait()
                            dve.tensor_tensor(d, d, dsum[:], ALU.add).then_inc(den_ok.sem, 1)
                            assert v.n % PER == 0, v.n

                        add(0, 0, 0)
                        turns = dve.value_load(ctl[0:1, C_TURNS:C_TURNS + 1], min_val=1, max_val=MAX_TURNS)
                        with dve.Fori(0, turns) as i:
                            t = sum_tiles(dve, -1, U + 2, i)
                            v = Steps(dve, dve_step, i * (PER * U) + FIRST)
                            for u in range(U):
                                top_ok.wait(dve, i, u - 1)
                                arguments(v, i, u, t[u + 1])
                                add(i, u + 1, t[u + 2])
                                finish(i, u - 1, t[u])
                                den_ok.wait(dve, i, u - 1)
                                weigh(v, i, u, t[u + 1])
                        last, = sum_tiles(dve, -1, 1, turns)
                        finish(turns, -1, last)

        attention("first", HEADS, io["L0_gnn_attn1"], fd_d[0:N])

        rcnt = sb("rcnt", [P, NT + 1, RELS], F32)

        def settle(first):
            heads = HEADS if first else 1
            HD = D // heads
            table = h0_d[0:N] if first else io["x"]
            ln = ("L0_gnn_ln1_w", "L0_gnn_ln1_b") if first else ("L0_gnn_lno_w", "L0_gnn_lno_b")
            prods = ([("L0_gnn_Wos", "L0_gnn_bos"), ("L0_gnn_Wod", "L0_gnn_bod")] if first
                     else [("L1_gnn_W_root", "L1_gnn_b_rgcn")])
            NW = len(prods)
            with stage() as st:
                wt = [sb(f"wt{w}", [P, KC, D], F32, st) for w in range(NW)]
                bias = [sb(f"bias{w}", [P, D], F32, st) for w in range(NW)]
                lnw = sb("lnw", [P, D], F32, st)
                lnb = sb("lnb", [P, D], F32, st)
                attr = sb("attr", [P, D], F32, st)
                lost = sb("lost", [P, D], F32, st)
                rden = sb("rden", [P, NT, heads], F32, st)
                csum = sb("csum", [P, NT + 1, RELS + 1], F32, st)
                o = sb("o", [P, D], F32, st)
                low = sb("low", [P, D], F32, st)
                y = sb("y", [P, D], F32, st)
                hg = [sb(f"hg{b}", [P, D], F32, st) for b in range(2)]
                ht = [sb(f"ht{b}", [P, D], F32, st) for b in range(2)]
                hT = [sb(f"hT{b}", [P, D], F32, st) for b in range(2)]
                of = [sb(f"of{b}", [P, W], F32, st) for b in range(2)]
                stats = sb("stats", [P, 2, 6], F32, st)
                mv = sb("mv", [P, 4], F32, st)
                gindex = [sb(f"gindex{b}", [P, 1], I32, st) for b in range(2)]
                sindex = [sb(f"sindex{b}", [P, 1], I32, st) for b in range(2)]
                recc = [sb(f"recc{b}", [EP, 8, 2], I32, st) for b in range(2)]
                pT = pb("pT", [P, 2, 512], F32, st)
                pO = [pb(f"pO{w}", [P, 2, 512], F32, st) for w in range(NW)]
                w_in, v_in, dve4, dve4b, copied, posted, pre_ok = sems(st, "w_in", "v_in", "dve4", "dve4b", "copied", "posted", "pre_ok")
                hg_in = sems(st, "hg_in0", "hg_in1")
                placed = sems(st, "placed0", "placed1")
                f_out = sems(st, "f_out0", "f_out1")
                low_ok = Signal(st, "low_ok", 1, 2, 2)
                exp_ok = Signal(st, "exp_ok", 1, 2, 2)
                y_ok = Signal(st, "y_ok", 1, 2, 2)
                NV = 1 if first else 2
                var_ok = Signal(st, "var_ok", NV, 2, 2)
                root_ok = Signal(st, "root_ok", NV, 2, 2)
                affine_ok = Signal(st, "affine_ok", 1, 2, 2)
                h_ok = Signal(st, "h_ok", 1, 2, 2)
                t_ok = Signal(st, "t_ok", 1, 2, 2)
                hT_ok = Signal(st, "hT_ok", 1, 2, 2)
                prod_ok = Signal(st, "prod_ok", NW, 2, 2)
                evac_ok = Signal(st, "evac_ok", NW, 2, 2)
                kept_ok = Signal(st, "kept_ok", 1, 2, 2)

                def of_tile(ap, i, b):
                    if isinstance(i, int):
                        return ap[:, 2 * i + b]
                    x = ap[:, ds(i * 2 + b, 1)]
                    return x.rearrange("p o f -> p (o f)") if len(x.shape) == 3 else x

                def twice(step, eng):
                    step(eng, 0, 0, True)
                    with eng.Fori(0, 4) as i:
                        step(eng, i, 1, True)
                        step(eng, i, 0, False)
                        step(eng, i + 1, 0, True)
                        step(eng, i, 1, False)
                    step(eng, 4, 1, True)
                    step(eng, 4, 0, False)
                    step(eng, 4, 1, False)

                with nc.Block() as block:
                    @block.sync
                    def _(sp):
                        sp.dma_start(lnw[:], io[ln[0]].partition_broadcast(P)).then_inc(v_in, 16)
                        sp.dma_start(lnb[:], io[ln[1]].partition_broadcast(P)).then_inc(v_in, 16)
                        sp.dma_start(attr[:], io["L0_gnn_attno"].rearrange("h d -> (h d)").partition_broadcast(P))\
                          .then_inc(v_in, 16)
                        for w, (wn, bn) in enumerate(prods):
                            sp.dma_start(bias[w][:], io[bn].partition_broadcast(P)).then_inc(v_in, 16)
                        for w, (wn, bn) in enumerate(prods):
                            sp.dma_start(wt[w][:], w_view(io[wn])).then_inc(w_in, 16)
                        sp.wait_ge(v_in, 16 * (NW + 3))
                        sp.wait_ge(w_in, 16 * NW)

                    @block.gpsimd
                    def _(pool):
                        def gather(i, b, c):
                            y_ok.wait(pool, i, b - 2)
                            pool.sem_inc(posted, 1)
                            pool.tensor_copy(gindex[b][:], of_col(permc, i, b)).then_inc(copied, 1)
                            return c

                        def of_col(ap, i, b):
                            return ap[:, ds(i * 2 + b, 1)] if not isinstance(i, int) else ap[:, 2 * i + b:2 * i + b + 1]

                        def fetch(b):
                            pool.indirect_dma_start(hg[b][:], None, table, bass.IndirectOffsetOnAxis(
                                ap=gindex[b][:], axis=0)).then_inc(hg_in[b], 16)

                        pool.tensor_copy(gindex[0][:], permc[:, 0:1]).then_inc(copied, 1)
                        pool.wait_ge(copied, 1)
                        fetch(0)
                        COPIES = 8 if first else 4
                        with pool.Fori(0, NT // 2) as i:
                            for b in range(2):
                                n = COPIES // 2 * b
                                y_ok.wait(pool, i, b - 1)
                                pool.wait_ge(hg_in[1 - b], i * 16 + 16 * b)
                                pool.sem_inc(posted, 1)
                                pool.tensor_copy(gindex[1 - b][:], permc[:, ds(i * 2 + (b + 1), 1)]).then_inc(copied, 1)
                                pool.wait_ge(f_out[b], i * 16)
                                pool.sem_inc(posted, 1)
                                pool.tensor_copy(sindex[b][:], perm[:, ds(i * 2 + b, 1)]).then_inc(copied, 1)
                                pool.wait_ge(copied, i * COPIES + (n + 3))
                                pool.sem_inc(posted, 1)
                                fetch(1 - b)
                                if first:
                                    for q in range(2):
                                        pool.wait_ge(placed[q], i * 256 + b * 128)
                                        pool.sem_inc(posted, 1)
                                        pool.tensor_copy(recc[q][:], recs[:, ds(i * 32 + (b * 16 + q * 8), 8), :])\
                                            .then_inc(copied, 1)
                                        pool.wait_ge(copied, i * COPIES + (n + 4 + q))
                                        pool.sem_inc(posted, 1)
                                        for j in range(8):
                                            pool.indirect_dma_start(byrel_d, bass.IndirectOffsetOnAxis(
                                                ap=recc[q][:, j, 1:2], axis=0), recc[q][:, j, 0:1], None)\
                                                .then_inc(placed[q], 16)
                                if first:
                                    evac_ok.wait(pool, i, b, 1)
                                    pool.sem_inc(posted, 1)
                                    pool.indirect_dma_start(fs_d, bass.IndirectOffsetOnAxis(ap=sindex[b][:], axis=0),
                                                            of[b][:], None).then_inc(f_out[b], 16)
                                else:
                                    h_ok.wait(pool, i, b)
                                    pool.sem_inc(posted, 1)
                                    pool.indirect_dma_start(hr_d, bass.IndirectOffsetOnAxis(ap=sindex[b][:], axis=0),
                                                            ht[b][:], None).then_inc(f_out[b], 16)
                        for b in range(2):
                            pool.wait_ge(f_out[b], 16 * NT // 2)
                            pool.wait_ge(hg_in[b], 16 * NT // 2 + 16 * (1 - b))
                            if first:
                                pool.wait_ge(placed[b], EC // 2 * 16)

                    @block.scalar
                    def _(act):
                        for s in (exp_ok, root_ok, h_ok, hT_ok, kept_ok):
                            if s is not h_ok or not first:
                                s.open(act)

                        def step(act, i, b, ahead):
                            if ahead:
                                low_ok.wait(act, i, b)
                                act.activation(low[:], low[:], ACT.Exp).then_inc(exp_ok.sem, 1)
                                for k in range(NV):
                                    var_ok.wait(act, i, b, k + 1)
                                    act.activation(mv[:, 2:3], mv[:, 1:2], ACT.Sqrt).then_inc(root_ok.sem, 1)
                                if not first:
                                    affine_ok.wait(act, i, b)
                                    act.activation(of_tile(fdt, i, b)[:, 0:D], y[:], ACT.Copy).then_inc(kept_ok.sem, 1)
                                    t_ok.wait(act, i, b - 2)
                                    act.wait_ge(f_out[b], 16 * i)
                                    act.activation(ht[b][:], y[:], ACT.Relu, bias=mv[:, 3:4], scale=mv[:, 2:3])\
                                       .then_inc(h_ok.sem, 1)
                                t_ok.wait(act, i, b)
                                prod_ok.wait(act, i, b - 2)
                                act.activation(split(hT[b][:]), halves(pT), ACT.Copy).then_inc(hT_ok.sem, 1)

                        twice(step, act)

                    @block.tensor
                    def _(pe):
                        for s in (t_ok, prod_ok):
                            s.open(pe)

                        def step(pe, i, b, ahead):
                            if ahead:
                                h_ok.wait(pe, i, b)
                                hT_ok.wait(pe, i, b - 1)
                                pe_transpose(pe, pT, ht[b], P).then_inc(t_ok.sem, 1)
                            else:
                                hT_ok.wait(pe, i, b)
                                for w in range(NW):
                                    evac_ok.wait(pe, i, b - 1, w + 1)
                                    pe_product(pe, pO[w], hT[b], wt[w], P).then_inc(prod_ok.sem, 1)

                        step(pe, 0, 0, True)
                        pe.wait_ge(w_in, 16 * NW)
                        with pe.Fori(0, 4) as i:
                            step(pe, i, 0, False)
                            step(pe, i, 1, True)
                            step(pe, i, 1, False)
                            step(pe, i + 1, 0, True)
                        step(pe, 4, 0, False)
                        step(pe, 4, 1, True)
                        step(pe, 4, 1, False)

                    @block.vector
                    def _(dve):
                        for s in (low_ok, y_ok, var_ok, affine_ok, evac_ok) + ((h_ok,) if first else ()):
                            s.open(dve)
                        dve.wait_ge(v_in, 16 * (NW + 3))
                        pre = Steps(dve, pre_ok)
                        pre.link(dve.tensor_scalar(rden[:], den[:, 0:NT, 0:heads], 1e-30, None, ALU.max))
                        pre.link(dve.reciprocal(rden[:], rden[:]))
                        if first:
                            for b in range(2):
                                pre.link(dve.memset(of[b][:, D:W], 0.0))
                        else:
                            pre.link(dve.tensor_reduce(csum[:], cntge[:].rearrange("p t (s r) -> p t r s", s=S), X, ALU.add))
                            pre.link(dve.tensor_copy(csum[:, :, 0], degr[:]))
                            pre.link(dve.tensor_tensor(rcnt[:], csum[:, :, 0:RELS], csum[:, :, 1:RELS + 1], ALU.subtract))
                            pre.link(dve.tensor_scalar(rcnt[:], rcnt[:], 1.0, None, ALU.max))
                            pre.link(dve.reciprocal(rcnt[:], rcnt[:]))
                        PER = 14 if first else 22

                        def step(dve, i, b, ahead):
                            if ahead:
                                v = Steps(dve, dve4, i * (2 * PER) + b * PER)
                                v.wait()
                                h_ok.wait(dve, i, b - 1)
                                rd = (rden[:, 2 * i + b, :] if isinstance(i, int)
                                      else rden[:, ds(i * 2 + b, 1), :].rearrange("p o h -> p (o h)"))
                                v.link(dve.tensor_tensor(
                                    o[:].rearrange("p (h d) -> p h d", h=heads),
                                    of_tile(acc, i, b)[:, 0:D].rearrange("p (h d) -> p h d", h=heads),
                                    over(rd, 2, [P, heads, HD]), ALU.mult))
                                v.link(dve.tensor_scalar(low[:], o[:], 0.0, None, ALU.min))
                                dve.sem_inc(low_ok.sem, 1)
                                exp_ok.wait(dve, i, b)
                                v.link(dve.scalar_tensor_tensor(out=o[:], in0=o[:], scalar=0.0, in1=low[:],
                                                                op0=ALU.max, op1=ALU.add))
                                dve.wait_ge(hg_in[b], i * 16 + 16)
                                if first:
                                    v.link(dve.scalar_tensor_tensor(out=y[:], in0=o[:], scalar=-1.0, in1=hg[b][:],
                                                                    op0=ALU.add, op1=ALU.add))
                                    dve.sem_inc(y_ok.sem, 1)
                                else:
                                    kept_ok.wait(dve, i, b - 1)
                                    v.link(dve.tensor_scalar(y[:], o[:], -1.0, None, ALU.add))
                                row_stats(dve, v, y, stats, mv, P)
                                dve.sem_inc(var_ok.sem, 1)
                                root_ok.wait(dve, i, b, 1)
                                row_affine(dve, v, mv, P)
                                v.link(dve.tensor_scalar(y[:], y[:], mv[:, 2:3], mv[:, 3:4], ALU.mult, ALU.add))
                                if first:
                                    v.link(dve.tensor_tensor(y[:], y[:], lnw[:], ALU.mult))
                                    t_ok.wait(dve, i, b - 2)
                                    v.mark(dve.tensor_tensor(ht[b][:], y[:], lnb[:], ALU.add))
                                    v.wait()
                                    dve.sem_inc(h_ok.sem, 1)
                                else:
                                    v.link(dve.tensor_tensor(y[:], y[:], lnw[:], ALU.mult))
                                    v.link(dve.tensor_tensor(y[:], y[:], lnb[:], ALU.add))
                                    v.link(dve.tensor_tensor(y[:], y[:], hg[b][:], ALU.add))
                                    dve.sem_inc(y_ok.sem, 1)
                                    row_stats(dve, v, y, stats, mv, P)
                                    dve.sem_inc(var_ok.sem, 1)
                                    root_ok.wait(dve, i, b, 2)
                                    row_affine(dve, v, mv, P)
                                    dve.sem_inc(affine_ok.sem, 1)
                                assert v.n == PER, v.n
                                return
                            if first:
                                v = Steps(dve, dve4b, i * 8 + b * 4)
                                v.wait()
                                prod_ok.wait(dve, i, b, 1)
                                dve.wait_ge(f_out[b], 16 * i)
                                v.link(dve.tensor_tensor(split(of[b][:, 0:D]), halves(pO[0]), split(bias[0][:]), ALU.add))
                                linear_part(dve, v, of[b], attr, lost, 1, P)
                                dve.sem_inc(evac_ok.sem, 1)
                                prod_ok.wait(dve, i, b, 2)
                                row = of_tile(fdt, i, b)
                                v.link(dve.tensor_tensor(split(o2[:]), halves(pO[1]), split(bias[1][:]), ALU.add))
                                v.mark(dve.tensor_tensor_reduce(
                                    out=lost[:], in0=o2[:], in1=attr[:], scale=0.2, scalar=0.0, op0=ALU.mult,
                                    op1=ALU.add, accum_out=lin2[:]))
                                v.wait()
                                dve.sem_inc(evac_ok.sem, 1)
                                kept(dve, row, i, b)
                            else:
                                prod_ok.wait(dve, i, b, 1)
                                dve.tensor_tensor(split(of_tile(acc, i, b)[:, 0:D]), halves(pO[0]), split(bias[0][:]),
                                                  ALU.add).then_inc(evac_ok.sem, 1)

                        if first:
                            o2 = sb("o2", [P, D], F32, st)
                            lin2 = sb("lin2", [P, 1], F32, st)
                            fd_ok = Signal(st, "fd_ok", 2, 2, 2)
                            fd_ok.open(dve)

                            def kept(dve, row, i, b):
                                dve.tensor_copy(row[:, 0:D], o2[:]).then_inc(fd_ok.sem, 1)
                                dve.tensor_copy(row[:, D:D + 1], lin2[:]).then_inc(fd_ok.sem, 1)
                                fd_ok.wait(dve, i, b)

                        twice(step, dve)

        settle(True)
        attention("second", 1, io["L0_gnn_attno"], None)
        settle(False)

        CUT = -4096
        F32R = mybir.dt.float32r
        with stage() as st:
            byrel = [sb(f"byrel{k}", [P, P], I32, st) for k in range(2)]
            byrelf = [sb(f"byrelf{k}", [P, P], F32, st) for k in range(2)]
            source = sb("source", [P, 2 * P], I32, st)
            gindex = sb("gindex", [P, 1], I32, st)
            g = sb("g", [P, D], F32, st)
            cut = cntge[:].rearrange("p t f -> p (t f)")[:, 0:2 * D].rearrange("p (a f) -> p a f", a=2)
            gT = sb("gT", [P, KC, 2, P], F32, st)
            y = nrow
            wh = [sb(f"wh{b}", [P, KC, D], F32, st) for b in range(2)]
            wl = [sb(f"wl{b}", [P, KC, D], F32, st) for b in range(2)]
            RAW = KC - 1
            raw = [sb(f"raw{c}", [P, D], F32, st) for c in range(RAW)]
            pT = pb("pT", [P, 2, 512], F32, st)
            pO = pb("pO", [P, 2, 512], F32, st)
            pI = pb("pI", [P, 512], F32, st)
            byrel_in, byrel_f, byrel_t, source_ok, copied, posted, g_in, all_out, pe_posted, sp_posted = sems(
                st, "byrel_in", "byrel_f", "byrel_t", "source_ok", "copied", "posted", "g_in",
                "all_out", "pe_posted", "sp_posted")
            w_in, = sems(st, "w_in")
            y_out = sems(st, "y_out0", "y_out1")
            rows_first, w_first = sems(st, "rows_first", "w_first")
            t_ok = Signal(st, "t_ok", 1, 1)
            cut_ok = Signal(st, "cut_ok", 1, 1)
            gT_ok = Signal(st, "gT_ok", KC, 1)
            w_ok = Signal(st, "w_ok", KC, 0, 2)
            used = Signal(st, "used", KC, 1)
            prod_ok = Signal(st, "prod_ok", 1, 1)
            evac_ok = Signal(st, "evac_ok", 2, 1)
            MORE = RT - P

            def ends(eng, i, b):
                at = [i * 2 + (C_REL + b + k) for k in (-1, 0)]
                first, end = (ctl[0:1, a:a + 1] if isinstance(a, int) else ctl[0:1, ds(a, 1)] for a in at)
                return (eng.value_load(first, min_val=0, max_val=RT - LEAST),
                        eng.value_load(end, min_val=LEAST, max_val=RT))

            with nc.Block() as block:
                @block.sync
                def _(sp):
                    sp.dma_start(byrel[0][:], byrel_d[0:P * P].rearrange("(t p) o -> t (p o)", p=P)).then_inc(byrel_in, 16)
                    sp.dma_start(byrel[1][0:MORE], byrel_d[P * P:RT * P].rearrange("(t p) o -> t (p o)", p=P))\
                      .then_inc(byrel_in, 16)
                    w_all = io["L1_gnn_W_rel"].rearrange("r (c p) n -> r p c n", p=P)

                    def load(rel):
                        for c in range(KC):
                            if c == KC - 1:
                                sp.wait_ge(w_ok.sem, rel * KC + 1)
                            elif not isinstance(rel, int):
                                sp.wait_ge(w_ok.sem, rel * KC - (KC - c - 1 if c > 0 else 0))
                            if c == KC - 1 or not isinstance(rel, int):
                                sp.sem_inc(sp_posted, 1)
                            if c > 0 or not isinstance(rel, int):
                                sp.wait_ge(w_in, rel * (16 * KC) + 16 * c)
                            src = w_all[rel] if isinstance(rel, int) else w_all[ds(rel, 1)].rearrange("r p c n -> p (r c) n")
                            sp.dma_start(raw[c % RAW][:], src[:, c, :]).then_inc(w_in, 16)

                    load(0)
                    with sp.Fori(1, RELS) as rel:
                        load(rel)
                    sp.wait_ge(w_in, 16 * KC * RELS)

                @block.gpsimd
                def _(pool):
                    def fetch():
                        pool.indirect_dma_start(g[:], None, hr_d, bass.IndirectOffsetOnAxis(ap=gindex[:], axis=0))\
                            .then_inc(g_in, 16)

                    pool.wait_ge(source_ok, 3)
                    pool.tensor_copy(gindex[:], source[:, 0:1]).then_inc(copied, 1)
                    pool.wait_ge(copied, 1)
                    fetch()
                    tiles = tiles_of(pool)
                    with pool.Fori(0, tiles) as n:
                        pool.wait_ge(g_in, n * 16 + 16)
                        pool.sem_inc(posted, 1)
                        pool.tensor_copy(gindex[:], source[:, ds(n + 1, 1)]).then_inc(copied, 1)
                        pool.wait_ge(copied, n + 2)
                        t_ok.wait(pool, n, 0)
                        pool.sem_inc(posted, 1)
                        fetch()
                    pool.wait_ge(g_in, tiles * 16 + 16)
                    pool.sem_inc(posted, 1)

                @block.scalar
                def _(act):
                    for s in (gT_ok, evac_ok):
                        s.open(act)

                    def copy(n, off):
                        cut_ok.wait(act, n, off)
                        for c in range(KC):
                            used.wait(act, n, off - 1, c + 1)
                            act.activation(gT[:, c].bitcast(F32R), cut[:, :, c * P:(c + 1) * P], ACT.Copy).then_inc(gT_ok.sem, 1)

                    copy(0, 0)
                    tiles = tiles_of(act)
                    with act.Fori(0, tiles) as n:
                        for q, lo, up in HB:
                            if q == 1:
                                copy(n, 1)
                            (prod_ok, used)[q].wait(act, n, 0)
                            act.wait_ge(y_out[q], n * 16)
                            act.activation(y[:, lo:up], pO[:, q, 0:HALF], ACT.Copy).then_inc(evac_ok.sem, 1)
                            evac_ok.wait(act, n, 0, q + 1)
                            act.dma_start(y_d[ds(n * P, P), lo:up], y[:, lo:up]).then_inc(y_out[q], 16)
                    for q in range(2):
                        act.wait_ge(y_out[q], tiles * 16)
                    act.sem_inc(all_out, 1)

                @block.tensor
                def _(pe):
                    for s in (t_ok, used, prod_ok):
                        s.open(pe)
                    for k in range(2):
                        rows = P if k == 0 else MORE
                        pe.wait_ge(byrel_f, k + 1)
                        pe.transpose(pI[:, k * P:k * P + rows], byrelf[k][0:rows, :], ident[0:rows, 0:rows])\
                            .then_inc(byrel_t, 1)

                    def turn(n, off):
                        pe.wait_ge(g_in, n * 16 + 16 * (off + 1))
                        cut_ok.wait(pe, n, off - 1)
                        pe_transpose(pe, pT, g, P).then_inc(t_ok.sem, 1)

                    turn(0, 0)
                    with pe.Fori(0, RELS // 2) as i:
                        for b in range(2):
                            first, end = ends(pe, i, b)
                            w_ok.wait(pe, i, b, 1)
                            pe.sem_inc(pe_posted, 1)
                            with pe.Fori(first, end) as n:
                                turn(n, 1)
                                for q, lo, up in HB:
                                    evac_ok.wait(pe, n, -1, q + 1)
                                    for c in range(KC):
                                        if q == 0:
                                            gT_ok.wait(pe, n, 0, c + 1)
                                            w_ok.wait(pe, i, b, c + 1)
                                        for k, (half, w) in enumerate(((0, wh[b]), (0, wl[b]), (1, wh[b]))):
                                            last = pe.matmul(pO[:, q, 0:HALF], gT[:, c, half, :].bitcast(F32R),
                                                             w[:, c, lo:up].bitcast(F32R),
                                                             start=c == 0 and k == 0, stop=c == KC - 1 and k == 2)
                                        if q == 1:
                                            last.then_inc(used.sem, 1)
                                    if q == 0:
                                        last.then_inc(prod_ok.sem, 1)

                @block.vector
                def _(dve):
                    cut_ok.open(dve)
                    dve.wait_ge(byrel_in, 32)
                    dve.memset(source[:, RT:2 * P], 0).then_inc(source_ok, 1)
                    for k in range(2):
                        rows = P if k == 0 else MORE
                        dve.tensor_copy(byrelf[k][0:rows], byrel[k][0:rows]).then_inc(byrel_f, 1)
                    dve.wait_ge(byrel_t, 2)
                    for k in range(2):
                        rows = P if k == 0 else MORE
                        dve.tensor_copy(source[:, k * P:k * P + rows], pI[:, k * P:k * P + rows]).then_inc(source_ok, 1)

                    def cut_rows(n, off):
                        t_ok.wait(dve, n, off)
                        gT_ok.wait(dve, n, off - 1)
                        dve.tensor_scalar(split(cut[:, 0, :].bitcast(I32)), halves(pT).bitcast(I32), CUT, None,
                                          ALU.bitwise_and).then_inc(rows_first, 1)
                        dve.wait_ge(rows_first, n + (off + 1))
                        dve.tensor_tensor(split(cut[:, 1, :]), halves(pT), split(cut[:, 0, :]), ALU.subtract)\
                           .then_inc(cut_ok.sem, 1)

                    def cut_weights(i, off, chunks):
                        b = off % 2
                        for c in chunks:
                            dve.wait_ge(w_in, i * (32 * KC) + 16 * (off * KC + c + 1))
                            dve.tensor_copy(wh[b][:, c, :].bitcast(F32R), raw[c % RAW][:]).then_inc(w_first, 1)
                            dve.wait_ge(w_first, i * (2 * KC) + (off * KC + c + 1))
                            dve.tensor_tensor(wl[b][:, c, :].bitcast(F32R), raw[c % RAW][:], wh[b][:, c, :],
                                              ALU.subtract).then_inc(w_ok.sem, 1)

                    def relation(i, b, more):
                        first, end = ends(dve, i, b)
                        with dve.Fori(first, end - 1) as n:
                            cut_rows(n, 1)
                        if more:
                            cut_weights(i, b + 1, range(KC // 2))
                        cut_rows(end, 0)
                        if more:
                            cut_weights(i, b + 1, range(KC // 2, KC))

                    cut_rows(0, 0)
                    cut_weights(0, 0, range(KC))
                    with dve.Fori(0, RELS // 2 - 1) as i:
                        for b in range(2):
                            relation(i, b, True)
                    relation(RELS // 2 - 1, 0, True)
                    relation(RELS // 2 - 1, 1, False)

        def slot_sum(relations):
            with stage() as st:
                b = slot_buffers(st, D)
                b["places"] = [sb(f"places{u}", [P, S], F32, st) for u in range(U)]
                b["posted"], = sems(st, "rows_posted")
                ge = sb("ge", [P, S, RELS + 1], F32, st)
                of_rel = sb("of_rel", [P, S, RELS], F32, st)
                weight = sb("weight", [P, S], F32, st)
                dve_step, = sems(st, "dve_step")
                used = Signal(st, "used", S, U, U)
                with nc.Block() as block:
                    @block.gpsimd
                    def _(pool):
                        if relations:
                            gather_edges(pool, b, y_d, 1, used, masks=False, keep_places=True)
                        else:
                            gather_edges(pool, b, xs_d, 0, used, masks=False)

                    @block.vector
                    def _(dve):
                        used.open(dve)
                        PER = 7 if relations else 2
                        pre = Steps(dve, dve_step)
                        pre.link(dve.tensor_copy(b["left"][:], degr[:]))
                        dve.wait_ge(b["slot_ok"], 1)
                        turns = dve.value_load(ctl[0:1, C_TURNS:C_TURNS + 1], min_val=1, max_val=MAX_TURNS)
                        with dve.Fori(0, turns) as i:
                            t = sum_tiles(dve, 0, U, i)
                            for u in range(U):
                                v = Steps(dve, dve_step, i * (PER * U) + (u * PER + pre.n))
                                v.wait()
                                used.wait(dve, i, u - 1)
                                w = b["val"][u]
                                left = b["left"][:, ds(t[u], 1)]
                                v.link(dve.tensor_tensor(w[:], left.to_broadcast([P, S]), b["slot"][:], ALU.is_gt))
                                v.mark(dve.tensor_scalar(left, left, -float(S), None, ALU.add))
                                if relations:
                                    b["valid"].wait(dve, i, u)
                                    shape = [P, S, RELS + 1]
                                    v.link(dve.tensor_tensor(ge[:], over(b["places"][u][:], 2, shape),
                                                             over(relbase[:], 1, shape), ALU.is_ge))
                                    v.link(dve.tensor_tensor(of_rel[:], ge[:, :, 0:RELS], ge[:, :, 1:RELS + 1],
                                                             ALU.subtract))
                                    rc = rcnt[:, ds(t[u], 1), :].rearrange("p o r -> p (o r)")
                                    v.link(dve.tensor_tensor(of_rel[:], of_rel[:], over(rc, 1, [P, S, RELS]), ALU.mult))
                                    v.link(dve.tensor_reduce(weight[:], of_rel[:], X, ALU.add))
                                    v.link(dve.tensor_tensor(weight[:], weight[:], w[:], ALU.mult))
                                    w = weight
                                rows_wait(dve, b, i, u)
                                into = acc[:, ds(t[u], 1), 0:D].rearrange("p o f -> p (o f)")
                                for j in range(S):
                                    used.wait(dve, i, u, j)
                                    dve.scalar_tensor_tensor(out=into, in0=b["row"][u][:, j, :], scalar=w[:, j:j + 1], in1=into,
                                                             op0=ALU.mult, op1=ALU.add).then_inc(used.sem, 1)

        slot_sum(True)

        dinv = sb("dinv", [P, NT + 1], F32)
        xs_d = dram("xs_d", (NP, D), F32)
        with stage() as st:
            wg = sb("wg", [P, KC, D], F32, st)
            ht = [sb(f"ht{b}", [P, D], F32, st) for b in range(2)]
            hT = [sb(f"hT{b}", [P, D], F32, st) for b in range(2)]
            of = [sb(f"of{b}", [P, D], F32, st) for b in range(2)]
            pT = pb("pT", [P, 2, 512], F32, st)
            pO = pb("pO", [P, 2, 512], F32, st)
            w_in, deg_ok, root_ok = sems(st, "w_in", "deg_ok", "root_ok")
            f_out = sems(st, "f_out0", "f_out1")
            h_ok, t_ok, hT_ok, prod_ok = (Signal(st, n, 1, 2, 2) for n in ("h_ok", "t_ok", "hT_ok", "prod_ok"))
            evac_ok = Signal(st, "evac_ok", 1, 2, 2)
            kept_ok = Signal(st, "kept_ok", 1, 2, 2)
            with nc.Block() as block:
                @block.sync
                def _(sp):
                    sp.dma_start(wg[:], w_view(io["L1_gnn_W_gcn"])).then_inc(w_in, 16)
                    sp.wait_ge(w_in, 16)

                @block.gpsimd
                def _(pool):
                    for n in range(NT):
                        evac_ok.wait(pool, 0, n)
                        pool.indirect_dma_start(xs_d, bass.IndirectOffsetOnAxis(ap=perm[:, n:n + 1], axis=0),
                                                of[n % 2][:], None).then_inc(f_out[n % 2], 16)
                    for b in range(2):
                        pool.wait_ge(f_out[b], 16 * NT // 2)

                @block.scalar
                def _(act):
                    for s in (h_ok, hT_ok):
                        s.open(act)
                    act.wait_ge(deg_ok, 1)
                    act.activation(dinv[:], dinv[:], ACT.Sqrt).then_inc(root_ok, 1)

                    def rows(i, b):
                        t_ok.wait(act, i, b - 2)
                        act.activation(ht[b][:], acc[:, ds(i * 2 + b, 1), 0:D].rearrange("p o f -> p (o f)"), ACT.Copy)\
                           .then_inc(h_ok.sem, 1)

                    with act.Fori(0, NT // 2) as i:
                        for b in range(2):
                            rows(i, b)
                            t_ok.wait(act, i, b)
                            prod_ok.wait(act, i, b - 2)
                            act.activation(split(hT[b][:]), halves(pT), ACT.Copy).then_inc(hT_ok.sem, 1)

                @block.tensor
                def _(pe):
                    for s in (t_ok, prod_ok):
                        s.open(pe)

                    def product(i, off):
                        hT_ok.wait(pe, i, off)
                        evac_ok.wait(pe, i, off - 1)
                        pe_product(pe, pO, hT[off % 2], wg, P).then_inc(prod_ok.sem, 1)

                    def turn(i, off):
                        h_ok.wait(pe, i, off)
                        hT_ok.wait(pe, i, off - 1)
                        pe_transpose(pe, pT, ht[off % 2], P).then_inc(t_ok.sem, 1)

                    turn(0, 0)
                    pe.wait_ge(w_in, 16)
                    with pe.Fori(0, NT // 2 - 1) as i:
                        for b in range(2):
                            product(i, b)
                            turn(i, b + 1)
                    product(NT // 2 - 1, 0)
                    turn(NT // 2 - 1, 1)
                    product(NT // 2 - 1, 1)

                @block.vector
                def _(dve):
                    for s in (evac_ok, kept_ok):
                        s.open(dve)
                    dve.tensor_scalar(dinv[:], degr[:], 1.0, None, ALU.add).then_inc(deg_ok, 1)
                    dve.wait_ge(root_ok, 1)
                    dve.reciprocal(dinv[:], dinv[:]).then_inc(root_ok, 1)
                    dve.wait_ge(root_ok, 2)
                    with dve.Fori(0, NT // 2) as i:
                        for b in range(2):
                            prod_ok.wait(dve, i, b)
                            dve.wait_ge(f_out[b], i * 16)
                            kept_ok.wait(dve, i, b - 2)
                            dve.tensor_scalar(split(of[b][:]), halves(pO), dinv[:, ds(i * 2 + b, 1)], None, ALU.mult)\
                               .then_inc(evac_ok.sem, 1)
                            evac_ok.wait(dve, i, b)
                            dve.tensor_copy(acc[:, ds(i * 2 + b, 1), 0:D].rearrange("p o f -> p (o f)"), of[b][:])\
                               .then_inc(kept_ok.sem, 1)

        slot_sum(False)

        with stage() as st:
            bg = sb("bg", [P, D], F32, st)
            b_in, stored = sems(st, "b_in", "stored")
            scaled2, final = sems(st, "scaled2", "final")
            with nc.Block() as block:
                @block.sync
                def _(sp):
                    sp.dma_start(bg[:], io["L1_gnn_b_gcn"].partition_broadcast(P)).then_inc(b_in, 16)
                    sp.wait_ge(b_in, 16)

                @block.vector
                def _(dve):
                    dve.wait_ge(b_in, 16)
                    for t in range(NT):
                        dve.scalar_tensor_tensor(out=acc[:, t, 0:D], in0=acc[:, t, 0:D], scalar=dinv[:, t:t + 1],
                                                 in1=bg[:], op0=ALU.mult, op1=ALU.add).then_inc(scaled2, 1)
                        dve.wait_ge(scaled2, t + 1)
                        dve.tensor_tensor(acc[:, t, 0:D], acc[:, t, 0:D], fdt[:, t, 0:D], ALU.add).then_inc(final, 1)

                @block.gpsimd
                def _(pool):
                    for t in range(NT):
                        rows = P if t < NT - 1 else LAST
                        pool.wait_ge(final, t + 1)
                        pool.indirect_dma_start(out, bass.IndirectOffsetOnAxis(ap=perm[0:rows, t:t + 1], axis=0),
                                                acc[0:rows, t, 0:D], None).then_inc(stored, 16)
                    pool.wait_ge(stored, 16 * NT)


_INS = ['x', 'src', 'dst', 'edge_type_34', 'L0_gnn_W1s', 'L0_gnn_b1s', 'L0_gnn_W1d', 'L0_gnn_b1d', 'L0_gnn_attn1',
        'L0_gnn_ln1_w', 'L0_gnn_ln1_b', 'L0_gnn_Wos', 'L0_gnn_bos', 'L0_gnn_Wod', 'L0_gnn_bod', 'L0_gnn_attno',
        'L0_gnn_lno_w', 'L0_gnn_lno_b', 'L1_gnn_W_rel', 'L1_gnn_W_root', 'L1_gnn_b_rgcn', 'L1_gnn_W_gcn',
        'L1_gnn_b_gcn']


def kernel(**inputs):
    import numpy as _np
    import concourse.bacc as _bacc
    from concourse import mybir as _mybir
    from concourse.bass_utils import run_bass_kernel_spmd as _run

    nc = _bacc.Bacc("TRN2", target_bir_lowering=False, num_devices=1)
    arrays, io = {}, {}
    for name in _INS:
        a = _np.ascontiguousarray(inputs[name])
        arrays[f"in_{name}_dram"] = a
        io[name] = nc.dram_tensor(f"in_{name}_dram", a.shape, _mybir.dt.from_np(a.dtype), kind="ExternalInput").ap()
    out = nc.dram_tensor("out_0_dram", (N, D), _mybir.dt.float32, kind="ExternalOutput").ap()
    gnn_kernel(nc, io, out)
    r = _run(nc, [arrays], core_ids=[0])
    return r.results[0]["out_0_dram"]
```
